# Optimizing a Trainium2 kernel written in Bass

```python
import numpy as np
import jax
import jax.numpy as jnp

def _softmax(x, axis=-1):
    return jax.nn.softmax(x, axis=axis)

def _gelu(x):
    return jax.nn.gelu(x, approximate=True)

def _silu(x):
    return jax.nn.silu(x)

def _sigmoid(x):
    return jax.nn.sigmoid(x)

def _layernorm(x, axis=-1, eps=1e-05):
    m = jnp.mean(x, axis=axis, keepdims=True)
    v = jnp.var(x, axis=axis, keepdims=True)
    return (x - m) / jnp.sqrt(v + eps)

def _scatter_add(tgt, idx, src, axis=0):
    return tgt.at[idx].add(src)

def _segment_sum(src, seg, n):
    return jax.ops.segment_sum(src, seg, n)
kernel_name = 'mk_gnn_resnorm_d4_gnn_r8_be7076'

def setup_inputs(seed: int=0):
    np.random.seed(seed)
    _w = jnp.asarray

    def _rec_inputs():
        import jax
        import jax.numpy as jnp
        _gk = jax.random.key(seed)
        x = -0.0003713 + 1 * jax.random.normal(jax.random.fold_in(_gk, 1), (6250, 128), jnp.float32)
        src = jax.random.randint(jax.random.fold_in(_gk, 2), (100000,), 0, 6250, jnp.int32)
        dst = jnp.minimum((6250 * jax.random.uniform(jax.random.fold_in(_gk, 3), (100000,)) ** 2.0).astype(jnp.int32), 49999)
        _o = jnp.argsort(dst, stable=True)
        src = src[_o]
        dst = dst[_o]
        edge_attr_128 = 5.93493e-05 + 1.00006 * jax.random.normal(jax.random.fold_in(_gk, 11), (100000, 128), jnp.float32)
        edge_weight = jax.random.uniform(jax.random.fold_in(_gk, 13), (100000,), jnp.float32, 0.0, 0.999998)
        return (x, src, dst, edge_attr_128, edge_weight)
    x, src, dst, edge_attr_128, edge_weight = _rec_inputs()

    def _L0_gnn_setup():
        import jax, jax.numpy as jnp
        import numpy as np
        N = 12500
        E = 100000
        D_IN, D_H, D_OUT = (128, 128, 128)
        key = jax.random.key(seed)
        ks = jax.random.split(key, 8)
        x = jax.random.normal(ks[0], (N, D_IN), dtype=jnp.float32)
        edge_index = jax.random.randint(ks[1], (2, E), 0, N, dtype=jnp.int64)
        s = 1.0 / np.sqrt(D_IN)
        W1 = jax.random.uniform(ks[2], (D_H, D_IN), minval=-s, maxval=s, dtype=jnp.float32)
        b1 = jax.random.uniform(ks[3], (D_H,), minval=-s, maxval=s, dtype=jnp.float32)
        sh = 1.0 / np.sqrt(D_H)
        W2 = jax.random.uniform(ks[4], (D_H, D_H), minval=-sh, maxval=sh, dtype=jnp.float32)
        b2 = jax.random.uniform(ks[5], (D_H,), minval=-sh, maxval=sh, dtype=jnp.float32)
        W3 = jax.random.uniform(ks[6], (D_OUT, D_H), minval=-sh, maxval=sh, dtype=jnp.float32)
        b3 = jax.random.uniform(ks[7], (D_OUT,), minval=-sh, maxval=sh, dtype=jnp.float32)
        return {'x': x, 'edge_index': edge_index, 'W1': W1, 'b1': b1, 'W2': W2, 'b2': b2, 'W3': W3, 'b3': b3}
    _L0_gnn_all = _L0_gnn_setup()
    _L0_gnn_in = {k: v for k, v in _L0_gnn_all.items() if k in ('W1', 'b1', 'W2', 'b2', 'W3', 'b3')}
    del _L0_gnn_all

    def _L1_gnn_setup():
        import jax, jax.numpy as jnp
        import numpy as np
        EPS = 0.0
        key = jax.random.key(seed)
        kx, ke, kw, k1, k2 = jax.random.split(key, 5)
        N, E, D, H = (12500, 75000, 128, 128)
        x = jax.random.normal(kx, (N, D), dtype=jnp.float32)
        edge_index = jax.random.randint(ke, (2, E), 0, N, dtype=jnp.int64)
        edge_weight = jax.random.uniform(kw, (E,), dtype=jnp.float32)
        W1 = jax.random.normal(k1, (D, H), dtype=jnp.float32) * (1.0 / np.sqrt(D))
        b1 = jnp.zeros((H,), dtype=jnp.float32)
        W2 = jax.random.normal(k2, (H, D), dtype=jnp.float32) * (1.0 / np.sqrt(H))
        b2 = jnp.zeros((D,), dtype=jnp.float32)
        return {'x': x, 'edge_index': edge_index, 'edge_weight': edge_weight, 'W1': W1, 'b1': b1, 'W2': W2, 'b2': b2}
    _L1_gnn_all = _L1_gnn_setup()
    _L1_gnn_in = {k: v for k, v in _L1_gnn_all.items() if k in ('W1', 'b1', 'W2', 'b2')}
    del _L1_gnn_all

    def _L2_gnn_setup():
        import jax, jax.numpy as jnp
        import numpy as np
        H = 2
        C = 128
        K_ORDER = 4
        BETA = 0.5

        def _gcn_conv(x, row, col, deg_inv, n):
            msg = x[row]
            agg = jax.ops.segment_sum(msg, col, num_segments=n)
            return agg * deg_inv[:, None, None]

        def _attn_conv(qs, ks, vs):
            n = qs.shape[0]
            kvs = jnp.einsum('lhm,lhd->hmd', ks, vs)
            qkvs = jnp.einsum('nhm,hmd->nhd', qs, kvs)
            vs_sum = vs.sum(axis=0)
            num = qkvs + vs_sum[None, :, :]
            ks_sum = ks.sum(axis=0)
            qks_sum = jnp.einsum('nhm,hm->nh', qs, ks_sum)[:, :, None]
            den = qks_sum + jnp.asarray(n, qs.dtype)
            return num / den
        key = jax.random.key(seed)
        ks = jax.random.split(key, 8)
        N, E = (12500, 200000)
        x = jax.random.normal(ks[0], (N, C), jnp.float32)
        edge_index = jax.random.randint(ks[1], (2, E), 0, N, jnp.int64)
        s_in = 1.0 / np.sqrt(C)
        s_out = 1.0 / np.sqrt(H * C * (K_ORDER + 1))
        Wq_w = jax.random.normal(ks[2], (C, H * C), jnp.float32) * s_in
        Wq_b = jax.random.normal(ks[3], (H * C,), jnp.float32) * s_in
        Wk_w = jax.random.normal(ks[4], (C, H * C), jnp.float32) * s_in
        Wk_b = jax.random.normal(ks[5], (H * C,), jnp.float32) * s_in
        Wo_w = jax.random.normal(ks[6], (H * C * (K_ORDER + 1), C), jnp.float32) * s_out
        Wo_b = jax.random.normal(ks[7], (C,), jnp.float32) * s_out
        return {'x': x, 'edge_index': edge_index, 'Wq_w': Wq_w, 'Wq_b': Wq_b, 'Wk_w': Wk_w, 'Wk_b': Wk_b, 'Wo_w': Wo_w, 'Wo_b': Wo_b}
    _L2_gnn_all = _L2_gnn_setup()
    _L2_gnn_in = {k: v for k, v in _L2_gnn_all.items() if k in ('Wq_w', 'Wq_b', 'Wk_w', 'Wk_b', 'Wo_w', 'Wo_b')}
    del _L2_gnn_all

    def _L3_gnn_setup():
        import jax, jax.numpy as jnp
        import numpy as np
        H = 128
        key = jax.random.key(seed)
        ks = jax.random.split(key, 12)
        N, E = (12500, 75000)
        x = jax.random.normal(ks[0], (N, H), dtype=jnp.float32)
        edge_index = jax.random.randint(ks[1], (2, E), 0, N, dtype=jnp.int64)
        edge_attr = jax.random.normal(ks[2], (E, H), dtype=jnp.float32)
        s = 1.0 / np.sqrt(3 * H)
        W1 = jax.random.uniform(ks[3], (H, 3 * H), jnp.float32, -s, s)
        b1 = jax.random.uniform(ks[4], (H,), jnp.float32, -s, s)
        s2 = 1.0 / np.sqrt(H)
        W2 = jax.random.uniform(ks[5], (H, H), jnp.float32, -s2, s2)
        b2 = jax.random.uniform(ks[6], (H,), jnp.float32, -s2, s2)
        W_ih = jax.random.uniform(ks[7], (3 * H, H), jnp.float32, -s2, s2)
        b_ih = jax.random.uniform(ks[8], (3 * H,), jnp.float32, -s2, s2)
        W_hh = jax.random.uniform(ks[9], (3 * H, H), jnp.float32, -s2, s2)
        b_hh = jax.random.uniform(ks[10], (3 * H,), jnp.float32, -s2, s2)
        return {'x': x, 'edge_index': edge_index, 'edge_attr': edge_attr, 'W1': W1, 'b1': b1, 'W2': W2, 'b2': b2, 'W_ih': W_ih, 'b_ih': b_ih, 'W_hh': W_hh, 'b_hh': b_hh}
    _L3_gnn_all = _L3_gnn_setup()
    _L3_gnn_in = {k: v for k, v in _L3_gnn_all.items() if k in ('W1', 'b1', 'W2', 'b2', 'W_ih', 'b_ih', 'W_hh', 'b_hh')}
    del _L3_gnn_all
    return {'x': x, 'src': src, 'dst': dst, 'edge_attr_128': edge_attr_128, 'edge_weight': edge_weight, 'L0_gnn_W1': _L0_gnn_in['W1'], 'L0_gnn_b1': _L0_gnn_in['b1'], 'L0_gnn_W2': _L0_gnn_in['W2'], 'L0_gnn_b2': _L0_gnn_in['b2'], 'L0_gnn_W3': _L0_gnn_in['W3'], 'L0_gnn_b3': _L0_gnn_in['b3'], 'L1_gnn_W1': _L1_gnn_in['W1'], 'L1_gnn_b1': _L1_gnn_in['b1'], 'L1_gnn_W2': _L1_gnn_in['W2'], 'L1_gnn_b2': _L1_gnn_in['b2'], 'L2_gnn_Wq_w': _L2_gnn_in['Wq_w'], 'L2_gnn_Wq_b': _L2_gnn_in['Wq_b'], 'L2_gnn_Wk_w': _L2_gnn_in['Wk_w'], 'L2_gnn_Wk_b': _L2_gnn_in['Wk_b'], 'L2_gnn_Wo_w': _L2_gnn_in['Wo_w'], 'L2_gnn_Wo_b': _L2_gnn_in['Wo_b'], 'L3_gnn_W1': _L3_gnn_in['W1'], 'L3_gnn_b1': _L3_gnn_in['b1'], 'L3_gnn_W2': _L3_gnn_in['W2'], 'L3_gnn_b2': _L3_gnn_in['b2'], 'L3_gnn_W_ih': _L3_gnn_in['W_ih'], 'L3_gnn_b_ih': _L3_gnn_in['b_ih'], 'L3_gnn_W_hh': _L3_gnn_in['W_hh'], 'L3_gnn_b_hh': _L3_gnn_in['b_hh']}

def reference(x, src, dst, edge_attr_128, edge_weight, L0_gnn_W1, L0_gnn_b1, L0_gnn_W2, L0_gnn_b2, L0_gnn_W3, L0_gnn_b3, L1_gnn_W1, L1_gnn_b1, L1_gnn_W2, L1_gnn_b2, L2_gnn_Wq_w, L2_gnn_Wq_b, L2_gnn_Wk_w, L2_gnn_Wk_b, L2_gnn_Wo_w, L2_gnn_Wo_b, L3_gnn_W1, L3_gnn_b1, L3_gnn_W2, L3_gnn_b2, L3_gnn_W_ih, L3_gnn_b_ih, L3_gnn_W_hh, L3_gnn_b_hh):
    import jax
    import jax.numpy as jnp

    def _L0_gnn_ref(x, edge_index, W1, b1, W2, b2, W3, b3):
        import jax, jax.numpy as jnp
        import numpy as np
        N = 12500
        E = 100000
        D_IN, D_H, D_OUT = (128, 128, 128)
        row, col = (edge_index[0], edge_index[1])
        n = x.shape[0]
        deg = jnp.clip(jax.ops.segment_sum(jnp.ones_like(row, dtype=x.dtype), row, num_segments=n), 1.0)

        def mp(h):
            agg = jax.ops.segment_sum(h[col], row, num_segments=n)
            return jax.nn.relu(agg / deg[:, None])
        h = mp(x @ W1.T + b1)
        h = mp(h @ W2.T + b2)
        return h @ W3.T + b3

    def _L1_gnn_ref(x, edge_index, edge_weight, W1, b1, W2, b2):
        import jax, jax.numpy as jnp
        import numpy as np
        EPS = 0.0
        N = x.shape[0]
        src, dst = (edge_index[0], edge_index[1])
        msg = edge_weight[:, None] * x[src]
        agg = jax.ops.segment_sum(msg, dst, num_segments=N)
        out = (1.0 + EPS) * x + agg
        h = jax.nn.relu(out @ W1 + b1)
        return h @ W2 + b2

    def _L2_gnn_ref(x, edge_index, Wq_w, Wq_b, Wk_w, Wk_b, Wo_w, Wo_b):
        import jax, jax.numpy as jnp
        import numpy as np
        H = 2
        C = 128
        K_ORDER = 4
        BETA = 0.5

        def _gcn_conv(x, row, col, deg_inv, n):
            msg = x[row]
            agg = jax.ops.segment_sum(msg, col, num_segments=n)
            return agg * deg_inv[:, None, None]

        def _attn_conv(qs, ks, vs):
            n = qs.shape[0]
            kvs = jnp.einsum('lhm,lhd->hmd', ks, vs)
            qkvs = jnp.einsum('nhm,hmd->nhd', qs, kvs)
            vs_sum = vs.sum(axis=0)
            num = qkvs + vs_sum[None, :, :]
            ks_sum = ks.sum(axis=0)
            qks_sum = jnp.einsum('nhm,hm->nh', qs, ks_sum)[:, :, None]
            den = qks_sum + jnp.asarray(n, qs.dtype)
            return num / den
        n = x.shape[0]
        row, col = (edge_index[0], edge_index[1])
        deg = jax.ops.segment_sum(jnp.ones(row.shape[0], x.dtype), col, num_segments=n)
        deg_inv = jnp.where(deg > 0, 1.0 / deg, 0.0)
        query = (x @ Wq_w + Wq_b).reshape(n, H, C)
        key = (x @ Wk_w + Wk_b).reshape(n, H, C)
        qs = query / jnp.linalg.norm(query, axis=2, keepdims=True)
        ks = key / jnp.linalg.norm(key, axis=2, keepdims=True)
        x0 = jnp.broadcast_to(x[:, None, :], (n, H, C))
        terms = [x0]
        for _ in range(K_ORDER):
            prev = terms[-1]
            gcn_i = _gcn_conv(prev, row, col, deg_inv, n)
            attn_i = _attn_conv(qs, ks, prev)
            terms.append(BETA * gcn_i + attn_i)
        xcat = jnp.concatenate(terms, axis=-1)
        xcat = xcat.reshape(n, H * C * (K_ORDER + 1))
        return (xcat @ Wo_w + Wo_b) / H

    def _L3_gnn_ref(x, edge_index, edge_attr, W1, b1, W2, b2, W_ih, b_ih, W_hh, b_hh):
        import jax, jax.numpy as jnp
        import numpy as np
        H = 128
        src_idx = edge_index[0]
        dst_idx = edge_index[1]
        src_feats = x[src_idx]
        dst_feats = x[dst_idx]
        msg_input = jnp.concatenate([src_feats, dst_feats, edge_attr], axis=-1)
        h1 = jax.nn.relu(msg_input @ W1.T + b1)
        messages = h1 @ W2.T + b2
        aggregated = jax.ops.segment_sum(messages, dst_idx, num_segments=x.shape[0])
        gi = aggregated @ W_ih.T + b_ih
        gh = x @ W_hh.T + b_hh
        i_r, i_z, i_n = jnp.split(gi, 3, axis=-1)
        h_r, h_z, h_n = jnp.split(gh, 3, axis=-1)
        r = jax.nn.sigmoid(i_r + h_r)
        z = jax.nn.sigmoid(i_z + h_z)
        n = jnp.tanh(i_n + r * h_n)
        return (1.0 - z) * n + z * x
    edge_index = jnp.stack([src, dst])
    x = _layernorm(x + _L0_gnn_ref(x, edge_index, L0_gnn_W1, L0_gnn_b1, L0_gnn_W2, L0_gnn_b2, L0_gnn_W3, L0_gnn_b3), axis=-1)
    x = _layernorm(x + _L1_gnn_ref(x, edge_index, edge_weight, L1_gnn_W1, L1_gnn_b1, L1_gnn_W2, L1_gnn_b2), axis=-1)
    x = _layernorm(x + _L2_gnn_ref(x, edge_index, L2_gnn_Wq_w, L2_gnn_Wq_b, L2_gnn_Wk_w, L2_gnn_Wk_b, L2_gnn_Wo_w, L2_gnn_Wo_b), axis=-1)
    x = _layernorm(x + _L3_gnn_ref(x, edge_index, edge_attr_128, L3_gnn_W1, L3_gnn_b1, L3_gnn_W2, L3_gnn_b2, L3_gnn_W_ih, L3_gnn_b_ih, L3_gnn_W_hh, L3_gnn_b_hh), axis=-1)
    return x

_drawn_inputs = setup_inputs


def setup_inputs(seed=0):
    import zlib

    import numpy as np

    out = dict(_drawn_inputs(seed))
    spreads = {'L1_gnn_b1': (0.0, 0.1), 'L1_gnn_b2': (0.0, 0.1)}
    factors = {'L0_gnn_W1': 7.703,
     'L0_gnn_b1': 3.489,
     'L2_gnn_Wq_w': 8.0,
     'L2_gnn_Wq_b': 8.0,
     'L2_gnn_Wk_w': 8.0,
     'L2_gnn_Wk_b': 8.0,
     'L2_gnn_Wo_b': 4.663,
     'L3_gnn_b1': 2.703,
     'L3_gnn_b_ih': 3.719,
     'L3_gnn_b_hh': 5.736}
    for name, (base, spread) in spreads.items():
        noise = np.random.default_rng([zlib.crc32(name.encode()), seed]).standard_normal(out[name].shape)
        drawn = base * np.exp(spread * noise) if base else spread * noise
        out[name] = jnp.asarray(drawn.astype(out[name].dtype))
    for name, factor in factors.items():
        out[name] = (out[name] * factor).astype(out[name].dtype)
    return out
```

```python
import concourse.bass as bass
from concourse import mybir
from contextlib import ExitStack, contextmanager

F32 = mybir.dt.float32
BF16 = mybir.dt.bfloat16
I32 = mybir.dt.int32
I16 = mybir.dt.int16
ALU = mybir.AluOpType
ACT = mybir.ActivationFunctionType
AX = mybir.AxisListType

P = 128
N = 6250
E = 100000
EPS = 1e-5
WIN = (N + P - 1) // P
NP = WIN * P
AW = NP + P
GW = 7
G = WIN // GW
GC = GW * P
HC = GC // 2
FULL = E // P
REST = E - FULL * P
TILES = 784
CH = (TILES + P - 1) // P
U = 28
H = U // 2
SU = 16
SH = SU // 2
TABS = 4
HW = P + 4
TRASH = NP
HEADS = 2
ORDER = 4
REGS = 14


def prev(step, per, k):
    return step * per + k


def now(step, per, k):
    return step * per + per + k


def gnn_resnorm(nc, out, x, src, dst, edge_attr_128, edge_weight,
                L0_gnn_W1, L0_gnn_b1, L0_gnn_W2, L0_gnn_b2, L0_gnn_W3, L0_gnn_b3,
                L1_gnn_W1, L1_gnn_b1, L1_gnn_W2, L1_gnn_b2,
                L2_gnn_Wq_w, L2_gnn_Wq_b, L2_gnn_Wk_w, L2_gnn_Wk_b, L2_gnn_Wo_w, L2_gnn_Wo_b,
                L3_gnn_W1, L3_gnn_b1, L3_gnn_W2, L3_gnn_b2,
                L3_gnn_W_ih, L3_gnn_b_ih, L3_gnn_W_hh, L3_gnn_b_hh, upto=99):
    ctx = ExitStack()
    with ctx:
        ctx.enter_context(nc.allow_non_contiguous_dma(reason="biases by feature and one number per tile: a few thousand elements"))

        def sb(name, shape, dt=F32):
            return ctx.enter_context(nc.sbuf_tensor(name, shape, dt))

        def dram(name, shape, dt=F32):
            return nc.dram_tensor(name, shape, dt, kind="Internal").ap()

        def loop(eng, count):
            return nc.Fori(0, count, engines=(eng.engine,), hint_back_edge=True)

        def peeled(eng, count, body):
            body(0)
            with nc.Fori(1, count, engines=(eng.engine,), hint_back_edge=True) as i:
                body(i)

        def wait_past(eng, sem, value):
            if not isinstance(value, int) or value > 0:
                eng.wait_ge(sem, value)

        @contextmanager
        def stage(*names):
            stage.n += 1
            sems = [nc.alloc_semaphore(f"{n}_{stage.n}") for n in names]
            with nc.Block() as block:
                yield (block, *sems)
            nc.clear_and_free_semaphores(sems)
            nc.all_engine_barrier()
        stage.n = 0

        def two(ap):
            return ap.rearrange("p (b n) -> p b n", b=2)

        def windows(table, g, width):
            return table[bass.ds(g * GC, GC), 0:width].rearrange("(k p) f -> p k f", p=P)

        ident = sb("ident", [P, P])
        ident_bf = sb("ident_bf", [P, P], BF16)
        mean_mat = sb("mean_mat", [P, P])
        ones_mat = sb("ones_mat", [P, P])
        iota16 = sb("iota16", [P, P], I16)
        tri = sb("tri", [P, P])
        trash = sb("trash", [P, 1])
        eps_col = sb("eps_col", [P, 1])
        src_idx = sb("src_idx", [P, TILES], I32)
        src_col = sb("src_col", [P, TILES])
        loc_col = sb("loc_col", [P, TILES])
        ew_col = sb("ew_col", [P, TILES])
        scat_idx = sb("scat_idx", [P, TILES], I32)
        base_row = sb("base_row", [1, TILES], I32)
        dinv = sb("dinv", [P, NP])
        kv = sb("kv", [P, HEADS, P])
        kv_sums = sb("kv_sums", [P, 2 * HEADS])
        key_sum = sb("key_sum", [P, HEADS, P])
        xT = sb("xT", [P, AW])
        acc = sb("acc", [P, HEADS, AW])
        wts = sb("wts", [P, 30, P])
        cols = sb("cols", [P, 24])
        bias_rows = sb("bias_rows", [P, 5, P])
        ps = ctx.enter_context(nc.psum_tensor("ps", [P, 8, 512], F32))
        flat = ps[:, :, :].rearrange("p b n -> p (b n)")

        xpad = dram("xpad", [NP, P])
        h_tab = dram("h_tab", [AW, HW])
        sums = [[dram(f"sums{m}_{k}", [AW, HW]) for k in range(TABS)] for m in range(2)]
        src_rows = dram("src_rows", [TILES, P])
        tile_info = dram("tile_info", [2, CH * P])
        x_tab = dram("x_tab", [NP, P])
        xh_tab = dram("xh_tab", [NP, HEADS * P])
        k_tab = dram("k_tab", [NP, HEADS * P])
        q_tab = dram("q_tab", [HEADS * P, NP])
        rden_tab = dram("rden_tab", [HEADS * P, NP])
        deg_tab = dram("deg_tab", [P, NP])
        p_tab = dram("p_tab", [NP, P])
        q3_tab = dram("q3_tab", [AW, P])

        W0 = [0, 1, 2]
        W1A, W1B = 3, 4
        WQ, WK = [5, 6], [7, 8]
        WO = [[9 + h * (ORDER + 1) + k for k in range(ORDER + 1)] for h in range(HEADS)]
        W3 = [19, 20, 21]
        W3O = 22
        WIH, WHH = [23, 24, 25], [26, 27, 28]
        B03, B11, B12, BQ, BO, B32, BIH, BHH = 0, 1, 2, [3, 4], 5, 6, [7, 8, 9], [10, 11, 12]
        BRZ, BOH, VS = [13, 14], 15, [16, 17]

        def wt(n):
            return wts[:, n, :]

        def col(n):
            return cols[:, n:n + 1]

        def two_matmuls(eng, bank, lhsT, rhs, start=True, stop=True):
            for b in range(2):
                last = nc.tensor.matmul(ps[:, bank + b, 0:HC], lhsT, rhs[:, b * HC:(b + 1) * HC],
                                        start=start, stop=stop)
            return last

        def load_weights():
            with ExitStack() as st:
                raw = st.enter_context(nc.sbuf_tensor("raw_w", [P, 13, P], F32))
                with stage("w_in", "filled", "made", "turned", "copied", "padded") as (
                        block, w_in, filled, made, turned, copied, padded):
                    natural = [L0_gnn_W1, L0_gnn_W2, L0_gnn_W3]
                    natural += [L3_gnn_W1[:, k * P:(k + 1) * P] for k in range(3)] + [L3_gnn_W2]
                    natural += [L3_gnn_W_ih[k * P:(k + 1) * P, :] for k in range(3)]
                    natural += [L3_gnn_W_hh[k * P:(k + 1) * P, :] for k in range(3)]
                    places = W0 + W3 + [W3O] + WIH + WHH
                    direct = [(W1A, L1_gnn_W1), (W1B, L1_gnn_W2)]
                    for h in range(HEADS):
                        direct += [(WQ[h], L2_gnn_Wq_w[:, h * P:(h + 1) * P]),
                                   (WK[h], L2_gnn_Wk_w[:, h * P:(h + 1) * P])]
                        direct += [(WO[h][k], L2_gnn_Wo_w[(h * (ORDER + 1) + k) * P:(h * (ORDER + 1) + k + 1) * P, :])
                                   for k in range(ORDER + 1)]
                    columns = [(B03, L0_gnn_b3), (B11, L1_gnn_b1), (B12, L1_gnn_b2), (BO, L2_gnn_Wo_b),
                               (B32, L3_gnn_b2)]
                    columns += [(BQ[h], L2_gnn_Wq_b[h * P:(h + 1) * P]) for h in range(HEADS)]
                    columns += [(BIH[k], L3_gnn_b_ih[k * P:(k + 1) * P]) for k in range(3)]
                    columns += [(BHH[k], L3_gnn_b_hh[k * P:(k + 1) * P]) for k in range(3)]
                    along = [L0_gnn_b1, L0_gnn_b2, L3_gnn_b1, L2_gnn_Wk_b[0:P], L2_gnn_Wk_b[P:2 * P]]
                    loads = 16 * (len(natural) + len(direct) + len(columns) + len(along))

                    @block.sync
                    def _(sp):
                        for n, w in enumerate(natural):
                            sp.dma_start(raw[:, n, :], w).then_inc(w_in, 16)
                        for n, w in direct:
                            sp.dma_start(wt(n), w).then_inc(w_in, 16)
                        for n, b in columns:
                            sp.dma_start(col(n), b.rearrange("(p a) -> p a", a=1)).then_inc(w_in, 16)
                        for n, b in enumerate(along):
                            sp.dma_start(bias_rows[:, n, :], b.partition_broadcast(P)).then_inc(w_in, 16)
                        sp.dma_start(xpad[0:N, :], x).then_inc(padded, 16)
                        sp.wait_ge(filled, 2)
                        sp.dma_start(xpad[N:NP, :], acc[0:NP - N, 0, 0:P]).then_inc(padded, 16)
                        sp.dma_start(h_tab[NP:AW, :], acc[:, 0, 0:HW]).then_inc(padded, 16)
                        sp.dma_start(q3_tab[NP:AW, :], acc[:, 0, 0:P]).then_inc(padded, 16)
                        for m in range(2):
                            for k in range(TABS):
                                sp.dma_start(sums[m][k][:, :].rearrange("(p r) f -> p (r f)", p=P),
                                             acc[:, :, :].rearrange("p h n -> p (h n)")[:, 0:AW // P * HW]
                                             ).then_inc(padded, 16)
                        sp.wait_ge(padded, 16 * (4 + 2 * TABS))

                    @block.gpsimd
                    def _(pool):
                        nc.gpsimd.memset(ident[:, :], 0.0).then_inc(made, 1)
                        nc.gpsimd.memset(ones_mat[:, :], 1.0).then_inc(made, 1)
                        nc.gpsimd.iota(iota16[:, :], pattern=[[1, P]], base=0, channel_multiplier=0).then_inc(made, 1)
                        nc.gpsimd.iota(trash[:, :], pattern=[[0, 1]], base=TRASH, channel_multiplier=1,
                                       allow_small_or_imprecise_dtypes=True).then_inc(made, 1)
                        pool.wait_ge(made, 4)
                        nc.gpsimd.affine_select(out=ident[:, :], in_=ident[:, :], compare_op=ALU.not_equal, fill=1.0,
                                                base=0, pattern=[[-1, P]], channel_multiplier=1).then_inc(made, 1)
                        nc.gpsimd.affine_select(out=tri[:, :], in_=ones_mat[:, :], compare_op=ALU.is_gt, fill=0.0,
                                                base=0, pattern=[[-1, P]], channel_multiplier=1).then_inc(made, 1)

                    @block.vector
                    def _(dve):
                        nc.vector.memset(acc[:, :, :], 0.0).then_inc(filled, 1)
                        nc.vector.memset(xT[:, NP:AW], 0.0).then_inc(filled, 1)
                        nc.vector.memset(mean_mat[:, :], 1.0 / P).then_inc(filled, 1)
                        nc.vector.memset(eps_col[:, :], EPS).then_inc(filled, 1)
                        dve.wait_ge(made, 6)
                        nc.vector.tensor_copy(ident_bf[:, :], ident[:, :]).then_inc(filled, 1)
                        dve.wait_ge(w_in, loads)
                        for k in range(2):
                            nc.vector.tensor_tensor(col(BRZ[k]), col(BIH[k]), col(BHH[k]), ALU.add).then_inc(filled, 1)
                        nc.vector.tensor_scalar(col(BOH), col(BO), 1.0 / HEADS, None, ALU.mult).then_inc(filled, 1)

                    @block.tensor
                    def _(pe):
                        pe.wait_ge(w_in, loads)
                        pe.wait_ge(made, 6)
                        for n in range(len(natural)):
                            last = nc.tensor.transpose(flat[:, n * P:(n + 1) * P], raw[:, n, :], ident[:, :])
                        last.then_inc(turned, 1)

                    @block.scalar
                    def _(act):
                        act.wait_ge(turned, 1)
                        for n, place in enumerate(places):
                            nc.scalar.copy(wt(place), flat[:, n * P:(n + 1) * P]).then_inc(copied, 1)

        def prepare_edges():
            with ExitStack() as st:
                def tmp(name, shape, dt=F32):
                    return st.enter_context(nc.sbuf_tensor(name, shape, dt))
                src_i, dst_i = tmp("src_i", [P, CH, P], I32), tmp("dst_i", [P, CH, P], I32)
                src_f, dst_f, ew_f = tmp("src_f", [P, CH, P]), tmp("dst_f", [P, CH, P]), tmp("ew_f", [P, CH, P])
                loc_f = tmp("loc_f", [P, CH, P])
                info = tmp("info", [P, 2, CH])
                with stage("cleared", "e_in", "dve_done", "turned", "copied", "info_out", "info_in", "based") as (
                        block, cleared, e_in, dve_done, turned, copied, info_out, info_in, based):
                    last = CH - 1
                    lead = last * P
                    tail = FULL - lead
                    fill = (P - REST) // REST

                    @block.sync
                    def _(sp):
                        sp.wait_ge(cleared, 3)
                        for a, v in ((src_i, src), (dst_i, dst), (ew_f, edge_weight)):
                            sp.dma_start(a[:, 0:last, :], v[0:lead * P].rearrange("(c t p) -> t c p", c=last, p=P)).then_inc(e_in, 16)
                            sp.dma_start(a[0:tail, last, :], v[lead * P:FULL * P].rearrange("(t p) -> t p", p=P)).then_inc(e_in, 16)
                            for k in range(fill + 1):
                                sp.dma_start(a[tail:tail + 1, last, k * REST:(k + 1) * REST],
                                             v[FULL * P:E].rearrange("(t p) -> t p", t=1)).then_inc(e_in, 16)
                        sp.wait_ge(dve_done, 2)
                        sp.dma_start(src_rows[0:lead, :].rearrange("(c t) p -> t c p", c=last), src_f[:, 0:last, :]).then_inc(info_out, 16)
                        sp.dma_start(src_rows[lead:TILES, :], src_f[0:TILES - lead, last, :]).then_inc(info_out, 16)
                        sp.wait_ge(dve_done, 6)
                        for k in range(2):
                            sp.dma_start(tile_info[k, :].rearrange("(c t) -> t c", c=CH), info[:, k, :]).then_inc(info_out, 16)
                        sp.wait_ge(info_out, 64)
                        sp.dma_start(acc[0:1, 0, 0:CH * P], tile_info[0:1, :]).then_inc(info_in, 16)
                        sp.dma_start(acc[0:1, 1, 0:CH * P], tile_info[1:2, :]).then_inc(info_in, 16)

                    @block.vector
                    def _(dve):
                        for a in (src_i, dst_i, ew_f):
                            nc.vector.memset(a[:, last, :], 0).then_inc(cleared, 1)
                        dve.wait_ge(e_in, 16 * 3 * (fill + 3))
                        nc.vector.tensor_copy(src_f[:, :, :], src_i[:, :, :]).then_inc(dve_done, 1)
                        nc.vector.tensor_copy(dst_f[:, :, :], dst_i[:, :, :]).then_inc(dve_done, 1)
                        dve.wait_ge(dve_done, 2)
                        nc.vector.tensor_reduce(info[:, 0, :], dst_f[:, :, :], AX.X, ALU.min).then_inc(dve_done, 1)
                        nc.vector.tensor_reduce(info[:, 1, :], dst_f[:, :, :], AX.X, ALU.max).then_inc(dve_done, 1)
                        dve.wait_ge(dve_done, 4)
                        nc.vector.tensor_tensor(info[:, 1, :], info[:, 1, :], info[:, 0, :], ALU.subtract).then_inc(dve_done, 1)
                        nc.vector.tensor_tensor(loc_f[:, :, :], dst_f[:, :, :],
                                                info[:, 0, :].unsqueeze(2).to_broadcast([P, CH, P]), ALU.subtract).then_inc(dve_done, 1)
                        dve.wait_ge(info_in, 32)
                        nc.vector.tensor_copy(base_row[0:1, :], acc[0:1, 0, 0:TILES]).then_inc(based, 1)
                        dve.wait_ge(copied, 4)
                        for a in (loc_col, src_col):
                            nc.vector.memset(a[:, FULL + 1:TILES], -1.0).then_inc(based, 1)
                            for p0 in range(REST, P, 32):
                                nc.vector.memset(a[p0:p0 + 32, FULL:FULL + 1], -1.0).then_inc(based, 1)

                    @block.tensor
                    def _(pe):
                        pe.wait_ge(dve_done, 6)
                        for n, a in enumerate((src_f, loc_f, ew_f)):
                            for c in range(CH):
                                lastmm = nc.tensor.transpose(flat[:, n * 1024 + c * P:n * 1024 + (c + 1) * P], a[:, c, :], ident[:, :])
                            lastmm.then_inc(turned, 1)

                    @block.scalar
                    def _(act):
                        for n, to in ((0, src_col), (0, src_idx), (1, loc_col), (2, ew_col)):
                            act.wait_ge(turned, n + 1)
                            nc.scalar.copy(to[:, :], flat[:, n * 1024:n * 1024 + TILES]).then_inc(copied, 1)

        def scatter_rows():
            B = 8
            with ExitStack() as st:
                src_bc = st.enter_context(nc.sbuf_tensor("src_bc0", [P, 2, B * P], F32))
                hits = st.enter_context(nc.sbuf_tensor("hits", [P, 2, P], F32))
                earlier = st.enter_context(nc.sbuf_tensor("earlier", [P, TILES], F32))
                to_row = st.enter_context(nc.sbuf_tensor("to_row", [P, TILES], F32))
                with stage("bc0", "bc1", "counted", "dve_done") as (block, bc0, bc1, counted, dve_done):
                    bc = [bc0, bc1]

                    @block.sync
                    def _(sp):
                        with loop(sp, TILES // B // 2) as i:
                            for s in range(2):
                                sp.wait_ge(counted, prev(i, 2 * B, (s + 1) * B))
                                sp.dma_start(src_bc[:, s, :],
                                             src_rows[bass.ds(i * 2 * B + s * B, B), :].rearrange("t p -> (t p)").partition_broadcast(P)
                                             ).then_inc(bc[s], 16)

                    @block.vector
                    def _(dve):
                        nc.vector.sem_inc(counted, 2 * B)
                        with loop(dve, TILES // B // 2) as i:
                            for s in range(2):
                                dve.wait_ge(bc[s], 16 * i + 16)
                                for k in range(B):
                                    t = s * B + k
                                    dve.wait_ge(counted, now(i, 2 * B, t - 1))
                                    nc.vector.scalar_tensor_tensor(
                                        out=hits[:, k % 2, :], in0=src_bc[:, s, k * P:(k + 1) * P],
                                        scalar=src_col[:, bass.ds(i * 2 * B + t, 1)], in1=tri[:, :],
                                        op0=ALU.is_equal, op1=ALU.mult,
                                        accum_out=earlier[:, bass.ds(i * 2 * B + t, 1)]).then_inc(counted, 1)
                        dve.wait_ge(counted, 2 * B + TILES)
                        nc.vector.tensor_scalar(earlier[:, :], earlier[:, :], 1.0, None, ALU.min).then_inc(dve_done, 1)
                        nc.vector.tensor_scalar(to_row[:, :], src_col[:, :], trash[:, 0:1], -1.0,
                                                ALU.subtract, ALU.mult).then_inc(dve_done, 1)
                        dve.wait_ge(dve_done, 2)
                        nc.vector.tensor_tensor(to_row[:, :], to_row[:, :], earlier[:, :], ALU.mult).then_inc(dve_done, 1)
                        dve.wait_ge(dve_done, 3)
                        nc.vector.tensor_tensor(to_row[:, :], to_row[:, :], src_col[:, :], ALU.add).then_inc(dve_done, 1)
                        dve.wait_ge(dve_done, 4)
                        nc.vector.tensor_copy(to_row[:, FULL + 1:TILES],
                                              trash[:, 0:1].to_broadcast([P, TILES - FULL - 1])).then_inc(dve_done, 1)
                        for p0 in range(REST, P, 32):
                            nc.vector.tensor_copy(to_row[p0:p0 + 32, FULL:FULL + 1], trash[p0:p0 + 32, :]).then_inc(dve_done, 1)
                        dve.wait_ge(dve_done, 5 + (P - REST) // 32)
                        nc.vector.tensor_copy(scat_idx[:, :], to_row[:, :]).then_inc(dve_done, 1)

        def first_linear():
            with ExitStack() as st:
                rows = st.enter_context(nc.sbuf_tensor("x_rows", [P, GW, P], F32))
                zT = st.enter_context(nc.sbuf_tensor("zT0", [P, GC], F32))
                h_rows = st.enter_context(nc.sbuf_tensor("h_rows0", [P, GW, HW], F32))
                with stage("x_in", "pe_done", "act_done", "dve_done", "stored", "filled") as (
                        block, x_in, pe_done, act_done, dve_done, stored, filled):
                    @block.sync
                    def _(sp):
                        nc.sync.sem_inc(stored, 16)
                        sp.wait_ge(filled, 1)
                        with loop(sp, G) as g:
                            sp.wait_ge(pe_done, prev(g, 2, 1))
                            sp.dma_start(rows[:, :, :], windows(xpad, g, P)).then_inc(x_in, 16)
                            sp.wait_ge(dve_done, now(g, 1, 1))
                            sp.dma_start(windows(h_tab, g, HW), h_rows[:, :, :]).then_inc(stored, 16)
                        sp.wait_ge(stored, 16 * G + 16)

                    @block.tensor
                    def _(pe):
                        nc.tensor.sem_inc(pe_done, 2)
                        with loop(pe, G) as g:
                            pe.wait_ge(x_in, 16 * g + 16)
                            pe.wait_ge(act_done, prev(g, 2, 2))
                            for k in range(GW):
                                last = nc.tensor.transpose(flat[:, k * P:(k + 1) * P], rows[:, k, :], ident[:, :])
                            last.then_inc(pe_done, 1)
                            pe.wait_ge(act_done, now(g, 2, 1))
                            pe.wait_ge(dve_done, prev(g, 1, 1))
                            for k in range(GW):
                                last = nc.tensor.matmul(flat[:, 1024 + k * P:1024 + (k + 1) * P], zT[:, k * P:(k + 1) * P],
                                                        wt(W0[0]), start=True, stop=True)
                            last.then_inc(pe_done, 1)

                    @block.scalar
                    def _(act):
                        nc.scalar.sem_inc(act_done, 2)
                        with loop(act, G) as g:
                            act.wait_ge(pe_done, now(g, 2, 1))
                            nc.scalar.copy(zT[:, :], flat[:, 0:GC]).then_inc(act_done, 1)
                            nc.scalar.copy(xT[:, bass.ds(g * GC, GC)], flat[:, 0:GC]).then_inc(act_done, 1)

                    @block.vector
                    def _(dve):
                        nc.vector.memset(h_rows[:, :, P:HW], 1.0).then_inc(filled, 1)
                        nc.vector.sem_inc(dve_done, 1)
                        with loop(dve, G) as g:
                            dve.wait_ge(pe_done, now(g, 2, 2))
                            dve.wait_ge(stored, 16 * g + 16)
                            nc.vector.tensor_tensor(h_rows[:, :, 0:P], flat[:, 1024:1024 + GC].rearrange("p (k f) -> p k f", k=GW),
                                                    bias_rows[:, 0:1, :].to_broadcast([P, GW, P]), ALU.add).then_inc(dve_done, 1)

        def scatter_pass(m):
            W = 4
            with ExitStack() as st:
                def tmp(name, shape, dt=F32):
                    return st.enter_context(nc.sbuf_tensor(f"{name}_{m}", shape, dt))
                win = tmp("win", [P, W, HW])
                src_bc = tmp("src_bc", [P, 2, SH * P])
                onehot = tmp("onehot_s", [P, 2, P], BF16)
                same = tmp("same", [P, 2, P], BF16)
                pick = tmp("pick", [P, 2, P])
                out_rows = tmp("out_rows", [P, SU, HW])
                idx = tmp("idx_s", [P, 2, SH], I32)
                names = [f"win_in{k}" for k in range(W)] + ["bc0", "bc1"] + [f"added{k}" for k in range(TABS)]
                names += ["matched", "joined", "pick_copied", "summed", "sum_copied", "idx_copied", "begun"]
                with stage(*names) as (block, *s):
                    win_in, bc, added = s[0:W], s[W:W + 2], s[W + 2:W + 2 + TABS]
                    matched, joined, pick_copied, summed, sum_copied, idx_copied, begun = s[W + 2 + TABS:]
                    steps = TILES // SU
                    per = SU // TABS

                    @block.sync
                    def _(sp):
                        regs = [nc.sync.alloc_register(f"win_base{m}_{k}") for k in range(SH)]
                        with loop(sp, steps) as i:
                            for h in range(2):
                                nc.sync.load(regs, base_row[0:1, bass.ds(i * SU + h * SH, SH)])
                                base = [nc.sync.snap(r, min_val=0, max_val=N - 1) for r in regs]
                                sp.wait_ge(matched, prev(i, SU, (h + 1) * SH))
                                sp.dma_start(src_bc[:, h, :],
                                             src_rows[bass.ds(i * SU + h * SH, SH), :].rearrange("t p -> (t p)").partition_broadcast(P)
                                             ).then_inc(bc[h], 16)
                                for k in range(SH):
                                    j = h * SH + k
                                    sp.wait_ge(summed, i * SU + j + 1)
                                    sp.dma_start(win[:, j % W, :], h_tab[bass.ds(base[k], P), :]).then_inc(win_in[j % W], 16)

                    @block.vector
                    def _(dve):
                        nc.vector.sem_inc(matched, SU)
                        with loop(dve, steps) as i:
                            for j in range(SU):
                                t = bass.ds(i * SU + j, 1)
                                if j % SH == 0:
                                    dve.wait_ge(bc[j // SH], 16 * i + 16)
                                dve.wait_ge(joined, i * SU + j + 1)
                                nc.vector.tensor_scalar(onehot[:, j % 2, :], iota16[:, :], loc_col[:, t], None, ALU.is_equal)
                                nc.vector.tensor_scalar(same[:, j % 2, :], src_bc[:, j // SH, (j % SH) * P:(j % SH + 1) * P],
                                                        src_col[:, t], None, ALU.is_equal).then_inc(matched, 1)

                    @block.tensor
                    def _(pe):
                        nc.tensor.sem_inc(joined, 2)
                        nc.tensor.sem_inc(summed, W)

                        def sum_rows(i, j):
                            pe.wait_ge(pick_copied, i * SU + j + 3)
                            pe.wait_ge(win_in[j % W], 16 * (i * (SU // W) + j // W + 1))
                            pe.wait_ge(sum_copied, i * SU + j + 1)
                            nc.tensor.matmul(ps[:, 2 + j % 2, 0:HW], pick[:, j % 2, :], win[:, j % W, :],
                                             start=True, stop=True).then_inc(summed, 1)

                        with loop(pe, steps) as i:
                            for j in range(SU):
                                pe.wait_ge(matched, now(i, SU, j + 1))
                                pe.wait_ge(pick_copied, i * SU + j + 1)
                                nc.tensor.matmul(ps[:, j % 2, 0:P], onehot[:, j % 2, :], same[:, j % 2, :],
                                                 start=True, stop=True).then_inc(joined, 1)
                                if j:
                                    sum_rows(i, j - 1)
                            sum_rows(i, SU - 1)

                    @block.scalar
                    def _(act):
                        nc.scalar.sem_inc(pick_copied, 2)
                        nc.scalar.sem_inc(sum_copied, 2)

                        def copy_sum(i, j):
                            act.wait_ge(summed, i * SU + j + 1 + W)
                            wait_past(act, added[j % TABS], 16 * ((i - 1) * per + j // TABS + 1))
                            nc.scalar.copy(out_rows[:, j, :], ps[:, 2 + j % 2, 0:HW]).then_inc(sum_copied, 1)

                        def step(i):
                            for j in range(SU):
                                if j % SH == 0:
                                    for k in range(TABS):
                                        wait_past(act, added[k], 16 * ((i - 1) * per + (j // SH + 1) * (SH // TABS)))
                                    nc.scalar.copy(idx[:, j // SH, :], scat_idx[:, bass.ds(i * SU + j, SH)]).then_inc(idx_copied, 1)
                                act.wait_ge(joined, i * SU + j + 3)
                                act.wait_ge(summed, i * SU + j - 1 + W)
                                nc.scalar.copy(pick[:, j % 2, :], ps[:, j % 2, 0:P]).then_inc(pick_copied, 1)
                                if j:
                                    copy_sum(i, j - 1)
                            copy_sum(i, SU - 1)

                        peeled(act, steps, step)

                    @block.gpsimd
                    def _(pool):
                        def step(i):
                            for j in range(SU):
                                if j % SH == 0:
                                    pool.wait_ge(idx_copied, i * 2 + j // SH + 1)
                                pool.wait_ge(sum_copied, i * SU + j + 3)
                                wait_past(pool, added[j % TABS], 16 * (i * per + j // TABS))
                                nc.gpsimd.sem_inc(begun, 1)
                                nc.gpsimd.indirect_dma_start(
                                    sums[m][j % TABS],
                                    bass.IndirectOffsetOnAxis(ap=idx[:, j // SH, j % SH:j % SH + 1], axis=0),
                                    out_rows[:, j, :], None, compute_op=ALU.add).then_inc(added[j % TABS], 16)

                        peeled(pool, steps, step)
                        for k in range(TABS):
                            pool.wait_ge(added[k], 16 * (TILES // TABS))

        def degree_rows(g, dve, loaded, dve_done, tabs, h_rows, per):
            dve.wait_ge(loaded, 16 * TABS * (g + 1))
            nc.vector.tensor_tensor(tabs[:, 0], tabs[:, 0], tabs[:, 1], ALU.add).then_inc(dve_done, 1)
            nc.vector.tensor_tensor(tabs[:, 2], tabs[:, 2], tabs[:, 3], ALU.add).then_inc(dve_done, 1)
            dve.wait_ge(dve_done, now(g, per, 2))
            nc.vector.tensor_tensor(tabs[:, 0], tabs[:, 0], tabs[:, 2], ALU.add).then_inc(dve_done, 1)
            dve.wait_ge(dve_done, now(g, per, 3))
            nc.vector.tensor_scalar(tabs[:, 1, :, 0:1], tabs[:, 0, :, P:P + 1], 1.0, None, ALU.max).then_inc(dve_done, 1)
            dve.wait_ge(dve_done, now(g, per, 4))
            nc.vector.reciprocal(tabs[:, 1, :, 1:2], tabs[:, 1, :, 0:1]).then_inc(dve_done, 1)
            dve.wait_ge(dve_done, now(g, per, 5))
            nc.vector.tensor_tensor(h_rows[:, :, :], tabs[:, 0, :, 0:P],
                                    tabs[:, 1, :, 1:2].to_broadcast([P, GW, P]), ALU.mult).then_inc(dve_done, 1)

        def layer0_nodes(m):
            with ExitStack() as st:
                def tmp(name, shape, dt=F32):
                    return st.enter_context(nc.sbuf_tensor(f"{name}_n{m}", shape, dt))
                tabs = tmp("tabs", [P, TABS, GW, HW])
                h_rows = tmp("h_rows", [P, GW, P])
                r_rows = tmp("r_rows", [P, GW, P])
                zT = tmp("zT", [P, GC])
                o_rows = tmp("o_rows", [P, GW, HW])
                with stage("loaded", "pe_done", "act_done", "dve_done", "stored", "filled") as (
                        block, loaded, pe_done, act_done, dve_done, stored, filled):
                    @block.sync
                    def _(sp):
                        nc.sync.sem_inc(stored, 16)
                        sp.wait_ge(filled, 1)
                        with loop(sp, G) as g:
                            sp.wait_ge(dve_done, prev(g, 7, 6))
                            for k in range(TABS):
                                sp.dma_start(tabs[:, k], windows(sums[m][k], g, HW)).then_inc(loaded, 16)
                            if m == 0:
                                sp.wait_ge(dve_done, now(g, 7, 7))
                                sp.dma_start(windows(h_tab, g, HW), o_rows[:, :, :]).then_inc(stored, 16)
                        if m == 0:
                            sp.wait_ge(stored, 16 * G + 16)

                    @block.vector
                    def _(dve):
                        nc.vector.memset(o_rows[:, :, P:HW], 1.0).then_inc(filled, 1)
                        nc.vector.sem_inc(dve_done, 7)
                        with loop(dve, G) as g:
                            dve.wait_ge(act_done, prev(g, 2, 1))
                            degree_rows(g, dve, loaded, dve_done, tabs, h_rows, 7)
                            dve.wait_ge(pe_done, now(g, 2, 2))
                            if m == 0:
                                dve.wait_ge(stored, 16 * g + 16)
                                nc.vector.tensor_tensor(o_rows[:, :, 0:P], flat[:, 1024:1024 + GC].rearrange("p (k f) -> p k f", k=GW),
                                                        bias_rows[:, 1:2, :].to_broadcast([P, GW, P]), ALU.add).then_inc(dve_done, 1)
                            else:
                                xg = two(xT[:, bass.ds(g * GC, GC)])
                                nc.vector.scalar_tensor_tensor(out=xg, in0=ps[:, 2:4, 0:HC], scalar=col(B03), in1=xg,
                                                               op0=ALU.add, op1=ALU.add).then_inc(dve_done, 1)

                    @block.scalar
                    def _(act):
                        nc.scalar.sem_inc(act_done, 2)
                        with loop(act, G) as g:
                            act.wait_ge(dve_done, now(g, 7, 6))
                            act.wait_ge(pe_done, prev(g, 2, 1))
                            nc.scalar.activation(r_rows[:, :, :], h_rows[:, :, :], ACT.Relu).then_inc(act_done, 1)
                            act.wait_ge(pe_done, now(g, 2, 1))
                            nc.scalar.copy(zT[:, :], flat[:, 0:GC]).then_inc(act_done, 1)

                    @block.tensor
                    def _(pe):
                        nc.tensor.sem_inc(pe_done, 2)
                        with loop(pe, G) as g:
                            pe.wait_ge(act_done, now(g, 2, 1))
                            for k in range(GW):
                                last = nc.tensor.transpose(flat[:, k * P:(k + 1) * P], r_rows[:, k, :], ident[:, :])
                            last.then_inc(pe_done, 1)
                            pe.wait_ge(act_done, now(g, 2, 2))
                            pe.wait_ge(dve_done, prev(g, 7, 7))
                            if m == 0:
                                for k in range(GW):
                                    last = nc.tensor.matmul(flat[:, 1024 + k * P:1024 + (k + 1) * P], zT[:, k * P:(k + 1) * P],
                                                            wt(W0[1]), start=True, stop=True)
                            else:
                                last = two_matmuls(pe, 2, wt(W0[2]), zT)
                            last.then_inc(pe_done, 1)

        def normalize(n, table):
            with ExitStack() as st:
                def tmp(name, shape, dt=F32):
                    return st.enter_context(nc.sbuf_tensor(f"{name}_ln{n}", shape, dt))
                cen, sq, sd, rstd, y = [tmp(k, [P, GC]) for k in ("cen", "sq", "sd", "rstd", "y")]
                rows = tmp("rows", [P, GW, P])
                with stage("zeroed", "pe_done", "act_done", "dve_done", "stored") as (
                        block, zeroed, pe_done, act_done, dve_done, stored):
                    @block.sync
                    def _(sp):
                        nc.sync.sem_inc(stored, 16)
                        with loop(sp, G) as g:
                            sp.wait_ge(act_done, now(g, 4, 4))
                            sp.dma_start(windows(table, g, P), rows[:, :, :]).then_inc(stored, 16)
                        sp.wait_ge(stored, 16 * G + 16)

                    @block.vector
                    def _(dve):
                        nc.vector.memset(xT[:, N:AW], 0.0).then_inc(zeroed, 1)
                        nc.vector.sem_inc(dve_done, 3)
                        dve.wait_ge(zeroed, 1)
                        with loop(dve, G) as g:
                            xg = two(xT[:, bass.ds(g * GC, GC)])
                            dve.wait_ge(pe_done, now(g, 3, 1))
                            nc.vector.tensor_tensor(two(cen[:, :]), xg, ps[:, 0:2, 0:HC], ALU.subtract).then_inc(dve_done, 1)
                            dve.wait_ge(act_done, now(g, 4, 2))
                            nc.vector.reciprocal(rstd[:, :], sd[:, :]).then_inc(dve_done, 1)
                            dve.wait_ge(dve_done, now(g, 3, 2))
                            dve.wait_ge(act_done, prev(g, 4, 3))
                            dve.wait_ge(pe_done, prev(g, 3, 3))
                            nc.vector.tensor_tensor(y[:, :], cen[:, :], rstd[:, :], ALU.mult).then_inc(dve_done, 1)

                    @block.tensor
                    def _(pe):
                        nc.tensor.sem_inc(pe_done, 3)
                        pe.wait_ge(zeroed, 1)
                        with loop(pe, G) as g:
                            xg = xT[:, bass.ds(g * GC, GC)]
                            pe.wait_ge(dve_done, prev(g, 3, 1))
                            two_matmuls(pe, 0, mean_mat[:, :], xg).then_inc(pe_done, 1)
                            pe.wait_ge(act_done, now(g, 4, 1))
                            two_matmuls(pe, 2, mean_mat[:, :], sq).then_inc(pe_done, 1)
                            pe.wait_ge(dve_done, now(g, 3, 3))
                            pe.wait_ge(act_done, prev(g, 4, 4))
                            for k in range(GW):
                                last = nc.tensor.transpose(flat[:, 2048 + k * P:2048 + (k + 1) * P], y[:, k * P:(k + 1) * P], ident[:, :])
                            last.then_inc(pe_done, 1)

                    @block.scalar
                    def _(act):
                        nc.scalar.sem_inc(act_done, 4)
                        with loop(act, G) as g:
                            act.wait_ge(dve_done, now(g, 3, 1))
                            nc.scalar.activation(sq[:, :], cen[:, :], ACT.Square).then_inc(act_done, 1)
                            act.wait_ge(pe_done, now(g, 3, 2))
                            nc.scalar.activation(two(sd[:, :]), ps[:, 2:4, 0:HC], ACT.Sqrt, bias=eps_col[:, 0:1]).then_inc(act_done, 1)
                            act.wait_ge(dve_done, now(g, 3, 3))
                            nc.scalar.copy(xT[:, bass.ds(g * GC, GC)], y[:, :]).then_inc(act_done, 1)
                            act.wait_ge(pe_done, now(g, 3, 3))
                            act.wait_ge(stored, 16 * g + 16)
                            nc.scalar.copy(rows[:, :, :], flat[:, 2048:2048 + GC].rearrange("p (k f) -> p k f", k=GW)).then_inc(act_done, 1)

        def gather_pass(n, table, heads, weighted=False, degree=False):
            width = heads * P
            parts = 2 if degree else heads
            with ExitStack() as st:
                def tmp(name, shape, dt=F32):
                    return st.enter_context(nc.sbuf_tensor(f"{name}_g{n}", shape, dt))
                rows = tmp("rows", [P, U, width])
                onehot = tmp("onehot", [P, 2, P])
                idx = tmp("idx", [P, 2, H], I32)
                names = [f"rows_in{j}" for j in range(U)] + ["cleared", "idx_copied", "begun", "matched", "tile_done", "added"]
                with stage(*names) as (block, *s):
                    rows_in = s[0:U]
                    cleared, idx_copied, begun, matched, tile_done, added = s[U:]
                    steps = TILES // U

                    @block.gpsimd
                    def _(pool):
                        with loop(pool, steps) as i:
                            for j in range(U):
                                if j % H == 0:
                                    pool.wait_ge(idx_copied, 2 * i + j // H + 1)
                                    nc.gpsimd.sem_inc(begun, 1)
                                nc.gpsimd.indirect_dma_start(
                                    rows[:, j, :], None, table,
                                    bass.IndirectOffsetOnAxis(ap=idx[:, j // H, j % H:j % H + 1], axis=0)).then_inc(rows_in[j], 16)

                    @block.scalar
                    def _(act):
                        with loop(act, steps) as i:
                            for h in range(2):
                                act.wait_ge(tile_done, prev(i, U, H * (h + 1)))
                                nc.scalar.copy(idx[:, h, :], src_idx[:, bass.ds(i * U + h * H, H)]).then_inc(idx_copied, 1)

                    @block.vector
                    def _(dve):
                        regs = [nc.vector.alloc_register(f"base{n}_{k}") for k in range(H)]
                        nc.vector.sem_inc(added, 2)
                        nc.vector.memset(acc[:, 0:parts, :], 0.0).then_inc(cleared, 1)
                        dve.wait_ge(cleared, 1)

                        def add(i, j, base):
                            dve.wait_ge(tile_done, now(i, U, j + 1))
                            dve.wait_ge(added, i * U + j + 2)
                            a = acc[:, 0:parts, bass.ds(base, P)]
                            nc.vector.tensor_tensor(a, a, ps[:, j % 2, 0:parts * P].rearrange("p (h n) -> p h n", h=parts),
                                                    ALU.add).then_inc(added, 1)

                        with loop(dve, steps) as i:
                            bases = []
                            for j in range(U):
                                if j % H == 0:
                                    nc.vector.load(regs, base_row[0:1, bass.ds(i * U + j, H)])
                                    bases += [nc.vector.snap(r, min_val=0, max_val=N - 1) for r in regs]
                                dve.wait_ge(tile_done, now(i, U, j - 1))
                                t = bass.ds(i * U + j, 1)
                                if weighted:
                                    nc.vector.tensor_scalar(onehot[:, j % 2, :], iota16[:, :], loc_col[:, t], ew_col[:, t],
                                                            ALU.is_equal, ALU.mult).then_inc(matched, 1)
                                else:
                                    nc.vector.tensor_scalar(onehot[:, j % 2, :], iota16[:, :], loc_col[:, t], None,
                                                            ALU.is_equal).then_inc(matched, 1)
                                if j:
                                    add(i, j - 1, bases[j - 1])
                            add(i, U - 1, bases[U - 1])

                    @block.tensor
                    def _(pe):
                        nc.tensor.sem_inc(tile_done, U)
                        with loop(pe, steps) as i:
                            for j in range(U):
                                pe.wait_ge(rows_in[j], 16 * i + 16)
                                pe.wait_ge(matched, i * U + j + 1)
                                pe.wait_ge(added, i * U + j + 1)
                                for h in range(heads):
                                    last = nc.tensor.matmul(ps[:, j % 2, h * P:(h + 1) * P], rows[:, j, h * P:(h + 1) * P],
                                                            onehot[:, j % 2, :], start=True, stop=True)
                                if degree:
                                    last = nc.tensor.matmul(ps[:, j % 2, P:2 * P], ones_mat[:, :], onehot[:, j % 2, :],
                                                            start=True, stop=True)
                                last.then_inc(tile_done, 1)

        def layer1_nodes():
            with ExitStack() as st:
                mix = st.enter_context(nc.sbuf_tensor("mix1", [P, GC], F32))
                hid = st.enter_context(nc.sbuf_tensor("hid1", [P, GC], F32))
                with stage("pe_done", "act_done", "dve_done") as (block, pe_done, act_done, dve_done):
                    @block.vector
                    def _(dve):
                        nc.vector.sem_inc(dve_done, 2)
                        with loop(dve, G) as g:
                            xg = xT[:, bass.ds(g * GC, GC)]
                            dve.wait_ge(pe_done, prev(g, 2, 1))
                            nc.vector.tensor_tensor(mix[:, :], xg, acc[:, 0, bass.ds(g * GC, GC)], ALU.add).then_inc(dve_done, 1)
                            dve.wait_ge(pe_done, now(g, 2, 2))
                            dve.wait_ge(dve_done, now(g, 2, 1))
                            nc.vector.scalar_tensor_tensor(out=two(xg), in0=ps[:, 2:4, 0:HC], scalar=col(B12), in1=two(xg),
                                                           op0=ALU.add, op1=ALU.add).then_inc(dve_done, 1)

                    @block.tensor
                    def _(pe):
                        nc.tensor.sem_inc(pe_done, 2)
                        with loop(pe, G) as g:
                            pe.wait_ge(dve_done, now(g, 2, 1))
                            pe.wait_ge(act_done, prev(g, 1, 1))
                            two_matmuls(pe, 0, wt(W1A), mix).then_inc(pe_done, 1)
                            pe.wait_ge(act_done, now(g, 1, 1))
                            pe.wait_ge(dve_done, prev(g, 2, 2))
                            two_matmuls(pe, 2, wt(W1B), hid).then_inc(pe_done, 1)

                    @block.scalar
                    def _(act):
                        nc.scalar.sem_inc(act_done, 1)
                        with loop(act, G) as g:
                            act.wait_ge(pe_done, now(g, 2, 1))
                            act.wait_ge(pe_done, prev(g, 2, 2))
                            nc.scalar.activation(two(hid[:, :]), ps[:, 0:2, 0:HC], ACT.Relu, bias=col(B11)).then_inc(act_done, 1)

        def layer2_keys():
            KW = HEADS * P
            with ExitStack() as st:
                def tmp(name, shape, dt=F32):
                    return st.enter_context(nc.sbuf_tensor(f"{name}_k", shape, dt))
                xg = tmp("xg", [P, GC])
                q, qq, qn = [tmp(k, [P, HEADS, GC]) for k in ("q", "qq", "qn")]
                k_rows, kk = [tmp(k, [P, GW, KW]) for k in ("k_rows", "kk")]
                knorm = tmp("knorm", [P, 3, GW * HEADS])
                zero = tmp("zero", [NP - N, KW])
                with stage("pe_done", "act_done", "dve_done", "q_out", "k_out", "zeroed", "pad_out") as (
                        block, pe_done, act_done, dve_done, q_out, k_out, zeroed, pad_out):
                    PN, AN, DN = 3, 5, 8

                    def q_banks(h):
                        return ps[:, 2 * h:2 * h + 2, 0:HC]

                    @block.tensor
                    def _(pe):
                        nc.tensor.sem_inc(pe_done, PN)
                        with loop(pe, G) as g:
                            pe.wait_ge(act_done, now(g, AN, 1))
                            for h in range(HEADS):
                                last = two_matmuls(pe, 2 * h, wt(WQ[h]), xg)
                            last.then_inc(pe_done, 1)
                            pe.wait_ge(dve_done, prev(g, DN, 2))
                            for k in range(GW):
                                last = nc.tensor.matmul(flat[:, 2048 + k * KW:2048 + (k + 1) * KW], xg[:, k * P:(k + 1) * P],
                                                        wts[:, WK[0]:WK[1] + 1, :].rearrange("p a n -> p (a n)"), start=True, stop=True)
                            last.then_inc(pe_done, 1)
                            pe.wait_ge(dve_done, now(g, DN, 1))
                            for h in range(HEADS):
                                last = two_matmuls(pe, 2 * h, ones_mat[:, :], qq[:, h, :])
                            last.then_inc(pe_done, 1)

                    @block.scalar
                    def _(act):
                        nc.scalar.sem_inc(act_done, AN)
                        with loop(act, G) as g:
                            act.wait_ge(pe_done, prev(g, PN, 2))
                            nc.scalar.copy(xg[:, :], xT[:, bass.ds(g * GC, GC)]).then_inc(act_done, 1)
                            act.wait_ge(pe_done, now(g, PN, 1))
                            act.wait_ge(dve_done, prev(g, DN, 7))
                            for h in range(HEADS):
                                nc.scalar.activation(two(q[:, h, :]), q_banks(h), ACT.Identity, bias=col(BQ[h])).then_inc(act_done, 1)
                            act.wait_ge(pe_done, now(g, PN, 3))
                            nc.scalar.activation(qq[:, :, :].rearrange("p h (b n) -> p (h b) n", b=2), ps[:, 0:4, 0:HC], ACT.Sqrt).then_inc(act_done, 1)
                            act.wait_ge(dve_done, now(g, DN, 4))
                            nc.scalar.activation(knorm[:, 1, :], knorm[:, 0, :], ACT.Sqrt).then_inc(act_done, 1)

                    @block.vector
                    def _(dve):
                        nc.vector.memset(zero[:, :], 0.0).then_inc(zeroed, 1)
                        nc.vector.sem_inc(dve_done, DN)
                        with loop(dve, G) as g:
                            dve.wait_ge(act_done, now(g, AN, 3))
                            nc.vector.tensor_tensor(qq[:, :, :], q[:, :, :], q[:, :, :], ALU.mult).then_inc(dve_done, 1)
                            dve.wait_ge(pe_done, now(g, PN, 2))
                            dve.wait_ge(k_out, 16 * g + 16)
                            nc.vector.tensor_tensor(k_rows[:, :, :], flat[:, 2048:2048 + GW * KW].rearrange("p (k f) -> p k f", k=GW),
                                                    bias_rows[:, 3:5, :].rearrange("p (o a) n -> p o (a n)", o=1).to_broadcast([P, GW, KW]),
                                                    ALU.add).then_inc(dve_done, 1)
                            dve.wait_ge(dve_done, now(g, DN, 2))
                            nc.vector.tensor_tensor(kk[:, :, :], k_rows[:, :, :], k_rows[:, :, :], ALU.mult).then_inc(dve_done, 1)
                            dve.wait_ge(dve_done, now(g, DN, 3))
                            nc.vector.tensor_reduce(knorm[:, 0, :], kk[:, :, :].rearrange("p k (h f) -> p (k h) f", h=HEADS),
                                                    AX.X, ALU.add).then_inc(dve_done, 1)
                            dve.wait_ge(act_done, now(g, AN, 4))
                            dve.wait_ge(q_out, 32 * g + 32)
                            nc.vector.reciprocal(qn[:, :, :], qq[:, :, :]).then_inc(dve_done, 1)
                            dve.wait_ge(act_done, now(g, AN, 5))
                            nc.vector.reciprocal(knorm[:, 2, :], knorm[:, 1, :]).then_inc(dve_done, 1)
                            dve.wait_ge(dve_done, now(g, DN, 5))
                            nc.vector.tensor_tensor(qn[:, :, :], qn[:, :, :], q[:, :, :], ALU.mult).then_inc(dve_done, 1)
                            dve.wait_ge(dve_done, now(g, DN, 6))
                            kh = k_rows[:, :, :].rearrange("p k (h f) -> p (k h) f", h=HEADS)
                            nc.vector.tensor_tensor(kh, kh, knorm[:, 2, :].unsqueeze(2).to_broadcast([P, GW * HEADS, P]),
                                                    ALU.mult).then_inc(dve_done, 1)

                    @block.sync
                    def _(sp):
                        nc.sync.sem_inc(q_out, 32)
                        nc.sync.sem_inc(k_out, 16)
                        with loop(sp, G) as g:
                            sp.wait_ge(dve_done, now(g, DN, 7))
                            for h in range(HEADS):
                                sp.dma_start(q_tab[h * P:(h + 1) * P, bass.ds(g * GC, GC)], qn[:, h, :]).then_inc(q_out, 16)
                            sp.wait_ge(dve_done, now(g, DN, 8))
                            sp.dma_start(windows(k_tab, g, KW), k_rows[:, :, :]).then_inc(k_out, 16)
                        sp.wait_ge(q_out, 32 * G + 32)
                        sp.wait_ge(k_out, 16 * G + 16)
                        sp.wait_ge(zeroed, 1)
                        sp.dma_start(k_tab[N:NP, :], zero[:, :]).then_inc(pad_out, 16)
                        sp.wait_ge(pad_out, 16)

        def layer2_keys_values(n, table, heads):
            KW = HEADS * P
            with ExitStack() as st:
                def tmp(name, shape, dt=F32):
                    return st.enter_context(nc.sbuf_tensor(f"{name}_kv{n}", shape, dt))
                k_rows = tmp("k_rows", [P, 2, GW, KW])
                x_rows = tmp("x_rows", [P, 2, GW, heads * P])
                with stage("rows_in", "rows_in_last", "pe_done", "dve_done", "cleared") as (
                        block, rows_in, rows_in_last, pe_done, dve_done, cleared):
                    @block.sync
                    def _(sp):
                        with loop(sp, G) as g:
                            sp.wait_ge(pe_done, g + 1)
                            sp.dma_start(k_rows[:, 0], windows(k_tab, g, KW)).then_inc(rows_in, 16)
                            sp.dma_start(x_rows[:, 0], windows(table, g, heads * P)).then_inc(rows_in, 16)

                    @block.tensor
                    def _(pe):
                        nc.tensor.sem_inc(pe_done, 1)
                        with loop(pe, G) as g:
                            pe.wait_ge(rows_in, 32 * g + 32)
                            pe.wait_ge(dve_done, prev(g, 2, 2))
                            for h in range(HEADS):
                                at = (h % heads) * P
                                for k in range(GW):
                                    nc.tensor.matmul(ps[:, h, 0:P], k_rows[:, 0, k, h * P:(h + 1) * P], x_rows[:, 0, k, at:at + P],
                                                     start=(k == 0), stop=(k == GW - 1))
                                for k in range(GW):
                                    nc.tensor.matmul(ps[:, 2 + h, 0:1], x_rows[:, 0, k, at:at + P], ones_mat[:, 0:1],
                                                     start=(k == 0), stop=(k == GW - 1))
                                for k in range(GW):
                                    last = nc.tensor.matmul(ps[:, 4 + h, 0:1], k_rows[:, 0, k, h * P:(h + 1) * P], ones_mat[:, 0:1],
                                                            start=(k == 0), stop=(k == GW - 1))
                            last.then_inc(pe_done, 1)

                    @block.vector
                    def _(dve):
                        nc.vector.memset(kv[:, :, :], 0.0).then_inc(cleared, 1)
                        nc.vector.memset(kv_sums[:, :], 0.0).then_inc(cleared, 1)
                        nc.vector.sem_inc(dve_done, 2)
                        dve.wait_ge(cleared, 2)
                        with loop(dve, G) as g:
                            dve.wait_ge(pe_done, g + 2)
                            dve.wait_ge(dve_done, prev(g, 2, 2))
                            nc.vector.tensor_tensor(kv[:, :, :], kv[:, :, :], ps[:, 0:2, 0:P], ALU.add).then_inc(dve_done, 1)
                            nc.vector.tensor_tensor(kv_sums[:, :], kv_sums[:, :], ps[:, 2:6, 0:1].rearrange("p b n -> p (b n)"), ALU.add).then_inc(dve_done, 1)
                        dve.wait_ge(dve_done, 2 * G + 2)
                        for h in range(HEADS):
                            nc.vector.tensor_copy(key_sum[:, h, :], kv_sums[:, HEADS + h:HEADS + h + 1].to_broadcast([P, P])).then_inc(cleared, 1)

        def layer2_denominators():
            with ExitStack() as st:
                def tmp(name, shape, dt=F32):
                    return st.enter_context(nc.sbuf_tensor(f"{name}_d", shape, dt))
                q, rden, den = [tmp(k, [P, HEADS, GC]) for k in ("q", "rden", "den")]
                part = tmp("part", [P, GC])
                zero = tmp("zero", [P, 2 * (NP - N)])
                with stage("q_in", "pe_done", "dve_done", "stored", "zeroed", "pad_out") as (
                        block, q_in, pe_done, dve_done, stored, zeroed, pad_out):
                    DN = 5

                    @block.sync
                    def _(sp):
                        nc.sync.sem_inc(stored, 64)
                        with loop(sp, G) as g:
                            c = bass.ds(g * GC, GC)
                            sp.wait_ge(stored, 64 * g + 64)
                            for h in range(HEADS):
                                sp.dma_start(q[:, h, :], q_tab[h * P:(h + 1) * P, c]).then_inc(q_in, 16)
                            sp.wait_ge(dve_done, now(g, DN, 3))
                            for h in range(HEADS):
                                sp.dma_start(q_tab[h * P:(h + 1) * P, c], q[:, h, :]).then_inc(stored, 16)
                                sp.dma_start(rden_tab[h * P:(h + 1) * P, c], rden[:, h, :]).then_inc(stored, 16)
                        sp.wait_ge(stored, 64 * G + 64)
                        sp.wait_ge(zeroed, 1)
                        for h in range(HEADS):
                            for t in (q_tab, rden_tab):
                                sp.dma_start(t[h * P:(h + 1) * P, N:NP], zero[:, 0:NP - N]).then_inc(pad_out, 16)
                        sp.wait_ge(pad_out, 16 * 2 * HEADS)

                    @block.tensor
                    def _(pe):
                        nc.tensor.sem_inc(pe_done, 2)
                        with loop(pe, G) as g:
                            pe.wait_ge(q_in, 32 * g + 32)
                            pe.wait_ge(dve_done, prev(g, DN, 1))
                            for h in range(HEADS):
                                last = two_matmuls(pe, 2 * h, key_sum[:, h, :], q[:, h, :])
                            last.then_inc(pe_done, 1)
                            pe.wait_ge(dve_done, prev(g, DN, 4))
                            for h in range(HEADS):
                                for b in range(2):
                                    last = nc.tensor.matmul(ps[:, 4 + b, 0:HC], wt(WO[h][0]), xT[:, bass.ds(g * GC + b * HC, HC)],
                                                            start=(h == 0), stop=(h == HEADS - 1))
                            last.then_inc(pe_done, 1)

                    @block.vector
                    def _(dve):
                        nc.vector.memset(zero[:, :], 0.0).then_inc(zeroed, 1)
                        nc.vector.sem_inc(dve_done, DN)
                        with loop(dve, G) as g:
                            xg = xT[:, bass.ds(g * GC, GC)]
                            dve.wait_ge(pe_done, now(g, 2, 1))
                            nc.vector.tensor_scalar(den[:, :, :].rearrange("p h (b n) -> p (h b) n", b=2), ps[:, 0:4, 0:HC],
                                                    float(N), None, ALU.add).then_inc(dve_done, 1)
                            dve.wait_ge(dve_done, now(g, DN, 1))
                            dve.wait_ge(stored, 64 * g + 64)
                            nc.vector.reciprocal(rden[:, :, :], den[:, :, :]).then_inc(dve_done, 1)
                            dve.wait_ge(dve_done, now(g, DN, 2))
                            nc.vector.tensor_tensor(q[:, :, :], q[:, :, :], rden[:, :, :], ALU.mult).then_inc(dve_done, 1)
                            dve.wait_ge(pe_done, now(g, 2, 2))
                            dve.wait_ge(dve_done, prev(g, DN, 5))
                            nc.vector.tensor_scalar(two(part[:, :]), ps[:, 4:6, 0:HC], 1.0 / HEADS, col(BOH), ALU.mult, ALU.add).then_inc(dve_done, 1)
                            dve.wait_ge(dve_done, now(g, DN, 4))
                            nc.vector.tensor_tensor(xg, xg, part[:, :], ALU.add).then_inc(dve_done, 1)

        def layer2_degrees():
            with stage("dve_done", "deg_out") as (block, dve_done, deg_out):
                @block.vector
                def _(dve):
                    nc.vector.tensor_scalar(dinv[:, :], acc[:, 1, 0:NP], 1.0, None, ALU.max).then_inc(dve_done, 1)
                    dve.wait_ge(dve_done, 1)
                    nc.vector.reciprocal(dinv[:, :], dinv[:, :]).then_inc(dve_done, 1)
                    dve.wait_ge(dve_done, 2)
                    nc.vector.tensor_scalar(dinv[:, :], dinv[:, :], 0.5, None, ALU.mult).then_inc(dve_done, 1)

                @block.sync
                def _(sp):
                    sp.dma_start(deg_tab, acc[:, 1, 0:NP]).then_inc(deg_out, 16)
                    sp.wait_ge(deg_out, 16)

        def layer2_step(step):
            before_last = step == ORDER - 1
            with ExitStack() as st:
                def tmp(name, shape, dt=F32):
                    return st.enter_context(nc.sbuf_tensor(f"{name}_s{step}", shape, dt))
                q, rden, xh, mean = [tmp(k, [P, HEADS, GC]) for k in ("q", "rden", "xh", "mean")]
                rows = tmp("rows", [P, GW, HEADS * P])
                y_rows = tmp("y_rows", [P, GW, P])
                with stage("loaded", "pe_done", "act_done", "dve_done", "stored") as (
                        block, loaded, pe_done, act_done, dve_done, stored):
                    PN, AN, DN, OUT = 4 + before_last, 2 + before_last, 7, 16 + 16 * before_last

                    @block.sync
                    def _(sp):
                        nc.sync.sem_inc(stored, OUT)
                        with loop(sp, G) as g:
                            c = bass.ds(g * GC, GC)
                            sp.wait_ge(dve_done, prev(g, DN, 4))
                            for h in range(HEADS):
                                sp.dma_start(q[:, h, :], q_tab[h * P:(h + 1) * P, c]).then_inc(loaded, 16)
                                sp.dma_start(rden[:, h, :], rden_tab[h * P:(h + 1) * P, c]).then_inc(loaded, 16)
                            sp.wait_ge(act_done, now(g, AN, 2))
                            sp.dma_start(windows(xh_tab, g, HEADS * P), rows[:, :, :]).then_inc(stored, 16)
                            if before_last:
                                sp.wait_ge(act_done, now(g, AN, 3))
                                sp.dma_start(windows(x_tab, g, P), y_rows[:, :, :]).then_inc(stored, 16)
                        sp.wait_ge(stored, OUT * G + OUT)

                    @block.tensor
                    def _(pe):
                        nc.tensor.sem_inc(pe_done, PN)
                        with loop(pe, G) as g:
                            pe.wait_ge(loaded, 64 * g + 64)
                            pe.wait_ge(dve_done, prev(g, DN, 4))
                            if before_last:
                                pe.wait_ge(act_done, prev(g, AN, 3))
                            for h in range(HEADS):
                                last = two_matmuls(pe, 2 * h, kv[:, h, :], q[:, h, :])
                            last.then_inc(pe_done, 1)
                            pe.wait_ge(dve_done, now(g, DN, 6))
                            pe.wait_ge(dve_done, prev(g, DN, 7))
                            for h in range(HEADS):
                                last = two_matmuls(pe, 4, wt(WO[h][step]), xh[:, h, :], start=(h == 0), stop=(h == HEADS - 1))
                            last.then_inc(pe_done, 1)
                            for h in range(HEADS):
                                pe.wait_ge(act_done, now(g, AN, h) if h else prev(g, AN, 2))
                                for k in range(GW):
                                    last = nc.tensor.transpose(flat[:, 3072 + k * P:3072 + (k + 1) * P], xh[:, h, k * P:(k + 1) * P], ident[:, :])
                                last.then_inc(pe_done, 1)
                            if before_last:
                                for k in range(GW):
                                    for h in range(HEADS):
                                        last = nc.tensor.matmul(flat[:, k * P:(k + 1) * P], xh[:, h, k * P:(k + 1) * P], wt(WO[h][ORDER]),
                                                                start=(h == 0), stop=(h == HEADS - 1))
                                last.then_inc(pe_done, 1)

                    @block.scalar
                    def _(act):
                        nc.scalar.sem_inc(act_done, AN)
                        with loop(act, G) as g:
                            act.wait_ge(stored, OUT * g + OUT)
                            for h in range(HEADS):
                                act.wait_ge(pe_done, now(g, PN, 3 + h))
                                nc.scalar.copy(rows[:, :, h * P:(h + 1) * P],
                                               flat[:, 3072:3072 + GC].rearrange("p (k f) -> p k f", k=GW)).then_inc(act_done, 1)
                            if before_last:
                                act.wait_ge(pe_done, now(g, PN, 5))
                                nc.scalar.copy(y_rows[:, :, :], flat[:, 0:GC].rearrange("p (k f) -> p k f", k=GW)).then_inc(act_done, 1)

                    @block.vector
                    def _(dve):
                        nc.vector.sem_inc(dve_done, DN)
                        with loop(dve, G) as g:
                            c = bass.ds(g * GC, GC)
                            for h in range(HEADS):
                                nc.vector.tensor_tensor(mean[:, h, :], acc[:, h if step > 1 else 0, c], dinv[:, c], ALU.mult).then_inc(dve_done, 1)
                            dve.wait_ge(loaded, 64 * g + 64)
                            dve.wait_ge(pe_done, now(g, PN, 1))
                            dve.wait_ge(pe_done, prev(g, PN, PN))
                            for h in range(HEADS):
                                nc.vector.scalar_tensor_tensor(out=two(xh[:, h, :]), in0=two(rden[:, h, :]), scalar=kv_sums[:, h:h + 1],
                                                               in1=ps[:, 2 * h:2 * h + 2, 0:HC], op0=ALU.mult, op1=ALU.add).then_inc(dve_done, 1)
                            for h in range(HEADS):
                                dve.wait_ge(dve_done, now(g, DN, 3 + h))
                                nc.vector.tensor_tensor(xh[:, h, :], xh[:, h, :], mean[:, h, :], ALU.add).then_inc(dve_done, 1)
                            dve.wait_ge(pe_done, now(g, PN, 2))
                            nc.vector.scalar_tensor_tensor(out=two(xT[:, c]), in0=ps[:, 4:6, 0:HC], scalar=1.0 / HEADS, in1=two(xT[:, c]),
                                                           op0=ALU.mult, op1=ALU.add).then_inc(dve_done, 1)

        def layer2_last():
            with ExitStack() as st:
                def tmp(name, shape, dt=F32):
                    return st.enter_context(nc.sbuf_tensor(f"{name}_l", shape, dt))
                q, rden, att = [tmp(k, [P, HEADS, GC]) for k in ("q", "rden", "att")]
                mean, both = [tmp(k, [P, GC]) for k in ("mean", "both")]
                with stage("loaded", "pe_done", "dve_done") as (block, loaded, pe_done, dve_done):
                    DN = 5

                    @block.sync
                    def _(sp):
                        with loop(sp, G) as g:
                            c = bass.ds(g * GC, GC)
                            sp.wait_ge(dve_done, prev(g, DN, 3))
                            for h in range(HEADS):
                                sp.dma_start(q[:, h, :], q_tab[h * P:(h + 1) * P, c]).then_inc(loaded, 16)
                                sp.dma_start(rden[:, h, :], rden_tab[h * P:(h + 1) * P, c]).then_inc(loaded, 16)

                    @block.tensor
                    def _(pe):
                        nc.tensor.sem_inc(pe_done, 2)
                        with loop(pe, G) as g:
                            pe.wait_ge(loaded, 64 * g + 64)
                            pe.wait_ge(dve_done, prev(g, DN, 3))
                            for h in range(HEADS):
                                last = two_matmuls(pe, 2 * h, kv[:, h, :], q[:, h, :])
                            last.then_inc(pe_done, 1)
                            pe.wait_ge(dve_done, now(g, DN, 3))
                            pe.wait_ge(dve_done, prev(g, DN, 4))
                            for h in range(HEADS):
                                last = two_matmuls(pe, 4, wt(WO[h][ORDER]), att[:, h, :], start=(h == 0), stop=(h == HEADS - 1))
                            last.then_inc(pe_done, 1)

                    @block.vector
                    def _(dve):
                        nc.vector.sem_inc(dve_done, DN)
                        with loop(dve, G) as g:
                            c = bass.ds(g * GC, GC)
                            dve.wait_ge(dve_done, prev(g, DN, 4))
                            nc.vector.tensor_tensor(mean[:, :], acc[:, 0, c], dinv[:, c], ALU.mult).then_inc(dve_done, 1)
                            dve.wait_ge(loaded, 64 * g + 64)
                            dve.wait_ge(pe_done, now(g, 2, 1))
                            dve.wait_ge(pe_done, prev(g, 2, 2))
                            for h in range(HEADS):
                                nc.vector.scalar_tensor_tensor(out=two(att[:, h, :]), in0=two(rden[:, h, :]), scalar=kv_sums[:, h:h + 1],
                                                               in1=ps[:, 2 * h:2 * h + 2, 0:HC], op0=ALU.mult, op1=ALU.add).then_inc(dve_done, 1)
                            dve.wait_ge(pe_done, now(g, 2, 2))
                            dve.wait_ge(dve_done, prev(g, DN, 5))
                            dve.wait_ge(dve_done, now(g, DN, 1))
                            nc.vector.tensor_tensor(two(both[:, :]), two(mean[:, :]), ps[:, 4:6, 0:HC], ALU.add).then_inc(dve_done, 1)
                            dve.wait_ge(dve_done, now(g, DN, 4))
                            nc.vector.scalar_tensor_tensor(out=xT[:, c], in0=both[:, :], scalar=1.0 / HEADS, in1=xT[:, c],
                                                           op0=ALU.mult, op1=ALU.add).then_inc(dve_done, 1)

        def layer3_tables():
            with ExitStack() as st:
                def tmp(name, shape, dt=F32):
                    return st.enter_context(nc.sbuf_tensor(f"{name}_t", shape, dt))
                xg = tmp("xg", [P, GC])
                p_rows, q_rows = [tmp(k, [P, GW, P]) for k in ("p_rows", "q_rows")]
                with stage("pe_done", "act_done", "dve_done", "stored") as (block, pe_done, act_done, dve_done, stored):
                    def bank_rows(m):
                        return flat[:, 1024 * m:1024 * m + GC].rearrange("p (k f) -> p k f", k=GW)

                    @block.scalar
                    def _(act):
                        nc.scalar.sem_inc(act_done, 2)
                        with loop(act, G) as g:
                            act.wait_ge(pe_done, g + 1)
                            nc.scalar.copy(xg[:, :], xT[:, bass.ds(g * GC, GC)]).then_inc(act_done, 1)
                            act.wait_ge(pe_done, g + 2)
                            act.wait_ge(stored, 32 * g + 32)
                            nc.scalar.copy(p_rows[:, :, :], bank_rows(0)).then_inc(act_done, 1)

                    @block.tensor
                    def _(pe):
                        nc.tensor.sem_inc(pe_done, 1)
                        with loop(pe, G) as g:
                            pe.wait_ge(act_done, now(g, 2, 1))
                            pe.wait_ge(dve_done, g + 1)
                            for m in range(2):
                                for k in range(GW):
                                    last = nc.tensor.matmul(flat[:, 1024 * m + k * P:1024 * m + (k + 1) * P], xg[:, k * P:(k + 1) * P],
                                                            wt(W3[m]), start=True, stop=True)
                            last.then_inc(pe_done, 1)

                    @block.vector
                    def _(dve):
                        nc.vector.sem_inc(dve_done, 1)
                        with loop(dve, G) as g:
                            dve.wait_ge(pe_done, g + 2)
                            dve.wait_ge(stored, 32 * g + 32)
                            nc.vector.tensor_tensor(q_rows[:, :, :], bank_rows(1), bias_rows[:, 2:3, :].to_broadcast([P, GW, P]),
                                                    ALU.add).then_inc(dve_done, 1)

                    @block.sync
                    def _(sp):
                        nc.sync.sem_inc(stored, 32)
                        with loop(sp, G) as g:
                            sp.wait_ge(act_done, now(g, 2, 2))
                            sp.dma_start(windows(p_tab, g, P), p_rows[:, :, :]).then_inc(stored, 16)
                            sp.wait_ge(dve_done, g + 2)
                            sp.dma_start(windows(q3_tab, g, P), q_rows[:, :, :]).then_inc(stored, 16)
                        sp.wait_ge(stored, 32 * G + 32)

        def message_pass():
            W = 4
            with ExitStack() as st:
                def tmp(name, shape, dt=F32):
                    return st.enter_context(nc.sbuf_tensor(f"{name}_m", shape, dt))
                rows = tmp("rows", [P, U, P])
                attr = tmp("attr", [P, 2, H, P])
                win = tmp("win", [P, W, P])
                onehot = tmp("onehot", [P, 4, P])
                turn = tmp("turn", [P, 2, 2, P])
                pre, hid = tmp("pre", [P, 2, P]), tmp("hid", [P, 2, P])
                idx = tmp("idx", [P, 2, H], I32)
                names = [f"rows_in{j}" for j in range(U)] + [f"win_in{k}" for k in range(W)] + ["attr_in0", "attr_in1"]
                names += ["cleared", "idx_copied", "begun", "matched", "turned", "copied", "mixed", "met", "rectified", "summed", "added"]
                with stage(*names) as (block, *s):
                    rows_in, win_in, attr_in = s[0:U], s[U:U + W], s[U + W:U + W + 2]
                    cleared, idx_copied, begun, matched, turned, copied, mixed, met, rectified, summed, added = s[U + W + 2:]
                    steps = TILES // U

                    @block.gpsimd
                    def _(pool):
                        with loop(pool, steps) as i:
                            for j in range(U):
                                if j % H == 0:
                                    pool.wait_ge(idx_copied, 2 * i + j // H + 1)
                                    nc.gpsimd.sem_inc(begun, 1)
                                nc.gpsimd.indirect_dma_start(
                                    rows[:, j, :], None, p_tab,
                                    bass.IndirectOffsetOnAxis(ap=idx[:, j // H, j % H:j % H + 1], axis=0)).then_inc(rows_in[j], 16)

                    @block.sync
                    def _(sp):
                        regs = [nc.sync.alloc_register(f"msg_base{k}") for k in range(H)]

                        def step(i, tiles):
                            for h in range(2):
                                nc.sync.load(regs, base_row[0:1, bass.ds(i * U + h * H, H)])
                                base = [nc.sync.snap(r, min_val=0, max_val=N - 1) for r in regs]
                                sp.wait_ge(turned, prev(i, U, H * (h + 1)))
                                whole = min(H, tiles - h * H)
                                sp.dma_start(attr[:, h, 0:whole, :],
                                             edge_attr_128[bass.ds((i * U + h * H) * P, whole * P), :].rearrange("(t p) f -> p t f", p=P)
                                             ).then_inc(attr_in[h], 16)
                                if whole < H:
                                    sp.dma_start(attr[0:REST, h, whole, :], edge_attr_128[FULL * P:E, :]).then_inc(attr_in[h], 16)
                                for k in range(H):
                                    j = h * H + k
                                    sp.wait_ge(mixed, i * U + j + 1)
                                    sp.dma_start(win[:, j % W, :], q3_tab[bass.ds(base[k], P), :]).then_inc(win_in[j % W], 16)

                        with loop(sp, steps - 1) as i:
                            step(i, U)
                        step(steps - 1, FULL - (steps - 1) * U)

                    @block.vector
                    def _(dve):
                        regs = [nc.vector.alloc_register(f"msg_sum_base{k}") for k in range(H)]
                        nc.vector.sem_inc(met, U)
                        nc.vector.sem_inc(added, 2)
                        nc.vector.memset(acc[:, 0, :], 0.0).then_inc(cleared, 1)
                        dve.wait_ge(cleared, 1)

                        def meet(i, j):
                            dve.wait_ge(mixed, i * U + j + 1 + W)
                            dve.wait_ge(rows_in[j], 16 * i + 16)
                            dve.wait_ge(rectified, i * U + j + 1)
                            nc.vector.tensor_tensor(pre[:, j % 2, :], ps[:, 2 + j % 2, 0:P], rows[:, j, :], ALU.add).then_inc(met, 1)

                        def add(i, j, base):
                            dve.wait_ge(summed, i * U + j + 5)
                            dve.wait_ge(added, i * U + j + 2)
                            a = acc[:, 0, bass.ds(base, P)]
                            nc.vector.tensor_tensor(a, a, ps[:, 4 + j % 2, 0:P], ALU.add).then_inc(added, 1)

                        with loop(dve, steps) as i:
                            bases = []
                            for j in range(U + 2):
                                if j < U:
                                    if j % H == 0:
                                        nc.vector.load(regs, base_row[0:1, bass.ds(i * U + j, H)])
                                        bases += [nc.vector.snap(r, min_val=0, max_val=N - 1) for r in regs]
                                    dve.wait_ge(summed, i * U + j + 1)
                                    nc.vector.tensor_scalar(onehot[:, j % 4, :], iota16[:, :], loc_col[:, bass.ds(i * U + j, 1)], None,
                                                            ALU.is_equal).then_inc(matched, 1)
                                if 1 <= j <= U:
                                    meet(i, j - 1)
                                if j >= 2:
                                    add(i, j - 2, bases[j - 2])

                    @block.tensor
                    def _(pe):
                        nc.tensor.sem_inc(turned, U)
                        nc.tensor.sem_inc(mixed, W)
                        nc.tensor.sem_inc(summed, 4)

                        def mix(i, j):
                            pe.wait_ge(copied, i * U + j + 3)
                            pe.wait_ge(win_in[j % W], 16 * (i * (U // W) + j // W + 1))
                            pe.wait_ge(met, prev(i, U, 0) + U + j - 1)
                            nc.tensor.matmul(ps[:, 2 + j % 2, 0:P], turn[:, j % 2, 0, :], win[:, j % W, :], start=True, stop=False)
                            nc.tensor.matmul(ps[:, 2 + j % 2, 0:P], turn[:, j % 2, 1, :], wt(W3[2]), start=False, stop=True).then_inc(mixed, 1)

                        def total(i, j):
                            pe.wait_ge(rectified, i * U + j + 3)
                            pe.wait_ge(added, i * U + j + 1)
                            nc.tensor.matmul(ps[:, 4 + j % 2, 0:P], hid[:, j % 2, :], onehot[:, j % 4, :], start=True, stop=True).then_inc(summed, 1)

                        def step(i, last):
                            for j in range(U + 2):
                                if j < U:
                                    if j % H == 0:
                                        pe.wait_ge(attr_in[j // H], 16 * i + 16 + 16 * (last and j >= H))
                                    pe.wait_ge(matched, i * U + j + 1)
                                    pe.wait_ge(copied, i * U + j + 1)
                                    nc.tensor.transpose(ps[:, j % 2, 0:P], onehot[:, j % 4, :], ident[:, :])
                                    nc.tensor.transpose(ps[:, j % 2, P:2 * P], attr[:, j // H, j % H, :], ident[:, :]).then_inc(turned, 1)
                                if 1 <= j <= U:
                                    mix(i, j - 1)
                                if j >= 2:
                                    total(i, j - 2)

                        with loop(pe, steps - 1) as i:
                            step(i, False)
                        step(steps - 1, True)

                    @block.scalar
                    def _(act):
                        nc.scalar.sem_inc(copied, 2)
                        nc.scalar.sem_inc(rectified, 2)

                        def rectify(i, j):
                            act.wait_ge(met, i * U + U + j + 1)
                            act.wait_ge(summed, i * U + j + 3)
                            nc.scalar.activation(hid[:, j % 2, :], pre[:, j % 2, :], ACT.Relu).then_inc(rectified, 1)

                        with loop(act, steps) as i:
                            for j in range(U):
                                if j % H == 0:
                                    act.wait_ge(met, prev(i, U, j + H))
                                    nc.scalar.copy(idx[:, j // H, :], src_idx[:, bass.ds(i * U + j, H)]).then_inc(idx_copied, 1)
                                act.wait_ge(turned, now(i, U, j + 1))
                                act.wait_ge(mixed, i * U + j + 3)
                                nc.scalar.copy(turn[:, j % 2, :, :], ps[:, j % 2, 0:2 * P].rearrange("p (a n) -> p a n", a=2)).then_inc(copied, 1)
                                if j:
                                    rectify(i, j - 1)
                            rectify(i, U - 1)

        def layer3_nodes():
            with ExitStack() as st:
                def tmp(name, shape, dt=F32):
                    return st.enter_context(nc.sbuf_tensor(f"{name}_u", shape, dt))
                deg, msg, r, z, hn, cand, diff = [tmp(k, [P, GC]) for k in ("deg", "msg", "r", "z", "hn", "cand", "diff")]
                with stage("deg_in", "pe_done", "act_done", "dve_done") as (block, deg_in, pe_done, act_done, dve_done):
                    PN, AN, DN = 2, 3, 7

                    @block.sync
                    def _(sp):
                        with loop(sp, G) as g:
                            sp.wait_ge(dve_done, prev(g, DN, 1))
                            sp.dma_start(deg[:, :], deg_tab[:, bass.ds(g * GC, GC)]).then_inc(deg_in, 16)

                    @block.tensor
                    def _(pe):
                        nc.tensor.sem_inc(pe_done, PN)

                        def gate(bank, pairs):
                            for n, (w, rhs) in enumerate(pairs):
                                for b in range(2):
                                    last = nc.tensor.matmul(ps[:, bank + b, 0:HC], wt(w), rhs(b), start=(n == 0), stop=(n == len(pairs) - 1))
                            return last

                        with loop(pe, G) as g:
                            def sums(b):
                                return acc[:, 0, bass.ds(g * GC + b * HC, HC)]

                            def xs(b):
                                return xT[:, bass.ds(g * GC + b * HC, HC)]

                            def msgs(b):
                                return msg[:, b * HC:(b + 1) * HC]
                            pe.wait_ge(dve_done, prev(g, DN, 2))
                            gate(0, [(W3O, sums)]).then_inc(pe_done, 1)
                            pe.wait_ge(dve_done, now(g, DN, 1))
                            pe.wait_ge(act_done, prev(g, AN, 2))
                            pe.wait_ge(dve_done, prev(g, DN, 3))
                            gate(2, [(WIH[0], msgs), (WHH[0], xs)])
                            gate(4, [(WIH[1], msgs), (WHH[1], xs)])
                            gate(6, [(WIH[2], msgs)])
                            gate(0, [(WHH[2], xs)]).then_inc(pe_done, 1)

                    @block.scalar
                    def _(act):
                        nc.scalar.sem_inc(act_done, AN)
                        with loop(act, G) as g:
                            act.wait_ge(pe_done, now(g, PN, 2))
                            act.wait_ge(dve_done, prev(g, DN, 5))
                            nc.scalar.activation(two(r[:, :]), ps[:, 2:4, 0:HC], ACT.Sigmoid, bias=col(BRZ[0])).then_inc(act_done, 1)
                            nc.scalar.activation(two(z[:, :]), ps[:, 4:6, 0:HC], ACT.Sigmoid, bias=col(BRZ[1])).then_inc(act_done, 1)
                            act.wait_ge(dve_done, now(g, DN, 3))
                            act.wait_ge(dve_done, prev(g, DN, 6))
                            nc.scalar.activation(cand[:, :], hn[:, :], ACT.Tanh, bias=col(BIH[2])).then_inc(act_done, 1)

                    @block.vector
                    def _(dve):
                        nc.vector.sem_inc(dve_done, DN)
                        with loop(dve, G) as g:
                            xg = xT[:, bass.ds(g * GC, GC)]
                            dve.wait_ge(pe_done, now(g, PN, 1))
                            dve.wait_ge(deg_in, 16 * g + 16)
                            dve.wait_ge(pe_done, prev(g, PN, 2))
                            nc.vector.scalar_tensor_tensor(out=two(msg[:, :]), in0=two(deg[:, :]), scalar=col(B32), in1=ps[:, 0:2, 0:HC],
                                                           op0=ALU.mult, op1=ALU.add).then_inc(dve_done, 1)
                            dve.wait_ge(act_done, now(g, AN, 1))
                            dve.wait_ge(act_done, prev(g, AN, 3))
                            nc.vector.scalar_tensor_tensor(out=two(hn[:, :]), in0=ps[:, 0:2, 0:HC], scalar=col(BHH[2]), in1=two(r[:, :]),
                                                           op0=ALU.add, op1=ALU.mult).then_inc(dve_done, 1)
                            dve.wait_ge(dve_done, now(g, DN, 2))
                            nc.vector.tensor_tensor(two(hn[:, :]), two(hn[:, :]), ps[:, 6:8, 0:HC], ALU.add).then_inc(dve_done, 1)
                            dve.wait_ge(act_done, now(g, AN, 3))
                            nc.vector.tensor_tensor(diff[:, :], xg, cand[:, :], ALU.subtract).then_inc(dve_done, 1)
                            dve.wait_ge(dve_done, now(g, DN, 4))
                            nc.vector.tensor_tensor(diff[:, :], diff[:, :], z[:, :], ALU.mult).then_inc(dve_done, 1)
                            dve.wait_ge(dve_done, now(g, DN, 5))
                            nc.vector.tensor_tensor(diff[:, :], diff[:, :], cand[:, :], ALU.add).then_inc(dve_done, 1)
                            dve.wait_ge(dve_done, now(g, DN, 6))
                            dve.wait_ge(pe_done, now(g, PN, 2))
                            nc.vector.tensor_tensor(xg, xg, diff[:, :], ALU.add).then_inc(dve_done, 1)

        def store_output():
            with stage("stored") as (block, stored):
                @block.sync
                def _(sp):
                    sp.dma_start(out, x_tab[0:N, :]).then_inc(stored, 16)
                    sp.wait_ge(stored, 16)

        run = [load_weights, prepare_edges, scatter_rows, first_linear, lambda: scatter_pass(0), lambda: layer0_nodes(0),
               lambda: scatter_pass(1), lambda: layer0_nodes(1), lambda: normalize(0, x_tab),
               lambda: gather_pass(0, x_tab, 1, weighted=True), layer1_nodes, lambda: normalize(1, x_tab),
               layer2_keys, lambda: layer2_keys_values(0, x_tab, 1), layer2_denominators,
               lambda: gather_pass(1, x_tab, 1, degree=True), layer2_degrees, lambda: layer2_step(1),
               lambda: layer2_keys_values(1, xh_tab, HEADS), lambda: gather_pass(2, xh_tab, HEADS), lambda: layer2_step(2),
               lambda: layer2_keys_values(2, xh_tab, HEADS), lambda: gather_pass(3, xh_tab, HEADS), lambda: layer2_step(3),
               lambda: layer2_keys_values(3, xh_tab, HEADS), lambda: gather_pass(4, x_tab, 1), layer2_last,
               lambda: normalize(2, x_tab), layer3_tables, message_pass, layer3_nodes, lambda: normalize(3, x_tab), store_output]
        for f in run[0:upto + 1]:
            f()


_INS = ["x", "src", "dst", "edge_attr_128", "edge_weight", "L0_gnn_W1", "L0_gnn_b1", "L0_gnn_W2", "L0_gnn_b2",
        "L0_gnn_W3", "L0_gnn_b3", "L1_gnn_W1", "L1_gnn_b1", "L1_gnn_W2", "L1_gnn_b2", "L2_gnn_Wq_w", "L2_gnn_Wq_b",
        "L2_gnn_Wk_w", "L2_gnn_Wk_b", "L2_gnn_Wo_w", "L2_gnn_Wo_b", "L3_gnn_W1", "L3_gnn_b1", "L3_gnn_W2", "L3_gnn_b2",
        "L3_gnn_W_ih", "L3_gnn_b_ih", "L3_gnn_W_hh", "L3_gnn_b_hh"]


def kernel(**inputs):
    import numpy as np
    import concourse.bacc as bacc
    from concourse.bass_utils import run_bass_kernel_spmd

    nc = bacc.Bacc("TRN2", target_bir_lowering=False, num_devices=1)
    arrays, args = {}, {}
    for name in _INS:
        a = np.ascontiguousarray(inputs[name])
        arrays[f"in_{name}"] = a
        args[name] = nc.dram_tensor(f"in_{name}", a.shape, mybir.dt.from_np(a.dtype), kind="ExternalInput").ap()
    out = nc.dram_tensor("out_0", (N, P), F32, kind="ExternalOutput").ap()
    gnn_resnorm(nc, out, **args)
    r = run_bass_kernel_spmd(nc, [arrays], core_ids=[0])
    return r.results[0]["out_0"]
```

```python
import concourse.bass as bass
from concourse import mybir
from contextlib import ExitStack, contextmanager

F32 = mybir.dt.float32
BF16 = mybir.dt.bfloat16
I32 = mybir.dt.int32
I16 = mybir.dt.int16
ALU = mybir.AluOpType
ACT = mybir.ActivationFunctionType
AX = mybir.AxisListType

P = 128
N = 6250
E = 100000
EPS = 1e-5
WIN = (N + P - 1) // P
NP = WIN * P
AW = NP + P
GW = 7
G = WIN // GW
GC = GW * P
HC = GC // 2
FULL = E // P
REST = E - FULL * P
TILES = 784
CH = (TILES + P - 1) // P
U = 28
H = U // 2
SU = 16
SH = SU // 2
TABS = 8
HW = P + 4
TRASH = NP
HEADS = 2
ORDER = 4
MU = 56
MH = MU // 2
ROUNDS = WIN


def prev(step, per, k):
    return step * per + k


def now(step, per, k):
    return step * per + per + k


def gnn_resnorm(nc, out, x, src, dst, edge_attr_128, edge_weight,
                L0_gnn_W1, L0_gnn_b1, L0_gnn_W2, L0_gnn_b2, L0_gnn_W3, L0_gnn_b3,
                L1_gnn_W1, L1_gnn_b1, L1_gnn_W2, L1_gnn_b2,
                L2_gnn_Wq_w, L2_gnn_Wq_b, L2_gnn_Wk_w, L2_gnn_Wk_b, L2_gnn_Wo_w, L2_gnn_Wo_b,
                L3_gnn_W1, L3_gnn_b1, L3_gnn_W2, L3_gnn_b2,
                L3_gnn_W_ih, L3_gnn_b_ih, L3_gnn_W_hh, L3_gnn_b_hh, upto=99):
    ctx = ExitStack()
    with ctx:
        ctx.enter_context(nc.allow_non_contiguous_dma(reason="biases by feature and one number per tile: a few thousand elements"))

        def sb(name, shape, dt=F32):
            return ctx.enter_context(nc.sbuf_tensor(name, shape, dt))

        def dram(name, shape, dt=F32):
            return nc.dram_tensor(name, shape, dt, kind="Internal").ap()

        def loop(eng, count):
            return nc.Fori(0, count, engines=(eng.engine,), hint_back_edge=True)

        def peeled(eng, count, body):
            body(0)
            with nc.Fori(1, count, engines=(eng.engine,), hint_back_edge=True) as i:
                body(i)

        def wait_past(eng, sem, value):
            if not isinstance(value, int) or value > 0:
                eng.wait_ge(sem, value)

        def when_wide(eng, name):
            flag = eng.alloc_register(name)
            eng.load(flag, wide[0:1, 0:1])
            return eng.If_ne(flag, 0)

        def move_windows(dve, moved, begun, r):
            nc.vector.tensor_scalar(loc_col[:, :], loc_col[:, :], float(P), None, ALU.subtract).then_inc(moved, 1)
            nc.vector.tensor_scalar(base_f[:, :], base_f[:, :], float(P), None, ALU.add).then_inc(moved, 1)
            dve.wait_ge(moved, 3 * r + 2)
            nc.vector.tensor_scalar(base_row[:, :], base_f[:, :], float(NP), None, ALU.min).then_inc(moved, 1)
            dve.wait_ge(moved, 3 * r + 3)
            nc.vector.sem_inc(begun, 1)

        def windows_back(dve, moved):
            back = float(P * (ROUNDS - 1))
            nc.vector.tensor_scalar(loc_col[:, :], loc_col[:, :], back, None, ALU.add).then_inc(moved, 1)
            nc.vector.tensor_scalar(base_f[:, :], base_f[:, :], back, None, ALU.subtract).then_inc(moved, 1)
            dve.wait_ge(moved, 3 * (ROUNDS - 1) + 2)
            nc.vector.tensor_copy(base_row[:, :], base_f[:, :]).then_inc(moved, 1)
            dve.wait_ge(moved, 3 * (ROUNDS - 1) + 3)

        def rounds(eng, name, wide_path, steps, step):
            if not wide_path:
                with loop(eng, steps) as i:
                    step(i, i)
                return
            with when_wide(eng, name):
                with loop(eng, ROUNDS - 1) as r:
                    with loop(eng, steps) as i:
                        step(r * steps + i, i)

        @contextmanager
        def stage(*names):
            stage.n += 1
            sems = [nc.alloc_semaphore(f"{n}_{stage.n}") for n in names]
            with nc.Block() as block:
                yield (block, *sems)
            nc.clear_and_free_semaphores(sems)
            nc.all_engine_barrier()
        stage.n = 0

        def two(ap):
            return ap.rearrange("p (b n) -> p b n", b=2)

        def windows(table, g, width):
            return table[bass.ds(g * GC, GC), 0:width].rearrange("(k p) f -> p k f", p=P)

        ident = sb("ident", [P, P])
        ident_bf = sb("ident_bf", [P, P], BF16)
        mean_mat = sb("mean_mat", [P, P])
        ones_mat = sb("ones_mat", [P, P])
        iota16 = sb("iota16", [P, P], I16)
        tri = sb("tri", [P, P])
        trash = sb("trash", [P, 1])
        eps_col = sb("eps_col", [P, 1])
        src_idx = sb("src_idx", [P, TILES + H], I32)
        src_col = sb("src_col", [P, TILES])
        loc_col = sb("loc_col", [P, TILES])
        ew_col = sb("ew_col", [P, TILES])
        scat_idx = sb("scat_idx", [P, TILES], I32)
        base_row = sb("base_row", [1, TILES], I32)
        base_f = sb("base_f", [1, TILES])
        wide = sb("wide", [1, 2], I32)
        dinv = sb("dinv", [P, NP])
        kv = sb("kv", [P, HEADS, P])
        kv_sums = sb("kv_sums", [P, 2 * HEADS])
        key_sum = sb("key_sum", [P, HEADS, P])
        xT = sb("xT", [P, AW])
        acc = sb("acc", [P, HEADS, AW])
        wts = sb("wts", [P, 30, P])
        cols = sb("cols", [P, 24])
        bias_rows = sb("bias_rows", [P, 5, P])
        ps = ctx.enter_context(nc.psum_tensor("ps", [P, 8, 512], F32))
        flat = ps[:, :, :].rearrange("p b n -> p (b n)")

        xpad = dram("xpad", [NP, P])
        h_tab = dram("h_tab", [AW, HW])
        sums = [[dram(f"sums{m}_{k}", [AW, HW]) for k in range(TABS)] for m in range(2)]
        src_rows = dram("src_rows", [TILES, P])
        tile_info = dram("tile_info", [2, CH * P])
        x_tab = dram("x_tab", [NP, P])
        xh_tab = dram("xh_tab", [NP, HEADS * P])
        k_tab = dram("k_tab", [NP, HEADS * P])
        q_tab = dram("q_tab", [HEADS * P, NP])
        rden_tab = dram("rden_tab", [HEADS * P, NP])
        deg_tab = dram("deg_tab", [P, NP])
        p_tab = dram("p_tab", [NP, P])
        q3_tab = dram("q3_tab", [AW, P])

        W0 = [0, 1, 2]
        W1A, W1B = 3, 4
        WQ, WK = [5, 6], [7, 8]
        WO = [[9 + h * (ORDER + 1) + k for k in range(ORDER + 1)] for h in range(HEADS)]
        W3 = [19, 20, 21]
        W3O = 22
        WIH, WHH = [23, 24, 25], [26, 27, 28]
        B03, B11, B12, BQ, BO, B32, BIH, BHH = 0, 1, 2, [3, 4], 5, 6, [7, 8, 9], [10, 11, 12]
        BRZ, BOH, VS = [13, 14], 15, [16, 17]

        def wt(n):
            return wts[:, n, :]

        def col(n):
            return cols[:, n:n + 1]

        def two_matmuls(eng, bank, lhsT, rhs, start=True, stop=True):
            for b in range(2):
                last = nc.tensor.matmul(ps[:, bank + b, 0:HC], lhsT, rhs[:, b * HC:(b + 1) * HC],
                                        start=start, stop=stop)
            return last

        def load_weights():
            with ExitStack() as st:
                raw = st.enter_context(nc.sbuf_tensor("raw_w", [P, 13, P], F32))
                with stage("w_in", "filled", "made", "turned", "copied", "padded") as (
                        block, w_in, filled, made, turned, copied, padded):
                    natural = [L0_gnn_W1, L0_gnn_W2, L0_gnn_W3]
                    natural += [L3_gnn_W1[:, k * P:(k + 1) * P] for k in range(3)] + [L3_gnn_W2]
                    natural += [L3_gnn_W_ih[k * P:(k + 1) * P, :] for k in range(3)]
                    natural += [L3_gnn_W_hh[k * P:(k + 1) * P, :] for k in range(3)]
                    places = W0 + W3 + [W3O] + WIH + WHH
                    direct = [(W1A, L1_gnn_W1), (W1B, L1_gnn_W2)]
                    for h in range(HEADS):
                        direct += [(WQ[h], L2_gnn_Wq_w[:, h * P:(h + 1) * P]),
                                   (WK[h], L2_gnn_Wk_w[:, h * P:(h + 1) * P])]
                        direct += [(WO[h][k], L2_gnn_Wo_w[(h * (ORDER + 1) + k) * P:(h * (ORDER + 1) + k + 1) * P, :])
                                   for k in range(ORDER + 1)]
                    columns = [(B03, L0_gnn_b3), (B11, L1_gnn_b1), (B12, L1_gnn_b2), (BO, L2_gnn_Wo_b),
                               (B32, L3_gnn_b2)]
                    columns += [(BQ[h], L2_gnn_Wq_b[h * P:(h + 1) * P]) for h in range(HEADS)]
                    columns += [(BIH[k], L3_gnn_b_ih[k * P:(k + 1) * P]) for k in range(3)]
                    columns += [(BHH[k], L3_gnn_b_hh[k * P:(k + 1) * P]) for k in range(3)]
                    along = [L0_gnn_b1, L0_gnn_b2, L3_gnn_b1, L2_gnn_Wk_b[0:P], L2_gnn_Wk_b[P:2 * P]]
                    loads = 16 * (len(natural) + len(direct) + len(columns) + len(along))

                    @block.sync
                    def _(sp):
                        for n, w in enumerate(natural):
                            sp.dma_start(raw[:, n, :], w).then_inc(w_in, 16)
                        for n, w in direct:
                            sp.dma_start(wt(n), w).then_inc(w_in, 16)
                        for n, b in columns:
                            sp.dma_start(col(n), b.rearrange("(p a) -> p a", a=1)).then_inc(w_in, 16)
                        for n, b in enumerate(along):
                            sp.dma_start(bias_rows[:, n, :], b.partition_broadcast(P)).then_inc(w_in, 16)
                        sp.dma_start(xpad[0:N, :], x).then_inc(padded, 16)
                        sp.wait_ge(filled, 2)
                        sp.dma_start(xpad[N:NP, :], acc[0:NP - N, 0, 0:P]).then_inc(padded, 16)
                        sp.dma_start(h_tab[NP:AW, :], acc[:, 0, 0:HW]).then_inc(padded, 16)
                        sp.dma_start(q3_tab[NP:AW, :], acc[:, 0, 0:P]).then_inc(padded, 16)
                        for m in range(2):
                            for k in range(TABS):
                                sp.dma_start(sums[m][k][:, :].rearrange("(p r) f -> p (r f)", p=P),
                                             acc[:, :, :].rearrange("p h n -> p (h n)")[:, 0:AW // P * HW]
                                             ).then_inc(padded, 16)
                        sp.wait_ge(padded, 16 * (4 + 2 * TABS))

                    @block.gpsimd
                    def _(pool):
                        nc.gpsimd.memset(ident[:, :], 0.0).then_inc(made, 1)
                        nc.gpsimd.memset(ones_mat[:, :], 1.0).then_inc(made, 1)
                        nc.gpsimd.iota(iota16[:, :], pattern=[[1, P]], base=0, channel_multiplier=0).then_inc(made, 1)
                        nc.gpsimd.iota(trash[:, :], pattern=[[0, 1]], base=TRASH, channel_multiplier=1,
                                       allow_small_or_imprecise_dtypes=True).then_inc(made, 1)
                        pool.wait_ge(made, 4)
                        nc.gpsimd.affine_select(out=ident[:, :], in_=ident[:, :], compare_op=ALU.not_equal, fill=1.0,
                                                base=0, pattern=[[-1, P]], channel_multiplier=1).then_inc(made, 1)
                        nc.gpsimd.affine_select(out=tri[:, :], in_=ones_mat[:, :], compare_op=ALU.is_gt, fill=0.0,
                                                base=0, pattern=[[-1, P]], channel_multiplier=1).then_inc(made, 1)

                    @block.vector
                    def _(dve):
                        nc.vector.memset(acc[:, :, :], 0.0).then_inc(filled, 1)
                        nc.vector.memset(xT[:, NP:AW], 0.0).then_inc(filled, 1)
                        nc.vector.memset(mean_mat[:, :], 1.0 / P).then_inc(filled, 1)
                        nc.vector.memset(eps_col[:, :], EPS).then_inc(filled, 1)
                        dve.wait_ge(made, 6)
                        nc.vector.tensor_copy(ident_bf[:, :], ident[:, :]).then_inc(filled, 1)
                        dve.wait_ge(w_in, loads)
                        for k in range(2):
                            nc.vector.tensor_tensor(col(BRZ[k]), col(BIH[k]), col(BHH[k]), ALU.add).then_inc(filled, 1)
                        nc.vector.tensor_scalar(col(BOH), col(BO), 1.0 / HEADS, None, ALU.mult).then_inc(filled, 1)

                    @block.tensor
                    def _(pe):
                        pe.wait_ge(w_in, loads)
                        pe.wait_ge(made, 6)
                        for n in range(len(natural)):
                            last = nc.tensor.transpose(flat[:, n * P:(n + 1) * P], raw[:, n, :], ident[:, :])
                        last.then_inc(turned, 1)

                    @block.scalar
                    def _(act):
                        act.wait_ge(turned, 1)
                        for n, place in enumerate(places):
                            nc.scalar.copy(wt(place), flat[:, n * P:(n + 1) * P]).then_inc(copied, 1)

        def prepare_edges():
            with ExitStack() as st:
                def tmp(name, shape, dt=F32):
                    return st.enter_context(nc.sbuf_tensor(name, shape, dt))
                src_i, dst_i = tmp("src_i", [P, CH, P], I32), tmp("dst_i", [P, CH, P], I32)
                src_f, dst_f, ew_f = tmp("src_f", [P, CH, P]), tmp("dst_f", [P, CH, P]), tmp("ew_f", [P, CH, P])
                loc_f = tmp("loc_f", [P, CH, P])
                info = tmp("info", [P, 2, CH])
                with stage("cleared", "e_in", "dve_done", "turned", "copied", "info_out", "info_in", "based") as (
                        block, cleared, e_in, dve_done, turned, copied, info_out, info_in, based):
                    last = CH - 1
                    lead = last * P
                    tail = FULL - lead
                    fill = (P - REST) // REST

                    @block.sync
                    def _(sp):
                        sp.wait_ge(cleared, 3)
                        for a, v in ((src_i, src), (dst_i, dst), (ew_f, edge_weight)):
                            sp.dma_start(a[:, 0:last, :], v[0:lead * P].rearrange("(c t p) -> t c p", c=last, p=P)).then_inc(e_in, 16)
                            sp.dma_start(a[0:tail, last, :], v[lead * P:FULL * P].rearrange("(t p) -> t p", p=P)).then_inc(e_in, 16)
                            for k in range(fill + 1):
                                sp.dma_start(a[tail:tail + 1, last, k * REST:(k + 1) * REST],
                                             v[FULL * P:E].rearrange("(t p) -> t p", t=1)).then_inc(e_in, 16)
                        sp.wait_ge(dve_done, 2)
                        sp.dma_start(src_rows[0:lead, :].rearrange("(c t) p -> t c p", c=last), src_f[:, 0:last, :]).then_inc(info_out, 16)
                        sp.dma_start(src_rows[lead:TILES, :], src_f[0:TILES - lead, last, :]).then_inc(info_out, 16)
                        sp.wait_ge(dve_done, 6)
                        for k in range(2):
                            sp.dma_start(tile_info[k, :].rearrange("(c t) -> t c", c=CH), info[:, k, :]).then_inc(info_out, 16)
                        sp.wait_ge(info_out, 64)
                        sp.dma_start(acc[0:1, 0, 0:CH * P], tile_info[0:1, :]).then_inc(info_in, 16)
                        sp.dma_start(acc[0:1, 1, 0:CH * P], tile_info[1:2, :]).then_inc(info_in, 16)

                    @block.vector
                    def _(dve):
                        for a in (src_i, dst_i, ew_f):
                            nc.vector.memset(a[:, last, :], 0).then_inc(cleared, 1)
                        dve.wait_ge(e_in, 16 * 3 * (fill + 3))
                        nc.vector.tensor_copy(src_f[:, :, :], src_i[:, :, :]).then_inc(dve_done, 1)
                        nc.vector.tensor_copy(dst_f[:, :, :], dst_i[:, :, :]).then_inc(dve_done, 1)
                        dve.wait_ge(dve_done, 2)
                        nc.vector.tensor_reduce(info[:, 0, :], dst_f[:, :, :], AX.X, ALU.min).then_inc(dve_done, 1)
                        nc.vector.tensor_reduce(info[:, 1, :], dst_f[:, :, :], AX.X, ALU.max).then_inc(dve_done, 1)
                        dve.wait_ge(dve_done, 4)
                        nc.vector.tensor_tensor(info[:, 1, :], info[:, 1, :], info[:, 0, :], ALU.subtract).then_inc(dve_done, 1)
                        nc.vector.tensor_tensor(loc_f[:, :, :], dst_f[:, :, :],
                                                info[:, 0, :].unsqueeze(2).to_broadcast([P, CH, P]), ALU.subtract).then_inc(dve_done, 1)
                        dve.wait_ge(info_in, 32)
                        nc.vector.tensor_copy(base_row[0:1, :], acc[0:1, 0, 0:TILES]).then_inc(based, 1)
                        nc.vector.tensor_copy(base_f[0:1, :], acc[0:1, 0, 0:TILES]).then_inc(based, 1)
                        nc.vector.tensor_reduce(acc[0:1, 0, CH * P:CH * P + 1], acc[0:1, 1, 0:TILES], AX.X, ALU.max).then_inc(based, 1)
                        dve.wait_ge(based, 3)
                        nc.vector.tensor_scalar(wide[0:1, 0:1], acc[0:1, 0, CH * P:CH * P + 1], float(P), None, ALU.is_ge).then_inc(based, 1)
                        dve.wait_ge(copied, 4)
                        nc.vector.memset(loc_col[:, FULL + 1:TILES], -1.0).then_inc(based, 1)
                        nc.vector.tensor_copy(src_col[:, FULL + 1:TILES], trash[:, 0:1].to_broadcast([P, TILES - FULL - 1])).then_inc(based, 1)
                        for p0 in range(REST, P, 32):
                            nc.vector.memset(loc_col[p0:p0 + 32, FULL:FULL + 1], -1.0).then_inc(based, 1)
                            nc.vector.tensor_copy(src_col[p0:p0 + 32, FULL:FULL + 1], trash[p0:p0 + 32, :]).then_inc(based, 1)

                    @block.tensor
                    def _(pe):
                        pe.wait_ge(dve_done, 6)
                        for n, a in enumerate((src_f, loc_f, ew_f)):
                            for c in range(CH):
                                lastmm = nc.tensor.transpose(flat[:, n * 1024 + c * P:n * 1024 + (c + 1) * P], a[:, c, :], ident[:, :])
                            lastmm.then_inc(turned, 1)

                    @block.scalar
                    def _(act):
                        for n, to in ((0, src_col), (0, src_idx), (1, loc_col), (2, ew_col)):
                            act.wait_ge(turned, n + 1)
                            nc.scalar.copy(to[:, 0:TILES], flat[:, n * 1024:n * 1024 + TILES]).then_inc(copied, 1)
                        nc.scalar.copy(src_idx[:, TILES:TILES + H], flat[:, 0:H]).then_inc(copied, 1)

        def first_linear():
            with ExitStack() as st:
                rows = st.enter_context(nc.sbuf_tensor("x_rows", [P, GW, P], F32))
                zT = st.enter_context(nc.sbuf_tensor("zT0", [P, GC], F32))
                h_rows = st.enter_context(nc.sbuf_tensor("h_rows0", [P, GW, HW], F32))
                with stage("x_in", "pe_done", "act_done", "dve_done", "stored", "filled") as (
                        block, x_in, pe_done, act_done, dve_done, stored, filled):
                    @block.sync
                    def _(sp):
                        nc.sync.sem_inc(stored, 16)
                        sp.wait_ge(filled, 1)
                        with loop(sp, G) as g:
                            sp.wait_ge(pe_done, prev(g, 2, 1))
                            sp.dma_start(rows[:, :, :], windows(xpad, g, P)).then_inc(x_in, 16)
                            sp.wait_ge(dve_done, now(g, 1, 1))
                            sp.dma_start(windows(h_tab, g, HW), h_rows[:, :, :]).then_inc(stored, 16)
                        sp.wait_ge(stored, 16 * G + 16)

                    @block.tensor
                    def _(pe):
                        nc.tensor.sem_inc(pe_done, 2)
                        with loop(pe, G) as g:
                            pe.wait_ge(x_in, 16 * g + 16)
                            pe.wait_ge(act_done, prev(g, 2, 2))
                            for k in range(GW):
                                last = nc.tensor.transpose(flat[:, k * P:(k + 1) * P], rows[:, k, :], ident[:, :])
                            last.then_inc(pe_done, 1)
                            pe.wait_ge(act_done, now(g, 2, 1))
                            pe.wait_ge(dve_done, prev(g, 1, 1))
                            for k in range(GW):
                                last = nc.tensor.matmul(flat[:, 1024 + k * P:1024 + (k + 1) * P], zT[:, k * P:(k + 1) * P],
                                                        wt(W0[0]), start=True, stop=True)
                            last.then_inc(pe_done, 1)

                    @block.scalar
                    def _(act):
                        nc.scalar.sem_inc(act_done, 2)
                        with loop(act, G) as g:
                            act.wait_ge(pe_done, now(g, 2, 1))
                            nc.scalar.copy(zT[:, :], flat[:, 0:GC]).then_inc(act_done, 1)
                            nc.scalar.copy(xT[:, bass.ds(g * GC, GC)], flat[:, 0:GC]).then_inc(act_done, 1)

                    @block.vector
                    def _(dve):
                        nc.vector.memset(h_rows[:, :, P:HW], 1.0).then_inc(filled, 1)
                        nc.vector.sem_inc(dve_done, 1)
                        with loop(dve, G) as g:
                            dve.wait_ge(pe_done, now(g, 2, 2))
                            dve.wait_ge(stored, 16 * g + 16)
                            nc.vector.tensor_tensor(h_rows[:, :, 0:P], flat[:, 1024:1024 + GC].rearrange("p (k f) -> p k f", k=GW),
                                                    bias_rows[:, 0:1, :].to_broadcast([P, GW, P]), ALU.add).then_inc(dve_done, 1)

        def scatter_pass(m, wide_path):
            W = 8
            rank = m == 0 and not wide_path
            tag = f"{m}{'w' if wide_path else ''}"
            with ExitStack() as st:
                def tmp(name, shape, dt=F32):
                    return st.enter_context(nc.sbuf_tensor(f"{name}_sc{tag}", shape, dt))
                win = tmp("win", [P, W, HW])
                src_bc = tmp("src_bc", [P, 2, SH * P])
                onehot = tmp("onehot", [P, 2, P], BF16)
                same = tmp("same", [P, 2, P], BF16)
                hits = tmp("hits", [P, 2, P])
                earlier, to_row = tmp("earlier", [P, SH]), tmp("to_row", [P, SH])
                pick = tmp("pick", [P, 2, P])
                out_rows = tmp("out_rows", [P, SU, HW])
                idx = tmp("idx", [P, 2, SH], I32)
                names = [f"win_in{k}" for k in range(W)] + ["bc0", "bc1"] + [f"added{k}" for k in range(TABS)]
                names += ["matched", "ranked", "joined", "pick_copied", "summed", "sum_copied", "idx_copied", "begun", "moved"]
                with stage(*names) as (block, *s):
                    win_in, bc, added = s[0:W], s[W:W + 2], s[W + 2:W + 2 + TABS]
                    matched, ranked, joined, pick_copied, summed, sum_copied, idx_copied, begun, moved = s[W + 2 + TABS:]
                    steps = TILES // SU
                    per = SU // TABS

                    def scatter_rounds(eng, step):
                        if not wide_path:
                            step(0, 0)
                            with nc.Fori(1, steps, engines=(eng.engine,), hint_back_edge=True) as i:
                                step(i, i)
                            return
                        with when_wide(eng, f"wide_{tag}"):
                            step(0, 0)
                            with nc.Fori(1, steps, engines=(eng.engine,), hint_back_edge=True) as i:
                                step(i, i)
                            with nc.Fori(1, ROUNDS - 1, engines=(eng.engine,), hint_back_edge=True) as r:
                                with loop(eng, steps) as i:
                                    step(r * steps + i, i)

                    @block.sync
                    def _(sp):
                        regs = [nc.sync.alloc_register(f"win_base{tag}_{k}") for k in range(SH)]

                        def step(n, i, r=None):
                            for h in range(2):
                                nc.sync.load(regs, base_row[0:1, bass.ds(i * SU + h * SH, SH)])
                                base = [nc.sync.snap(x, min_val=0, max_val=NP) for x in regs]
                                sp.wait_ge(matched, prev(n, SU, (h + 1) * SH))
                                sp.dma_start(src_bc[:, h, :],
                                             src_rows[bass.ds(i * SU + h * SH, SH), :].rearrange("t p -> (t p)").partition_broadcast(P)
                                             ).then_inc(bc[h], 16)
                                for k in range(SH):
                                    j = h * SH + k
                                    sp.wait_ge(summed, n * SU + j + 1)
                                    sp.dma_start(win[:, j % W, :], h_tab[bass.ds(base[k], P), :]).then_inc(win_in[j % W], 16)

                        if not wide_path:
                            rounds(sp, "", False, steps, step)
                        else:
                            with when_wide(nc.sync, f"wide_sp_{tag}"):
                                with loop(sp, ROUNDS - 1) as r:
                                    sp.wait_ge(moved, 3 * r + 3)
                                    nc.sync.sem_inc(begun, 1)
                                    with loop(sp, steps) as i:
                                        step(r * steps + i, i)

                    @block.vector
                    def _(dve):
                        nc.vector.sem_inc(matched, SU)

                        def rank_half(n, h):
                            for k in range(SH):
                                if k >= 2:
                                    dve.wait_ge(ranked, (2 * n + h) * (SH + 5) + k - 1)
                                nc.vector.scalar_tensor_tensor(
                                    out=hits[:, k % 2, :], in0=src_bc[:, h, k * P:(k + 1) * P],
                                    scalar=src_col[:, bass.ds(n * SU + h * SH + k, 1)], in1=tri[:, :],
                                    op0=ALU.is_equal, op1=ALU.mult, accum_out=earlier[:, k:k + 1]).then_inc(ranked, 1)
                            at = (2 * n + h) * (SH + 5) + SH
                            c = bass.ds(n * SU + h * SH, SH)
                            dve.wait_ge(ranked, at)
                            nc.vector.tensor_scalar(earlier[:, :], earlier[:, :], 1.0, None, ALU.min).then_inc(ranked, 1)
                            nc.vector.tensor_scalar(to_row[:, :], src_col[:, c], trash[:, 0:1], -1.0,
                                                    ALU.subtract, ALU.mult).then_inc(ranked, 1)
                            dve.wait_ge(ranked, at + 2)
                            nc.vector.tensor_tensor(to_row[:, :], to_row[:, :], earlier[:, :], ALU.mult).then_inc(ranked, 1)
                            dve.wait_ge(ranked, at + 3)
                            nc.vector.tensor_tensor(to_row[:, :], to_row[:, :], src_col[:, c], ALU.add).then_inc(ranked, 1)
                            dve.wait_ge(ranked, at + 4)
                            nc.vector.tensor_copy(scat_idx[:, c], to_row[:, :]).then_inc(ranked, 1)
                            dve.wait_ge(ranked, at + 5)

                        def step(n, i):
                            for j in range(SU):
                                t = bass.ds(i * SU + j, 1)
                                if j % SH == 0:
                                    dve.wait_ge(bc[j // SH], 16 * n + 16)
                                    if rank:
                                        rank_half(n, j // SH)
                                dve.wait_ge(joined, n * SU + j + 1)
                                nc.vector.tensor_scalar(onehot[:, j % 2, :], iota16[:, :], loc_col[:, t], None, ALU.is_equal)
                                nc.vector.tensor_scalar(same[:, j % 2, :], src_bc[:, j // SH, (j % SH) * P:(j % SH + 1) * P],
                                                        src_col[:, t], None, ALU.is_equal).then_inc(matched, 1)

                        if not wide_path:
                            rounds(dve, "", False, steps, step)
                        else:
                            with when_wide(nc.vector, f"wide_{tag}_dve"):
                                with loop(dve, ROUNDS - 1) as r:
                                    dve.wait_ge(summed, r * TILES + W)
                                    dve.wait_ge(matched, r * TILES + SU)
                                    move_windows(dve, moved, begun, r)
                                    with loop(dve, steps) as i:
                                        step(r * steps + i, i)
                                dve.wait_ge(summed, (ROUNDS - 1) * TILES + W)
                                dve.wait_ge(matched, (ROUNDS - 1) * TILES + SU)
                                windows_back(dve, moved)

                    @block.tensor
                    def _(pe):
                        nc.tensor.sem_inc(joined, 2)
                        nc.tensor.sem_inc(summed, W)

                        def sum_rows(n, j):
                            pe.wait_ge(pick_copied, n * SU + j + 3)
                            pe.wait_ge(win_in[j % W], 16 * (n * (SU // W) + j // W + 1))
                            pe.wait_ge(sum_copied, n * SU + j + 1)
                            nc.tensor.matmul(ps[:, 2 + j % 2, 0:HW], pick[:, j % 2, :], win[:, j % W, :],
                                             start=True, stop=True).then_inc(summed, 1)

                        def step(n, i):
                            for j in range(SU):
                                pe.wait_ge(matched, now(n, SU, j + 1))
                                pe.wait_ge(pick_copied, n * SU + j + 1)
                                nc.tensor.matmul(ps[:, j % 2, 0:P], onehot[:, j % 2, :], same[:, j % 2, :],
                                                 start=True, stop=True).then_inc(joined, 1)
                                if j:
                                    sum_rows(n, j - 1)
                            sum_rows(n, SU - 1)

                        rounds(pe, f"wide_{tag}_pe", wide_path, steps, step)

                    @block.scalar
                    def _(act):
                        nc.scalar.sem_inc(pick_copied, 2)
                        nc.scalar.sem_inc(sum_copied, 2)

                        def copy_sum(n, j):
                            act.wait_ge(summed, n * SU + j + 1 + W)
                            wait_past(act, added[j % TABS], 16 * ((n - 1) * per + j // TABS + 1))
                            nc.scalar.copy(out_rows[:, j, :], ps[:, 2 + j % 2, 0:HW]).then_inc(sum_copied, 1)

                        def step(n, i):
                            for j in range(SU):
                                if j % SH == 0:
                                    for k in range(TABS):
                                        wait_past(act, added[k], 16 * ((n - 1) * per + (j // SH + 1) * (SH // TABS)))
                                    if rank:
                                        act.wait_ge(ranked, (2 * n + j // SH + 1) * (SH + 5))
                                    nc.scalar.copy(idx[:, j // SH, :], scat_idx[:, bass.ds(i * SU + j, SH)]).then_inc(idx_copied, 1)
                                act.wait_ge(joined, n * SU + j + 3)
                                act.wait_ge(summed, n * SU + j - 1 + W)
                                nc.scalar.copy(pick[:, j % 2, :], ps[:, j % 2, 0:P]).then_inc(pick_copied, 1)
                                if j:
                                    copy_sum(n, j - 1)
                            copy_sum(n, SU - 1)

                        scatter_rounds(nc.scalar, step)

                    @block.gpsimd
                    def _(pool):
                        def step(n, i):
                            for j in range(SU):
                                if j % SH == 0:
                                    pool.wait_ge(idx_copied, n * 2 + j // SH + 1)
                                pool.wait_ge(sum_copied, n * SU + j + 3)
                                wait_past(pool, added[j % TABS], 16 * (n * per + j // TABS))
                                nc.gpsimd.sem_inc(begun, 1)
                                nc.gpsimd.indirect_dma_start(
                                    sums[m][j % TABS],
                                    bass.IndirectOffsetOnAxis(ap=idx[:, j // SH, j % SH:j % SH + 1], axis=0),
                                    out_rows[:, j, :], None, compute_op=ALU.add).then_inc(added[j % TABS], 16)

                        scatter_rounds(nc.gpsimd, step)
                        if not wide_path:
                            for k in range(TABS):
                                pool.wait_ge(added[k], 16 * (TILES // TABS))
                        else:
                            with when_wide(nc.gpsimd, f"wide_{tag}_end"):
                                for k in range(TABS):
                                    pool.wait_ge(added[k], 16 * (ROUNDS - 1) * (TILES // TABS))

        def degree_rows(g, dve, half_in, dve_done, tabs, h_rows, per):
            half = TABS // 2
            at = 0
            for b in range(2):
                dve.wait_ge(half_in[b], 16 * half * (g + 1))
                t = [tabs[:, b * half + k] for k in range(half)]
                nc.vector.tensor_tensor(t[0], t[0], t[1], ALU.add).then_inc(dve_done, 1)
                nc.vector.tensor_tensor(t[2], t[2], t[3], ALU.add).then_inc(dve_done, 1)
                dve.wait_ge(dve_done, now(g, per, at + 2))
                if b == 0:
                    dve.wait_ge(dve_done, now(g, per, 2))
                    nc.vector.tensor_tensor(tabs[:, TABS], t[0], t[2], ALU.add).then_inc(dve_done, 1)
                else:
                    nc.vector.tensor_tensor(t[0], t[0], t[2], ALU.add).then_inc(dve_done, 1)
                at += 3
            total, deg = tabs[:, TABS], tabs[:, TABS + 1]
            dve.wait_ge(dve_done, now(g, per, 6))
            nc.vector.tensor_tensor(total, total, tabs[:, half], ALU.add).then_inc(dve_done, 1)
            dve.wait_ge(dve_done, now(g, per, 7))
            nc.vector.tensor_scalar(deg[:, :, 0:1], total[:, :, P:P + 1], 1.0, None, ALU.max).then_inc(dve_done, 1)
            dve.wait_ge(dve_done, now(g, per, 8))
            nc.vector.reciprocal(deg[:, :, 1:2], deg[:, :, 0:1]).then_inc(dve_done, 1)
            dve.wait_ge(dve_done, now(g, per, 9))
            nc.vector.tensor_tensor(h_rows[:, :, :], total[:, :, 0:P], deg[:, :, 1:2].to_broadcast([P, GW, P]), ALU.mult).then_inc(dve_done, 1)

        def layer0_nodes(m):
            with ExitStack() as st:
                def tmp(name, shape, dt=F32):
                    return st.enter_context(nc.sbuf_tensor(f"{name}_n{m}", shape, dt))
                tabs = tmp("tabs", [P, TABS + 2, GW, HW])
                h_rows = tmp("h_rows", [P, GW, P])
                r_rows = tmp("r_rows", [P, GW, P])
                zT = tmp("zT", [P, GC])
                o_rows = tmp("o_rows", [P, GW, HW])
                DN = 11
                with stage("half0_in", "half1_in", "pe_done", "act_done", "dve_done", "stored", "filled") as (
                        block, half0_in, half1_in, pe_done, act_done, dve_done, stored, filled):
                    half_in = (half0_in, half1_in)

                    @block.sync
                    def _(sp):
                        with loop(sp, G) as g:
                            for b, used in enumerate((3, 7)):
                                sp.wait_ge(dve_done, prev(g, DN, used))
                                for k in range(b * TABS // 2, (b + 1) * TABS // 2):
                                    sp.dma_start(tabs[:, k], windows(sums[m][k], g, HW)).then_inc(half_in[b], 16)

                    @block.vector
                    def _(dve):
                        nc.vector.memset(o_rows[:, :, P:HW], 1.0).then_inc(filled, 1)
                        nc.vector.sem_inc(dve_done, DN)
                        with loop(dve, G) as g:
                            dve.wait_ge(act_done, prev(g, 2, 1))
                            degree_rows(g, dve, half_in, dve_done, tabs, h_rows, DN)
                            dve.wait_ge(pe_done, now(g, 2, 2))
                            if m == 0:
                                dve.wait_ge(stored, 16 * g + 16)
                                nc.vector.tensor_tensor(o_rows[:, :, 0:P], flat[:, 1024:1024 + GC].rearrange("p (k f) -> p k f", k=GW),
                                                        bias_rows[:, 1:2, :].to_broadcast([P, GW, P]), ALU.add).then_inc(dve_done, 1)
                            else:
                                xg = two(xT[:, bass.ds(g * GC, GC)])
                                nc.vector.scalar_tensor_tensor(out=xg, in0=ps[:, 2:4, 0:HC], scalar=col(B03), in1=xg,
                                                               op0=ALU.add, op1=ALU.add).then_inc(dve_done, 1)

                    @block.scalar
                    def _(act):
                        nc.scalar.sem_inc(act_done, 2)
                        nc.scalar.sem_inc(stored, 16)
                        act.wait_ge(filled, 1)
                        with loop(act, G) as g:
                            act.wait_ge(dve_done, now(g, DN, 10))
                            act.wait_ge(pe_done, prev(g, 2, 1))
                            nc.scalar.activation(r_rows[:, :, :], h_rows[:, :, :], ACT.Relu).then_inc(act_done, 1)
                            act.wait_ge(pe_done, now(g, 2, 1))
                            nc.scalar.copy(zT[:, :], flat[:, 0:GC]).then_inc(act_done, 1)
                            if m == 0:
                                act.wait_ge(dve_done, now(g, DN, 11))
                                act.dma_start(windows(h_tab, g, HW), o_rows[:, :, :]).then_inc(stored, 16)
                        if m == 0:
                            act.wait_ge(stored, 16 * G + 16)

                    @block.tensor
                    def _(pe):
                        nc.tensor.sem_inc(pe_done, 2)
                        with loop(pe, G) as g:
                            pe.wait_ge(act_done, now(g, 2, 1))
                            for k in range(GW):
                                last = nc.tensor.transpose(flat[:, k * P:(k + 1) * P], r_rows[:, k, :], ident[:, :])
                            last.then_inc(pe_done, 1)
                            pe.wait_ge(act_done, now(g, 2, 2))
                            pe.wait_ge(dve_done, prev(g, DN, 11))
                            if m == 0:
                                for k in range(GW):
                                    last = nc.tensor.matmul(flat[:, 1024 + k * P:1024 + (k + 1) * P], zT[:, k * P:(k + 1) * P],
                                                            wt(W0[1]), start=True, stop=True)
                            else:
                                last = two_matmuls(pe, 2, wt(W0[2]), zT)
                            last.then_inc(pe_done, 1)

        def normalize(n, table):
            with ExitStack() as st:
                def tmp(name, shape, dt=F32):
                    return st.enter_context(nc.sbuf_tensor(f"{name}_ln{n}", shape, dt))
                cen, sq, sd, rstd, y = [tmp(k, [P, GC]) for k in ("cen", "sq", "sd", "rstd", "y")]
                rows = tmp("rows", [P, GW, P])
                with stage("zeroed", "pe_done", "act_done", "dve_done", "stored") as (
                        block, zeroed, pe_done, act_done, dve_done, stored):
                    @block.sync
                    def _(sp):
                        nc.sync.sem_inc(stored, 16)
                        with loop(sp, G) as g:
                            sp.wait_ge(act_done, now(g, 4, 4))
                            sp.dma_start(windows(table, g, P), rows[:, :, :]).then_inc(stored, 16)
                        sp.wait_ge(stored, 16 * G + 16)

                    @block.vector
                    def _(dve):
                        nc.vector.memset(xT[:, N:AW], 0.0).then_inc(zeroed, 1)
                        nc.vector.sem_inc(dve_done, 3)
                        dve.wait_ge(zeroed, 1)
                        with loop(dve, G) as g:
                            xg = two(xT[:, bass.ds(g * GC, GC)])
                            dve.wait_ge(pe_done, now(g, 3, 1))
                            nc.vector.tensor_tensor(two(cen[:, :]), xg, ps[:, 0:2, 0:HC], ALU.subtract).then_inc(dve_done, 1)
                            dve.wait_ge(act_done, now(g, 4, 2))
                            nc.vector.reciprocal(rstd[:, :], sd[:, :]).then_inc(dve_done, 1)
                            dve.wait_ge(dve_done, now(g, 3, 2))
                            dve.wait_ge(act_done, prev(g, 4, 3))
                            dve.wait_ge(pe_done, prev(g, 3, 3))
                            nc.vector.tensor_tensor(y[:, :], cen[:, :], rstd[:, :], ALU.mult).then_inc(dve_done, 1)

                    @block.tensor
                    def _(pe):
                        nc.tensor.sem_inc(pe_done, 3)
                        pe.wait_ge(zeroed, 1)
                        with loop(pe, G) as g:
                            xg = xT[:, bass.ds(g * GC, GC)]
                            pe.wait_ge(dve_done, prev(g, 3, 1))
                            two_matmuls(pe, 0, mean_mat[:, :], xg).then_inc(pe_done, 1)
                            pe.wait_ge(act_done, now(g, 4, 1))
                            two_matmuls(pe, 2, mean_mat[:, :], sq).then_inc(pe_done, 1)
                            pe.wait_ge(dve_done, now(g, 3, 3))
                            pe.wait_ge(act_done, prev(g, 4, 4))
                            for k in range(GW):
                                last = nc.tensor.transpose(flat[:, 2048 + k * P:2048 + (k + 1) * P], y[:, k * P:(k + 1) * P], ident[:, :])
                            last.then_inc(pe_done, 1)

                    @block.scalar
                    def _(act):
                        nc.scalar.sem_inc(act_done, 4)
                        with loop(act, G) as g:
                            act.wait_ge(dve_done, now(g, 3, 1))
                            nc.scalar.activation(sq[:, :], cen[:, :], ACT.Square).then_inc(act_done, 1)
                            act.wait_ge(pe_done, now(g, 3, 2))
                            nc.scalar.activation(two(sd[:, :]), ps[:, 2:4, 0:HC], ACT.Sqrt, bias=eps_col[:, 0:1]).then_inc(act_done, 1)
                            act.wait_ge(dve_done, now(g, 3, 3))
                            nc.scalar.copy(xT[:, bass.ds(g * GC, GC)], y[:, :]).then_inc(act_done, 1)
                            act.wait_ge(pe_done, now(g, 3, 3))
                            act.wait_ge(stored, 16 * g + 16)
                            nc.scalar.copy(rows[:, :, :], flat[:, 2048:2048 + GC].rearrange("p (k f) -> p k f", k=GW)).then_inc(act_done, 1)

        def gather_pass(n, table, heads, wide_path, weighted=False, degree=False):
            width = heads * P
            parts = 2 if degree else heads
            tag = f"{n}{'w' if wide_path else ''}"
            with ExitStack() as st:
                def tmp(name, shape, dt=F32):
                    return st.enter_context(nc.sbuf_tensor(f"{name}_g{tag}", shape, dt))
                rows = tmp("rows", [P, U, width])
                onehot = tmp("onehot", [P, 2, P])
                idx = tmp("idx", [P, 2, H], I32)
                names = [f"rows_in{j}" for j in range(U)] + ["cleared", "idx_copied", "begun", "matched", "tile_done", "added", "moved"]
                with stage(*names) as (block, *s):
                    rows_in = s[0:U]
                    cleared, idx_copied, begun, matched, tile_done, added, moved = s[U:]
                    steps = TILES // U

                    @block.gpsimd
                    def _(pool):
                        def step(n, i):
                            for j in range(U):
                                if j % H == 0:
                                    pool.wait_ge(idx_copied, 2 * n + j // H + 1)
                                    nc.gpsimd.sem_inc(begun, 1)
                                nc.gpsimd.indirect_dma_start(
                                    rows[:, j, :], None, table,
                                    bass.IndirectOffsetOnAxis(ap=idx[:, j // H, j % H:j % H + 1], axis=0)).then_inc(rows_in[j], 16)

                        rounds(nc.gpsimd, f"wide_g{tag}_pool", wide_path, steps, step)

                    @block.scalar
                    def _(act):
                        def step(n, i):
                            for h in range(2):
                                act.wait_ge(tile_done, prev(n, U, H * (h + 1)))
                                nc.scalar.copy(idx[:, h, :], src_idx[:, bass.ds(i * U + h * H, H)]).then_inc(idx_copied, 1)

                        rounds(nc.scalar, f"wide_g{tag}_act", wide_path, steps, step)

                    @block.vector
                    def _(dve):
                        regs = [nc.vector.alloc_register(f"base{tag}_{k}") for k in range(H)]
                        nc.vector.sem_inc(added, 2)
                        if not wide_path:
                            nc.vector.memset(acc[:, 0:parts, :], 0.0).then_inc(cleared, 1)
                            dve.wait_ge(cleared, 1)

                        def add(n, j, base):
                            dve.wait_ge(tile_done, now(n, U, j + 1))
                            dve.wait_ge(added, n * U + j + 2)
                            a = acc[:, 0:parts, bass.ds(base, P)]
                            nc.vector.tensor_tensor(a, a, ps[:, j % 2, 0:parts * P].rearrange("p (h n) -> p h n", h=parts),
                                                    ALU.add).then_inc(added, 1)

                        def step(n, i):
                            bases = []
                            for j in range(U):
                                if j % H == 0:
                                    nc.vector.load(regs, base_row[0:1, bass.ds(i * U + j, H)])
                                    bases += [nc.vector.snap(r, min_val=0, max_val=NP) for r in regs]
                                dve.wait_ge(tile_done, now(n, U, j - 1))
                                t = bass.ds(i * U + j, 1)
                                if weighted:
                                    nc.vector.tensor_scalar(onehot[:, j % 2, :], iota16[:, :], loc_col[:, t], ew_col[:, t],
                                                            ALU.is_equal, ALU.mult).then_inc(matched, 1)
                                else:
                                    nc.vector.tensor_scalar(onehot[:, j % 2, :], iota16[:, :], loc_col[:, t], None,
                                                            ALU.is_equal).then_inc(matched, 1)
                                if j:
                                    add(n, j - 1, bases[j - 1])
                            add(n, U - 1, bases[U - 1])

                        if not wide_path:
                            rounds(dve, "", False, steps, step)
                        else:
                            with when_wide(nc.vector, f"wide_g{tag}_dve"):
                                with loop(dve, ROUNDS - 1) as r:
                                    move_windows(dve, moved, begun, r)
                                    with loop(dve, steps) as i:
                                        step(r * steps + i, i)
                                windows_back(dve, moved)

                    @block.tensor
                    def _(pe):
                        nc.tensor.sem_inc(tile_done, U)
                        def step(n, i):
                            for j in range(U):
                                pe.wait_ge(rows_in[j], 16 * n + 16)
                                pe.wait_ge(matched, n * U + j + 1)
                                pe.wait_ge(added, n * U + j + 1)
                                for h in range(heads):
                                    last = nc.tensor.matmul(ps[:, j % 2, h * P:(h + 1) * P], rows[:, j, h * P:(h + 1) * P],
                                                            onehot[:, j % 2, :], start=True, stop=True)
                                if degree:
                                    last = nc.tensor.matmul(ps[:, j % 2, P:2 * P], ones_mat[:, :], onehot[:, j % 2, :],
                                                            start=True, stop=True)
                                last.then_inc(tile_done, 1)

                        rounds(nc.tensor, f"wide_g{tag}_pe", wide_path, steps, step)

        def layer1_nodes():
            with ExitStack() as st:
                mix = st.enter_context(nc.sbuf_tensor("mix1", [P, GC], F32))
                hid = st.enter_context(nc.sbuf_tensor("hid1", [P, GC], F32))
                with stage("pe_done", "act_done", "dve_done") as (block, pe_done, act_done, dve_done):
                    @block.vector
                    def _(dve):
                        nc.vector.sem_inc(dve_done, 2)
                        with loop(dve, G) as g:
                            xg = xT[:, bass.ds(g * GC, GC)]
                            dve.wait_ge(pe_done, prev(g, 2, 1))
                            nc.vector.tensor_tensor(mix[:, :], xg, acc[:, 0, bass.ds(g * GC, GC)], ALU.add).then_inc(dve_done, 1)
                            dve.wait_ge(pe_done, now(g, 2, 2))
                            dve.wait_ge(dve_done, now(g, 2, 1))
                            nc.vector.scalar_tensor_tensor(out=two(xg), in0=ps[:, 2:4, 0:HC], scalar=col(B12), in1=two(xg),
                                                           op0=ALU.add, op1=ALU.add).then_inc(dve_done, 1)

                    @block.tensor
                    def _(pe):
                        nc.tensor.sem_inc(pe_done, 2)
                        with loop(pe, G) as g:
                            pe.wait_ge(dve_done, now(g, 2, 1))
                            pe.wait_ge(act_done, prev(g, 1, 1))
                            two_matmuls(pe, 0, wt(W1A), mix).then_inc(pe_done, 1)
                            pe.wait_ge(act_done, now(g, 1, 1))
                            pe.wait_ge(dve_done, prev(g, 2, 2))
                            two_matmuls(pe, 2, wt(W1B), hid).then_inc(pe_done, 1)

                    @block.scalar
                    def _(act):
                        nc.scalar.sem_inc(act_done, 1)
                        with loop(act, G) as g:
                            act.wait_ge(pe_done, now(g, 2, 1))
                            act.wait_ge(pe_done, prev(g, 2, 2))
                            nc.scalar.activation(two(hid[:, :]), ps[:, 0:2, 0:HC], ACT.Relu, bias=col(B11)).then_inc(act_done, 1)

        def layer2_keys():
            KW = HEADS * P
            with ExitStack() as st:
                def tmp(name, shape, dt=F32):
                    return st.enter_context(nc.sbuf_tensor(f"{name}_k", shape, dt))
                xg = tmp("xg", [P, GC])
                q, qq, qn = [tmp(k, [P, HEADS, GC]) for k in ("q", "qq", "qn")]
                k_rows, kk = [tmp(k, [P, GW, KW]) for k in ("k_rows", "kk")]
                knorm = tmp("knorm", [P, 3, GW * HEADS])
                zero = tmp("zero", [NP - N, KW])
                with stage("pe_done", "act_done", "dve_done", "q_out", "k_out", "zeroed", "pad_out") as (
                        block, pe_done, act_done, dve_done, q_out, k_out, zeroed, pad_out):
                    PN, AN, DN = 3, 5, 8

                    def q_banks(h):
                        return ps[:, 2 * h:2 * h + 2, 0:HC]

                    @block.tensor
                    def _(pe):
                        nc.tensor.sem_inc(pe_done, PN)
                        with loop(pe, G) as g:
                            pe.wait_ge(act_done, now(g, AN, 1))
                            for h in range(HEADS):
                                last = two_matmuls(pe, 2 * h, wt(WQ[h]), xg)
                            last.then_inc(pe_done, 1)
                            pe.wait_ge(dve_done, prev(g, DN, 2))
                            for k in range(GW):
                                last = nc.tensor.matmul(flat[:, 2048 + k * KW:2048 + (k + 1) * KW], xg[:, k * P:(k + 1) * P],
                                                        wts[:, WK[0]:WK[1] + 1, :].rearrange("p a n -> p (a n)"), start=True, stop=True)
                            last.then_inc(pe_done, 1)
                            pe.wait_ge(dve_done, now(g, DN, 1))
                            for h in range(HEADS):
                                last = two_matmuls(pe, 2 * h, ones_mat[:, :], qq[:, h, :])
                            last.then_inc(pe_done, 1)

                    @block.scalar
                    def _(act):
                        nc.scalar.sem_inc(act_done, AN)
                        with loop(act, G) as g:
                            act.wait_ge(pe_done, prev(g, PN, 2))
                            nc.scalar.copy(xg[:, :], xT[:, bass.ds(g * GC, GC)]).then_inc(act_done, 1)
                            act.wait_ge(pe_done, now(g, PN, 1))
                            act.wait_ge(dve_done, prev(g, DN, 7))
                            for h in range(HEADS):
                                nc.scalar.activation(two(q[:, h, :]), q_banks(h), ACT.Identity, bias=col(BQ[h])).then_inc(act_done, 1)
                            act.wait_ge(pe_done, now(g, PN, 3))
                            nc.scalar.activation(qq[:, :, :].rearrange("p h (b n) -> p (h b) n", b=2), ps[:, 0:4, 0:HC], ACT.Sqrt).then_inc(act_done, 1)
                            act.wait_ge(dve_done, now(g, DN, 4))
                            nc.scalar.activation(knorm[:, 1, :], knorm[:, 0, :], ACT.Sqrt).then_inc(act_done, 1)

                    @block.vector
                    def _(dve):
                        nc.vector.memset(zero[:, :], 0.0).then_inc(zeroed, 1)
                        nc.vector.sem_inc(dve_done, DN)
                        with loop(dve, G) as g:
                            dve.wait_ge(act_done, now(g, AN, 3))
                            nc.vector.tensor_tensor(qq[:, :, :], q[:, :, :], q[:, :, :], ALU.mult).then_inc(dve_done, 1)
                            dve.wait_ge(pe_done, now(g, PN, 2))
                            dve.wait_ge(k_out, 16 * g + 16)
                            nc.vector.tensor_tensor(k_rows[:, :, :], flat[:, 2048:2048 + GW * KW].rearrange("p (k f) -> p k f", k=GW),
                                                    bias_rows[:, 3:5, :].rearrange("p (o a) n -> p o (a n)", o=1).to_broadcast([P, GW, KW]),
                                                    ALU.add).then_inc(dve_done, 1)
                            dve.wait_ge(dve_done, now(g, DN, 2))
                            nc.vector.tensor_tensor(kk[:, :, :], k_rows[:, :, :], k_rows[:, :, :], ALU.mult).then_inc(dve_done, 1)
                            dve.wait_ge(dve_done, now(g, DN, 3))
                            nc.vector.tensor_reduce(knorm[:, 0, :], kk[:, :, :].rearrange("p k (h f) -> p (k h) f", h=HEADS),
                                                    AX.X, ALU.add).then_inc(dve_done, 1)
                            dve.wait_ge(act_done, now(g, AN, 4))
                            dve.wait_ge(q_out, 32 * g + 32)
                            nc.vector.reciprocal(qn[:, :, :], qq[:, :, :]).then_inc(dve_done, 1)
                            dve.wait_ge(act_done, now(g, AN, 5))
                            nc.vector.reciprocal(knorm[:, 2, :], knorm[:, 1, :]).then_inc(dve_done, 1)
                            dve.wait_ge(dve_done, now(g, DN, 5))
                            nc.vector.tensor_tensor(qn[:, :, :], qn[:, :, :], q[:, :, :], ALU.mult).then_inc(dve_done, 1)
                            dve.wait_ge(dve_done, now(g, DN, 6))
                            kh = k_rows[:, :, :].rearrange("p k (h f) -> p (k h) f", h=HEADS)
                            nc.vector.tensor_tensor(kh, kh, knorm[:, 2, :].unsqueeze(2).to_broadcast([P, GW * HEADS, P]),
                                                    ALU.mult).then_inc(dve_done, 1)

                    @block.sync
                    def _(sp):
                        nc.sync.sem_inc(q_out, 32)
                        nc.sync.sem_inc(k_out, 16)
                        with loop(sp, G) as g:
                            sp.wait_ge(dve_done, now(g, DN, 7))
                            for h in range(HEADS):
                                sp.dma_start(q_tab[h * P:(h + 1) * P, bass.ds(g * GC, GC)], qn[:, h, :]).then_inc(q_out, 16)
                            sp.wait_ge(dve_done, now(g, DN, 8))
                            sp.dma_start(windows(k_tab, g, KW), k_rows[:, :, :]).then_inc(k_out, 16)
                        sp.wait_ge(q_out, 32 * G + 32)
                        sp.wait_ge(k_out, 16 * G + 16)
                        sp.wait_ge(zeroed, 1)
                        sp.dma_start(k_tab[N:NP, :], zero[:, :]).then_inc(pad_out, 16)
                        sp.wait_ge(pad_out, 16)

        def layer2_keys_values(n, table, heads):
            KW = HEADS * P
            with ExitStack() as st:
                def tmp(name, shape, dt=F32):
                    return st.enter_context(nc.sbuf_tensor(f"{name}_kv{n}", shape, dt))
                k_rows = tmp("k_rows", [P, 2, GW, KW])
                x_rows = tmp("x_rows", [P, 2, GW, heads * P])
                with stage("rows_in", "rows_in_last", "pe_done", "dve_done", "cleared") as (
                        block, rows_in, rows_in_last, pe_done, dve_done, cleared):
                    @block.sync
                    def _(sp):
                        with loop(sp, G) as g:
                            sp.wait_ge(pe_done, g + 1)
                            sp.dma_start(k_rows[:, 0], windows(k_tab, g, KW)).then_inc(rows_in, 16)
                            sp.dma_start(x_rows[:, 0], windows(table, g, heads * P)).then_inc(rows_in, 16)

                    @block.tensor
                    def _(pe):
                        nc.tensor.sem_inc(pe_done, 1)
                        with loop(pe, G) as g:
                            pe.wait_ge(rows_in, 32 * g + 32)
                            pe.wait_ge(dve_done, prev(g, 2, 2))
                            for h in range(HEADS):
                                at = (h % heads) * P
                                for k in range(GW):
                                    nc.tensor.matmul(ps[:, h, 0:P], k_rows[:, 0, k, h * P:(h + 1) * P], x_rows[:, 0, k, at:at + P],
                                                     start=(k == 0), stop=(k == GW - 1))
                                for k in range(GW):
                                    nc.tensor.matmul(ps[:, 2 + h, 0:1], x_rows[:, 0, k, at:at + P], ones_mat[:, 0:1],
                                                     start=(k == 0), stop=(k == GW - 1))
                                for k in range(GW):
                                    last = nc.tensor.matmul(ps[:, 4 + h, 0:1], k_rows[:, 0, k, h * P:(h + 1) * P], ones_mat[:, 0:1],
                                                            start=(k == 0), stop=(k == GW - 1))
                            last.then_inc(pe_done, 1)

                    @block.vector
                    def _(dve):
                        nc.vector.memset(kv[:, :, :], 0.0).then_inc(cleared, 1)
                        nc.vector.memset(kv_sums[:, :], 0.0).then_inc(cleared, 1)
                        nc.vector.sem_inc(dve_done, 2)
                        dve.wait_ge(cleared, 2)
                        with loop(dve, G) as g:
                            dve.wait_ge(pe_done, g + 2)
                            dve.wait_ge(dve_done, prev(g, 2, 2))
                            nc.vector.tensor_tensor(kv[:, :, :], kv[:, :, :], ps[:, 0:2, 0:P], ALU.add).then_inc(dve_done, 1)
                            nc.vector.tensor_tensor(kv_sums[:, :], kv_sums[:, :], ps[:, 2:6, 0:1].rearrange("p b n -> p (b n)"), ALU.add).then_inc(dve_done, 1)
                        dve.wait_ge(dve_done, 2 * G + 2)
                        for h in range(HEADS):
                            nc.vector.tensor_copy(key_sum[:, h, :], kv_sums[:, HEADS + h:HEADS + h + 1].to_broadcast([P, P])).then_inc(cleared, 1)

        def layer2_denominators():
            with ExitStack() as st:
                def tmp(name, shape, dt=F32):
                    return st.enter_context(nc.sbuf_tensor(f"{name}_d", shape, dt))
                q, rden, den = [tmp(k, [P, HEADS, GC]) for k in ("q", "rden", "den")]
                part = tmp("part", [P, GC])
                zero = tmp("zero", [P, 2 * (NP - N)])
                with stage("q_in", "pe_done", "dve_done", "stored", "zeroed", "pad_out") as (
                        block, q_in, pe_done, dve_done, stored, zeroed, pad_out):
                    DN = 5

                    @block.sync
                    def _(sp):
                        nc.sync.sem_inc(stored, 64)
                        with loop(sp, G) as g:
                            c = bass.ds(g * GC, GC)
                            sp.wait_ge(stored, 64 * g + 64)
                            for h in range(HEADS):
                                sp.dma_start(q[:, h, :], q_tab[h * P:(h + 1) * P, c]).then_inc(q_in, 16)
                            sp.wait_ge(dve_done, now(g, DN, 3))
                            for h in range(HEADS):
                                sp.dma_start(q_tab[h * P:(h + 1) * P, c], q[:, h, :]).then_inc(stored, 16)
                                sp.dma_start(rden_tab[h * P:(h + 1) * P, c], rden[:, h, :]).then_inc(stored, 16)
                        sp.wait_ge(stored, 64 * G + 64)
                        sp.wait_ge(zeroed, 1)
                        for h in range(HEADS):
                            for t in (q_tab, rden_tab):
                                sp.dma_start(t[h * P:(h + 1) * P, N:NP], zero[:, 0:NP - N]).then_inc(pad_out, 16)
                        sp.wait_ge(pad_out, 16 * 2 * HEADS)

                    @block.tensor
                    def _(pe):
                        nc.tensor.sem_inc(pe_done, 2)
                        with loop(pe, G) as g:
                            pe.wait_ge(q_in, 32 * g + 32)
                            pe.wait_ge(dve_done, prev(g, DN, 1))
                            for h in range(HEADS):
                                last = two_matmuls(pe, 2 * h, key_sum[:, h, :], q[:, h, :])
                            last.then_inc(pe_done, 1)
                            pe.wait_ge(dve_done, prev(g, DN, 4))
                            for h in range(HEADS):
                                for b in range(2):
                                    last = nc.tensor.matmul(ps[:, 4 + b, 0:HC], wt(WO[h][0]), xT[:, bass.ds(g * GC + b * HC, HC)],
                                                            start=(h == 0), stop=(h == HEADS - 1))
                            last.then_inc(pe_done, 1)

                    @block.vector
                    def _(dve):
                        nc.vector.memset(zero[:, :], 0.0).then_inc(zeroed, 1)
                        nc.vector.sem_inc(dve_done, DN)
                        with loop(dve, G) as g:
                            xg = xT[:, bass.ds(g * GC, GC)]
                            dve.wait_ge(pe_done, now(g, 2, 1))
                            nc.vector.tensor_scalar(den[:, :, :].rearrange("p h (b n) -> p (h b) n", b=2), ps[:, 0:4, 0:HC],
                                                    float(N), None, ALU.add).then_inc(dve_done, 1)
                            dve.wait_ge(dve_done, now(g, DN, 1))
                            dve.wait_ge(stored, 64 * g + 64)
                            nc.vector.reciprocal(rden[:, :, :], den[:, :, :]).then_inc(dve_done, 1)
                            dve.wait_ge(dve_done, now(g, DN, 2))
                            nc.vector.tensor_tensor(q[:, :, :], q[:, :, :], rden[:, :, :], ALU.mult).then_inc(dve_done, 1)
                            dve.wait_ge(pe_done, now(g, 2, 2))
                            dve.wait_ge(dve_done, prev(g, DN, 5))
                            nc.vector.tensor_scalar(two(part[:, :]), ps[:, 4:6, 0:HC], 1.0 / HEADS, col(BOH), ALU.mult, ALU.add).then_inc(dve_done, 1)
                            dve.wait_ge(dve_done, now(g, DN, 4))
                            nc.vector.tensor_tensor(xg, xg, part[:, :], ALU.add).then_inc(dve_done, 1)

        def layer2_degrees():
            with stage("dve_done", "deg_out") as (block, dve_done, deg_out):
                @block.vector
                def _(dve):
                    nc.vector.tensor_scalar(dinv[:, :], acc[:, 1, 0:NP], 1.0, None, ALU.max).then_inc(dve_done, 1)
                    dve.wait_ge(dve_done, 1)
                    nc.vector.reciprocal(dinv[:, :], dinv[:, :]).then_inc(dve_done, 1)
                    dve.wait_ge(dve_done, 2)
                    nc.vector.tensor_scalar(dinv[:, :], dinv[:, :], 0.5, None, ALU.mult).then_inc(dve_done, 1)

                @block.sync
                def _(sp):
                    sp.dma_start(deg_tab, acc[:, 1, 0:NP]).then_inc(deg_out, 16)
                    sp.wait_ge(deg_out, 16)

        def layer2_step(step):
            before_last = step == ORDER - 1
            with ExitStack() as st:
                def tmp(name, shape, dt=F32):
                    return st.enter_context(nc.sbuf_tensor(f"{name}_s{step}", shape, dt))
                q, rden, xh, mean = [tmp(k, [P, HEADS, GC]) for k in ("q", "rden", "xh", "mean")]
                rows = tmp("rows", [P, GW, HEADS * P])
                y_rows = tmp("y_rows", [P, GW, P])
                with stage("loaded", "pe_done", "act_done", "dve_done", "stored") as (
                        block, loaded, pe_done, act_done, dve_done, stored):
                    PN, AN, DN, OUT = 4 + before_last, 2 + before_last, 7, 16 + 16 * before_last

                    @block.sync
                    def _(sp):
                        nc.sync.sem_inc(stored, OUT)
                        with loop(sp, G) as g:
                            c = bass.ds(g * GC, GC)
                            sp.wait_ge(dve_done, prev(g, DN, 4))
                            for h in range(HEADS):
                                sp.dma_start(q[:, h, :], q_tab[h * P:(h + 1) * P, c]).then_inc(loaded, 16)
                                sp.dma_start(rden[:, h, :], rden_tab[h * P:(h + 1) * P, c]).then_inc(loaded, 16)
                            sp.wait_ge(act_done, now(g, AN, 2))
                            sp.dma_start(windows(xh_tab, g, HEADS * P), rows[:, :, :]).then_inc(stored, 16)
                            if before_last:
                                sp.wait_ge(act_done, now(g, AN, 3))
                                sp.dma_start(windows(x_tab, g, P), y_rows[:, :, :]).then_inc(stored, 16)
                        sp.wait_ge(stored, OUT * G + OUT)

                    @block.tensor
                    def _(pe):
                        nc.tensor.sem_inc(pe_done, PN)
                        with loop(pe, G) as g:
                            pe.wait_ge(loaded, 64 * g + 64)
                            pe.wait_ge(dve_done, prev(g, DN, 4))
                            if before_last:
                                pe.wait_ge(act_done, prev(g, AN, 3))
                            for h in range(HEADS):
                                last = two_matmuls(pe, 2 * h, kv[:, h, :], q[:, h, :])
                            last.then_inc(pe_done, 1)
                            pe.wait_ge(dve_done, now(g, DN, 6))
                            pe.wait_ge(dve_done, prev(g, DN, 7))
                            for h in range(HEADS):
                                last = two_matmuls(pe, 4, wt(WO[h][step]), xh[:, h, :], start=(h == 0), stop=(h == HEADS - 1))
                            last.then_inc(pe_done, 1)
                            for h in range(HEADS):
                                pe.wait_ge(act_done, now(g, AN, h) if h else prev(g, AN, 2))
                                for k in range(GW):
                                    last = nc.tensor.transpose(flat[:, 3072 + k * P:3072 + (k + 1) * P], xh[:, h, k * P:(k + 1) * P], ident[:, :])
                                last.then_inc(pe_done, 1)
                            if before_last:
                                for k in range(GW):
                                    for h in range(HEADS):
                                        last = nc.tensor.matmul(flat[:, k * P:(k + 1) * P], xh[:, h, k * P:(k + 1) * P], wt(WO[h][ORDER]),
                                                                start=(h == 0), stop=(h == HEADS - 1))
                                last.then_inc(pe_done, 1)

                    @block.scalar
                    def _(act):
                        nc.scalar.sem_inc(act_done, AN)
                        with loop(act, G) as g:
                            act.wait_ge(stored, OUT * g + OUT)
                            for h in range(HEADS):
                                act.wait_ge(pe_done, now(g, PN, 3 + h))
                                nc.scalar.copy(rows[:, :, h * P:(h + 1) * P],
                                               flat[:, 3072:3072 + GC].rearrange("p (k f) -> p k f", k=GW)).then_inc(act_done, 1)
                            if before_last:
                                act.wait_ge(pe_done, now(g, PN, 5))
                                nc.scalar.copy(y_rows[:, :, :], flat[:, 0:GC].rearrange("p (k f) -> p k f", k=GW)).then_inc(act_done, 1)

                    @block.vector
                    def _(dve):
                        nc.vector.sem_inc(dve_done, DN)
                        with loop(dve, G) as g:
                            c = bass.ds(g * GC, GC)
                            for h in range(HEADS):
                                nc.vector.tensor_tensor(mean[:, h, :], acc[:, h if step > 1 else 0, c], dinv[:, c], ALU.mult).then_inc(dve_done, 1)
                            dve.wait_ge(loaded, 64 * g + 64)
                            dve.wait_ge(pe_done, now(g, PN, 1))
                            dve.wait_ge(pe_done, prev(g, PN, PN))
                            for h in range(HEADS):
                                nc.vector.scalar_tensor_tensor(out=two(xh[:, h, :]), in0=two(rden[:, h, :]), scalar=kv_sums[:, h:h + 1],
                                                               in1=ps[:, 2 * h:2 * h + 2, 0:HC], op0=ALU.mult, op1=ALU.add).then_inc(dve_done, 1)
                            for h in range(HEADS):
                                dve.wait_ge(dve_done, now(g, DN, 3 + h))
                                nc.vector.tensor_tensor(xh[:, h, :], xh[:, h, :], mean[:, h, :], ALU.add).then_inc(dve_done, 1)
                            dve.wait_ge(pe_done, now(g, PN, 2))
                            nc.vector.scalar_tensor_tensor(out=two(xT[:, c]), in0=ps[:, 4:6, 0:HC], scalar=1.0 / HEADS, in1=two(xT[:, c]),
                                                           op0=ALU.mult, op1=ALU.add).then_inc(dve_done, 1)

        def layer2_last():
            with ExitStack() as st:
                def tmp(name, shape, dt=F32):
                    return st.enter_context(nc.sbuf_tensor(f"{name}_l", shape, dt))
                q, rden, att = [tmp(k, [P, HEADS, GC]) for k in ("q", "rden", "att")]
                mean, both = [tmp(k, [P, GC]) for k in ("mean", "both")]
                with stage("loaded", "pe_done", "dve_done") as (block, loaded, pe_done, dve_done):
                    DN = 5

                    @block.sync
                    def _(sp):
                        with loop(sp, G) as g:
                            c = bass.ds(g * GC, GC)
                            sp.wait_ge(dve_done, prev(g, DN, 3))
                            for h in range(HEADS):
                                sp.dma_start(q[:, h, :], q_tab[h * P:(h + 1) * P, c]).then_inc(loaded, 16)
                                sp.dma_start(rden[:, h, :], rden_tab[h * P:(h + 1) * P, c]).then_inc(loaded, 16)

                    @block.tensor
                    def _(pe):
                        nc.tensor.sem_inc(pe_done, 2)
                        with loop(pe, G) as g:
                            pe.wait_ge(loaded, 64 * g + 64)
                            pe.wait_ge(dve_done, prev(g, DN, 3))
                            for h in range(HEADS):
                                last = two_matmuls(pe, 2 * h, kv[:, h, :], q[:, h, :])
                            last.then_inc(pe_done, 1)
                            pe.wait_ge(dve_done, now(g, DN, 3))
                            pe.wait_ge(dve_done, prev(g, DN, 4))
                            for h in range(HEADS):
                                last = two_matmuls(pe, 4, wt(WO[h][ORDER]), att[:, h, :], start=(h == 0), stop=(h == HEADS - 1))
                            last.then_inc(pe_done, 1)

                    @block.vector
                    def _(dve):
                        nc.vector.sem_inc(dve_done, DN)
                        with loop(dve, G) as g:
                            c = bass.ds(g * GC, GC)
                            dve.wait_ge(dve_done, prev(g, DN, 4))
                            nc.vector.tensor_tensor(mean[:, :], acc[:, 0, c], dinv[:, c], ALU.mult).then_inc(dve_done, 1)
                            dve.wait_ge(loaded, 64 * g + 64)
                            dve.wait_ge(pe_done, now(g, 2, 1))
                            dve.wait_ge(pe_done, prev(g, 2, 2))
                            for h in range(HEADS):
                                nc.vector.scalar_tensor_tensor(out=two(att[:, h, :]), in0=two(rden[:, h, :]), scalar=kv_sums[:, h:h + 1],
                                                               in1=ps[:, 2 * h:2 * h + 2, 0:HC], op0=ALU.mult, op1=ALU.add).then_inc(dve_done, 1)
                            dve.wait_ge(pe_done, now(g, 2, 2))
                            dve.wait_ge(dve_done, prev(g, DN, 5))
                            dve.wait_ge(dve_done, now(g, DN, 1))
                            nc.vector.tensor_tensor(two(both[:, :]), two(mean[:, :]), ps[:, 4:6, 0:HC], ALU.add).then_inc(dve_done, 1)
                            dve.wait_ge(dve_done, now(g, DN, 4))
                            nc.vector.scalar_tensor_tensor(out=xT[:, c], in0=both[:, :], scalar=1.0 / HEADS, in1=xT[:, c],
                                                           op0=ALU.mult, op1=ALU.add).then_inc(dve_done, 1)

        def layer3_tables():
            with ExitStack() as st:
                def tmp(name, shape, dt=F32):
                    return st.enter_context(nc.sbuf_tensor(f"{name}_t", shape, dt))
                xg = tmp("xg", [P, GC])
                p_rows, q_rows = [tmp(k, [P, GW, P]) for k in ("p_rows", "q_rows")]
                with stage("pe_done", "act_done", "dve_done", "stored") as (block, pe_done, act_done, dve_done, stored):
                    def bank_rows(m):
                        return flat[:, 1024 * m:1024 * m + GC].rearrange("p (k f) -> p k f", k=GW)

                    @block.scalar
                    def _(act):
                        nc.scalar.sem_inc(act_done, 2)
                        with loop(act, G) as g:
                            act.wait_ge(pe_done, g + 1)
                            nc.scalar.copy(xg[:, :], xT[:, bass.ds(g * GC, GC)]).then_inc(act_done, 1)
                            act.wait_ge(pe_done, g + 2)
                            act.wait_ge(stored, 32 * g + 32)
                            nc.scalar.copy(p_rows[:, :, :], bank_rows(0)).then_inc(act_done, 1)

                    @block.tensor
                    def _(pe):
                        nc.tensor.sem_inc(pe_done, 1)
                        with loop(pe, G) as g:
                            pe.wait_ge(act_done, now(g, 2, 1))
                            pe.wait_ge(dve_done, g + 1)
                            for m in range(2):
                                for k in range(GW):
                                    last = nc.tensor.matmul(flat[:, 1024 * m + k * P:1024 * m + (k + 1) * P], xg[:, k * P:(k + 1) * P],
                                                            wt(W3[m]), start=True, stop=True)
                            last.then_inc(pe_done, 1)

                    @block.vector
                    def _(dve):
                        nc.vector.sem_inc(dve_done, 1)
                        with loop(dve, G) as g:
                            dve.wait_ge(pe_done, g + 2)
                            dve.wait_ge(stored, 32 * g + 32)
                            nc.vector.tensor_tensor(q_rows[:, :, :], bank_rows(1), bias_rows[:, 2:3, :].to_broadcast([P, GW, P]),
                                                    ALU.add).then_inc(dve_done, 1)

                    @block.sync
                    def _(sp):
                        nc.sync.sem_inc(stored, 32)
                        with loop(sp, G) as g:
                            sp.wait_ge(act_done, now(g, 2, 2))
                            sp.dma_start(windows(p_tab, g, P), p_rows[:, :, :]).then_inc(stored, 16)
                            sp.wait_ge(dve_done, g + 2)
                            sp.dma_start(windows(q3_tab, g, P), q_rows[:, :, :]).then_inc(stored, 16)
                        sp.wait_ge(stored, 32 * G + 32)

        def message_pass(wide_path):
            W = 14
            OH = 7
            tag = "_w" if wide_path else ""
            with ExitStack() as st:
                def tmp(name, shape, dt=F32):
                    return st.enter_context(nc.sbuf_tensor(f"{name}_m{tag}", shape, dt))
                rows = tmp("rows", [P, U, P])
                attr = tmp("attr", [P, 2, MH, P])
                win = tmp("win", [P, W, P])
                onehot = tmp("onehot", [P, OH, P])
                turn = tmp("turn", [P, 2, 2, P])
                pre, hid = tmp("pre", [P, 2, P]), tmp("hid", [P, 2, P])
                idx = tmp("idx", [P, 2, H], I32)
                names = [f"rows_in{j}" for j in range(U)] + [f"win_in{k}" for k in range(W)] + ["attr_in0", "attr_in1"]
                names += ["cleared", "idx_copied", "begun", "matched", "turned", "copied", "mixed", "met", "rectified", "summed",
                          "added", "moved", "rest_in"]
                with stage(*names) as (block, *s):
                    rows_in, win_in, attr_in = s[0:U], s[U:U + W], s[U + W:U + W + 2]
                    cleared, idx_copied, begun, matched, turned, copied, mixed, met, rectified, summed, added, moved, rest_in = s[U + W + 2:]
                    steps = TILES // MU
                    lead = MH + 1

                    def done(n, j):
                        return n * MU + j + 1 + lead

                    ends = FULL - (steps - 1) * MU

                    def ended_rounds(eng, step):
                        if not wide_path:
                            with loop(eng, steps - 1) as i:
                                step(i, i, 0, False)
                            step(steps - 1, steps - 1, 0, True)
                            return
                        with loop(eng, ROUNDS - 1) as r:
                            if eng is nc.sync:
                                eng.wait_ge(moved, 3 * r + 3)
                                eng.sem_inc(begun, 1)
                            with loop(eng, steps - 1) as i:
                                step(r * steps + i, i, r, False)
                            step(r * steps + (steps - 1), steps - 1, r, True)

                    @block.gpsimd
                    def _(pool):
                        def step(n, i):
                            for j in range(U):
                                if j % H == 0:
                                    pool.wait_ge(idx_copied, 2 * n + j // H + 1)
                                    nc.gpsimd.sem_inc(begun, 1)
                                nc.gpsimd.indirect_dma_start(
                                    rows[:, j, :], None, p_tab,
                                    bass.IndirectOffsetOnAxis(ap=idx[:, j // H, j % H:j % H + 1], axis=0)).then_inc(rows_in[j], 16)

                        rounds(nc.gpsimd, "wide_m_pool", wide_path, TILES // U, step)

                    @block.sync
                    def _(sp):
                        regs = [nc.sync.alloc_register(f"msg_base{tag}{k}") for k in range(H)]

                        def step(n, i, r, last):
                            for j in range(MU):
                                if j % H == 0:
                                    nc.sync.load(regs, base_row[0:1, bass.ds(i * MU + j, H)])
                                    base = [nc.sync.snap(r, min_val=0, max_val=NP) for r in regs]
                                if j % MH == 0:
                                    h = j // MH
                                    sp.wait_ge(turned, done(n, j - MH - 1))
                                    nc.sync.sem_inc(begun, 1)
                                    for k in range(0, MH, H):
                                        whole = min(H, ends - j - k) if last else H
                                        sp.dma_start(attr[:, h, k:k + whole, :],
                                                     edge_attr_128[bass.ds((i * MU + j + k) * P, whole * P), :].rearrange("(t p) f -> p t f", p=P)
                                                     ).then_inc(attr_in[h], 16)
                                        if whole < H:
                                            sp.dma_start(attr[0:REST, h, k + whole, :], edge_attr_128[FULL * P:E, :]).then_inc(rest_in, 16)
                                sp.wait_ge(mixed, done(n, j - W))
                                sp.dma_start(win[:, j % W, :], q3_tab[bass.ds(base[j % H], P), :]).then_inc(win_in[j % W], 16)

                        if not wide_path:
                            ended_rounds(nc.sync, step)
                        else:
                            with when_wide(nc.sync, "wide_m_sp"):
                                ended_rounds(nc.sync, step)

                    @block.vector
                    def _(dve):
                        regs = [nc.vector.alloc_register(f"msg_sum_base{tag}{k}") for k in range(H)]
                        for sem in (matched, met, added):
                            nc.vector.sem_inc(sem, lead)
                        if not wide_path:
                            nc.vector.memset(acc[:, 0, :], 0.0).then_inc(cleared, 1)
                            dve.wait_ge(cleared, 1)

                        def meet(n, j):
                            dve.wait_ge(mixed, done(n, j))
                            dve.wait_ge(rows_in[j % U], 16 * (n * (MU // U) + j // U + 1))
                            dve.wait_ge(rectified, done(n, j - 2))
                            nc.vector.tensor_tensor(pre[:, j % 2, :], ps[:, 2 + j % 2, 0:P], rows[:, j % U, :], ALU.add).then_inc(met, 1)

                        def add(n, j, base):
                            dve.wait_ge(summed, done(n, j))
                            dve.wait_ge(added, done(n, j - 1))
                            a = acc[:, 0, bass.ds(base, P)]
                            nc.vector.tensor_tensor(a, a, ps[:, 4 + j % 2, 0:P], ALU.add).then_inc(added, 1)

                        def step(n, i):
                            bases = []
                            for j in range(MU + 4):
                                if j < MU:
                                    dve.wait_ge(summed, done(n, j - OH))
                                    nc.vector.tensor_scalar(onehot[:, j % OH, :], iota16[:, :], loc_col[:, bass.ds(i * MU + j, 1)], None,
                                                            ALU.is_equal).then_inc(matched, 1)
                                if 2 <= j < MU + 2:
                                    meet(n, j - 2)
                                if j >= 4:
                                    if (j - 4) % H == 0:
                                        nc.vector.load(regs, base_row[0:1, bass.ds(i * MU + j - 4, H)])
                                        bases += [nc.vector.snap(r, min_val=0, max_val=NP) for r in regs]
                                    add(n, j - 4, bases[j - 4])

                        if not wide_path:
                            rounds(dve, "", False, steps, step)
                        else:
                            with when_wide(nc.vector, "wide_m_dve"):
                                with loop(dve, ROUNDS - 1) as r:
                                    dve.wait_ge(mixed, r * TILES + lead)
                                    move_windows(dve, moved, begun, r)
                                    with loop(dve, steps) as i:
                                        step(r * steps + i, i)
                                dve.wait_ge(mixed, (ROUNDS - 1) * TILES + lead)
                                windows_back(dve, moved)

                    @block.tensor
                    def _(pe):
                        for sem in (turned, mixed, summed):
                            nc.tensor.sem_inc(sem, lead)

                        def mix(n, j):
                            pe.wait_ge(copied, done(n, j))
                            pe.wait_ge(win_in[j % W], 16 * (n * (MU // W) + j // W + 1))
                            pe.wait_ge(met, done(n, j - 2))
                            nc.tensor.matmul(ps[:, 2 + j % 2, 0:P], turn[:, j % 2, 0, :], win[:, j % W, :], start=True, stop=False)
                            nc.tensor.matmul(ps[:, 2 + j % 2, 0:P], turn[:, j % 2, 1, :], wt(W3[2]), start=False, stop=True).then_inc(mixed, 1)

                        def total(n, j):
                            pe.wait_ge(rectified, done(n, j))
                            pe.wait_ge(added, done(n, j - 2))
                            nc.tensor.matmul(ps[:, 4 + j % 2, 0:P], hid[:, j % 2, :], onehot[:, j % OH, :], start=True, stop=True).then_inc(summed, 1)

                        def step(n, i, r, last):
                            for j in range(MU + 3):
                                if j < MU:
                                    if j % MH == 0:
                                        pe.wait_ge(attr_in[j // MH], 32 * n + 32)
                                    if last and j == ends:
                                        pe.wait_ge(rest_in, 16 * r + 16)
                                    pe.wait_ge(matched, done(n, j))
                                    pe.wait_ge(copied, done(n, j - 2))
                                    nc.tensor.transpose(ps[:, j % 2, 0:P], onehot[:, j % OH, :], ident[:, :])
                                    nc.tensor.transpose(ps[:, j % 2, P:2 * P], attr[:, j // MH, j % MH, :], ident[:, :]).then_inc(turned, 1)
                                if 1 <= j <= MU:
                                    mix(n, j - 1)
                                if j >= 3:
                                    total(n, j - 3)

                        if not wide_path:
                            ended_rounds(nc.tensor, step)
                        else:
                            with when_wide(nc.tensor, "wide_m_pe"):
                                ended_rounds(nc.tensor, step)

                    @block.scalar
                    def _(act):
                        for sem in (copied, rectified):
                            nc.scalar.sem_inc(sem, lead)
                        nc.scalar.copy(idx[:, 0, :], src_idx[:, 0:H]).then_inc(idx_copied, 1)

                        def rectify(n, j):
                            act.wait_ge(met, done(n, j))
                            act.wait_ge(summed, done(n, j - 2))
                            nc.scalar.activation(hid[:, j % 2, :], pre[:, j % 2, :], ACT.Relu).then_inc(rectified, 1)

                        def step(n, i):
                            for j in range(MU + 2):
                                if j < MU:
                                    if j % H == 3:
                                        act.wait_ge(met, done(n, j - 4))
                                        nc.scalar.copy(idx[:, (j // H + 1) % 2, :], src_idx[:, bass.ds(i * MU + j - 3 + H, H)]).then_inc(idx_copied, 1)
                                    act.wait_ge(turned, done(n, j))
                                    act.wait_ge(mixed, done(n, j - 2))
                                    nc.scalar.copy(turn[:, j % 2, :, :], ps[:, j % 2, 0:2 * P].rearrange("p (a n) -> p a n", a=2)).then_inc(copied, 1)
                                if j >= 2:
                                    rectify(n, j - 2)

                        rounds(nc.scalar, "wide_m_act", wide_path, steps, step)

        def layer3_nodes():
            with ExitStack() as st:
                def tmp(name, shape, dt=F32):
                    return st.enter_context(nc.sbuf_tensor(f"{name}_u", shape, dt))
                deg, msg, r, z, hn, cand, diff = [tmp(k, [P, GC]) for k in ("deg", "msg", "r", "z", "hn", "cand", "diff")]
                with stage("deg_in", "pe_done", "act_done", "dve_done") as (block, deg_in, pe_done, act_done, dve_done):
                    PN, AN, DN = 2, 3, 7

                    @block.sync
                    def _(sp):
                        with loop(sp, G) as g:
                            sp.wait_ge(dve_done, prev(g, DN, 1))
                            sp.dma_start(deg[:, :], deg_tab[:, bass.ds(g * GC, GC)]).then_inc(deg_in, 16)

                    @block.tensor
                    def _(pe):
                        nc.tensor.sem_inc(pe_done, PN)

                        def gate(bank, pairs):
                            for n, (w, rhs) in enumerate(pairs):
                                for b in range(2):
                                    last = nc.tensor.matmul(ps[:, bank + b, 0:HC], wt(w), rhs(b), start=(n == 0), stop=(n == len(pairs) - 1))
                            return last

                        with loop(pe, G) as g:
                            def sums(b):
                                return acc[:, 0, bass.ds(g * GC + b * HC, HC)]

                            def xs(b):
                                return xT[:, bass.ds(g * GC + b * HC, HC)]

                            def msgs(b):
                                return msg[:, b * HC:(b + 1) * HC]
                            pe.wait_ge(dve_done, prev(g, DN, 2))
                            gate(0, [(W3O, sums)]).then_inc(pe_done, 1)
                            pe.wait_ge(dve_done, now(g, DN, 1))
                            pe.wait_ge(act_done, prev(g, AN, 2))
                            pe.wait_ge(dve_done, prev(g, DN, 3))
                            gate(2, [(WIH[0], msgs), (WHH[0], xs)])
                            gate(4, [(WIH[1], msgs), (WHH[1], xs)])
                            gate(6, [(WIH[2], msgs)])
                            gate(0, [(WHH[2], xs)]).then_inc(pe_done, 1)

                    @block.scalar
                    def _(act):
                        nc.scalar.sem_inc(act_done, AN)
                        with loop(act, G) as g:
                            act.wait_ge(pe_done, now(g, PN, 2))
                            act.wait_ge(dve_done, prev(g, DN, 5))
                            nc.scalar.activation(two(r[:, :]), ps[:, 2:4, 0:HC], ACT.Sigmoid, bias=col(BRZ[0])).then_inc(act_done, 1)
                            nc.scalar.activation(two(z[:, :]), ps[:, 4:6, 0:HC], ACT.Sigmoid, bias=col(BRZ[1])).then_inc(act_done, 1)
                            act.wait_ge(dve_done, now(g, DN, 3))
                            act.wait_ge(dve_done, prev(g, DN, 6))
                            nc.scalar.activation(cand[:, :], hn[:, :], ACT.Tanh, bias=col(BIH[2])).then_inc(act_done, 1)

                    @block.vector
                    def _(dve):
                        nc.vector.sem_inc(dve_done, DN)
                        with loop(dve, G) as g:
                            xg = xT[:, bass.ds(g * GC, GC)]
                            dve.wait_ge(pe_done, now(g, PN, 1))
                            dve.wait_ge(deg_in, 16 * g + 16)
                            dve.wait_ge(pe_done, prev(g, PN, 2))
                            nc.vector.scalar_tensor_tensor(out=two(msg[:, :]), in0=two(deg[:, :]), scalar=col(B32), in1=ps[:, 0:2, 0:HC],
                                                           op0=ALU.mult, op1=ALU.add).then_inc(dve_done, 1)
                            dve.wait_ge(act_done, now(g, AN, 1))
                            dve.wait_ge(act_done, prev(g, AN, 3))
                            nc.vector.scalar_tensor_tensor(out=two(hn[:, :]), in0=ps[:, 0:2, 0:HC], scalar=col(BHH[2]), in1=two(r[:, :]),
                                                           op0=ALU.add, op1=ALU.mult).then_inc(dve_done, 1)
                            dve.wait_ge(dve_done, now(g, DN, 2))
                            nc.vector.tensor_tensor(two(hn[:, :]), two(hn[:, :]), ps[:, 6:8, 0:HC], ALU.add).then_inc(dve_done, 1)
                            dve.wait_ge(act_done, now(g, AN, 3))
                            nc.vector.tensor_tensor(diff[:, :], xg, cand[:, :], ALU.subtract).then_inc(dve_done, 1)
                            dve.wait_ge(dve_done, now(g, DN, 4))
                            nc.vector.tensor_tensor(diff[:, :], diff[:, :], z[:, :], ALU.mult).then_inc(dve_done, 1)
                            dve.wait_ge(dve_done, now(g, DN, 5))
                            nc.vector.tensor_tensor(diff[:, :], diff[:, :], cand[:, :], ALU.add).then_inc(dve_done, 1)
                            dve.wait_ge(dve_done, now(g, DN, 6))
                            dve.wait_ge(pe_done, now(g, PN, 2))
                            nc.vector.tensor_tensor(xg, xg, diff[:, :], ALU.add).then_inc(dve_done, 1)

        def store_output():
            with stage("stored") as (block, stored):
                @block.sync
                def _(sp):
                    sp.dma_start(out, x_tab[0:N, :]).then_inc(stored, 16)
                    sp.wait_ge(stored, 16)

        def over_edges(pass_, *args, **kwargs):
            for wide_path in (False, True):
                pass_(*args, wide_path=wide_path, **kwargs)

        run = [load_weights, prepare_edges, first_linear, lambda: over_edges(scatter_pass, 0), lambda: layer0_nodes(0),
               lambda: over_edges(scatter_pass, 1), lambda: layer0_nodes(1), lambda: normalize(0, x_tab),
               lambda: over_edges(gather_pass, 0, x_tab, 1, weighted=True), layer1_nodes, lambda: normalize(1, x_tab),
               layer2_keys, lambda: layer2_keys_values(0, x_tab, 1), layer2_denominators,
               lambda: over_edges(gather_pass, 1, x_tab, 1, degree=True), layer2_degrees, lambda: layer2_step(1),
               lambda: layer2_keys_values(1, xh_tab, HEADS), lambda: over_edges(gather_pass, 2, xh_tab, HEADS), lambda: layer2_step(2),
               lambda: layer2_keys_values(2, xh_tab, HEADS), lambda: over_edges(gather_pass, 3, xh_tab, HEADS), lambda: layer2_step(3),
               lambda: layer2_keys_values(3, xh_tab, HEADS), lambda: over_edges(gather_pass, 4, x_tab, 1), layer2_last,
               lambda: normalize(2, x_tab), layer3_tables, lambda: over_edges(message_pass), layer3_nodes, lambda: normalize(3, x_tab), store_output]
        for f in run[0:upto + 1]:
            f()


_INS = ["x", "src", "dst", "edge_attr_128", "edge_weight", "L0_gnn_W1", "L0_gnn_b1", "L0_gnn_W2", "L0_gnn_b2",
        "L0_gnn_W3", "L0_gnn_b3", "L1_gnn_W1", "L1_gnn_b1", "L1_gnn_W2", "L1_gnn_b2", "L2_gnn_Wq_w", "L2_gnn_Wq_b",
        "L2_gnn_Wk_w", "L2_gnn_Wk_b", "L2_gnn_Wo_w", "L2_gnn_Wo_b", "L3_gnn_W1", "L3_gnn_b1", "L3_gnn_W2", "L3_gnn_b2",
        "L3_gnn_W_ih", "L3_gnn_b_ih", "L3_gnn_W_hh", "L3_gnn_b_hh"]


def kernel(**inputs):
    import numpy as np
    import concourse.bacc as bacc
    from concourse.bass_utils import run_bass_kernel_spmd

    nc = bacc.Bacc("TRN2", target_bir_lowering=False, num_devices=1)
    arrays, args = {}, {}
    for name in _INS:
        a = np.ascontiguousarray(inputs[name])
        arrays[f"in_{name}"] = a
        args[name] = nc.dram_tensor(f"in_{name}", a.shape, mybir.dt.from_np(a.dtype), kind="ExternalInput").ap()
    out = nc.dram_tensor("out_0", (N, P), F32, kind="ExternalOutput").ap()
    gnn_resnorm(nc, out, **args)
    r = run_bass_kernel_spmd(nc, [arrays], core_ids=[0])
    return r.results[0]["out_0"]
```

```python
import concourse.bass as bass
from concourse import mybir
from contextlib import ExitStack, contextmanager

F32 = mybir.dt.float32
BF16 = mybir.dt.bfloat16
I32 = mybir.dt.int32
I16 = mybir.dt.int16
ALU = mybir.AluOpType
ACT = mybir.ActivationFunctionType
AX = mybir.AxisListType

P = 128
N = 6250
E = 100000
EPS = 1e-5
WIN = (N + P - 1) // P
NP = WIN * P
AW = NP + P
GW = 7
G = WIN // GW
GC = GW * P
HC = GC // 2
FULL = E // P
REST = E - FULL * P
TILES = 784
CH = (TILES + P - 1) // P
U = 28
H = U // 2
SU = 56
SH = 8
NH = SU // SH
TABS = 8
HW = P + 4
TRASH = NP
HEADS = 2
ORDER = 4
MU = 56
MH = MU // 2
ROUNDS = WIN


def prev(step, per, k):
    return step * per + k


def now(step, per, k):
    return step * per + per + k


def gnn_resnorm(nc, out, x, src, dst, edge_attr_128, edge_weight,
                L0_gnn_W1, L0_gnn_b1, L0_gnn_W2, L0_gnn_b2, L0_gnn_W3, L0_gnn_b3,
                L1_gnn_W1, L1_gnn_b1, L1_gnn_W2, L1_gnn_b2,
                L2_gnn_Wq_w, L2_gnn_Wq_b, L2_gnn_Wk_w, L2_gnn_Wk_b, L2_gnn_Wo_w, L2_gnn_Wo_b,
                L3_gnn_W1, L3_gnn_b1, L3_gnn_W2, L3_gnn_b2,
                L3_gnn_W_ih, L3_gnn_b_ih, L3_gnn_W_hh, L3_gnn_b_hh):
    ctx = ExitStack()
    with ctx:
        ctx.enter_context(nc.allow_non_contiguous_dma(reason="biases by feature and one number per tile: a few thousand elements"))

        def sb(name, shape, dt=F32):
            return ctx.enter_context(nc.sbuf_tensor(name, shape, dt))

        def dram(name, shape, dt=F32):
            return nc.dram_tensor(name, shape, dt, kind="Internal").ap()

        def loop(eng, count):
            return nc.Fori(0, count, engines=(eng.engine,), hint_back_edge=True)

        def wait_past(eng, sem, value):
            if not isinstance(value, int) or value > 0:
                eng.wait_ge(sem, value)

        def when_wide(eng, name):
            flag = eng.alloc_register(name)
            eng.load(flag, wide[0:1, 0:1])
            return eng.If_ne(flag, 0)

        def move_windows(dve, moved, begun, r):
            nc.vector.tensor_scalar(loc_col[:, :], loc_col[:, :], float(P), None, ALU.subtract).then_inc(moved, 1)
            nc.vector.tensor_scalar(base_f[:, :], base_f[:, :], float(P), None, ALU.add).then_inc(moved, 1)
            dve.wait_ge(moved, 3 * r + 2)
            nc.vector.tensor_scalar(base_row[:, :], base_f[:, :], float(NP), None, ALU.min).then_inc(moved, 1)
            dve.wait_ge(moved, 3 * r + 3)
            nc.vector.sem_inc(begun, 1)

        def windows_back(dve, moved):
            back = float(P * (ROUNDS - 1))
            nc.vector.tensor_scalar(loc_col[:, :], loc_col[:, :], back, None, ALU.add).then_inc(moved, 1)
            nc.vector.tensor_scalar(base_f[:, :], base_f[:, :], back, None, ALU.subtract).then_inc(moved, 1)
            dve.wait_ge(moved, 3 * (ROUNDS - 1) + 2)
            nc.vector.tensor_copy(base_row[:, :], base_f[:, :]).then_inc(moved, 1)
            dve.wait_ge(moved, 3 * (ROUNDS - 1) + 3)

        def rounds(eng, name, wide_path, steps, step):
            if not wide_path:
                with loop(eng, steps) as i:
                    step(i, i)
                return
            with when_wide(eng, name):
                with loop(eng, ROUNDS - 1) as r:
                    with loop(eng, steps) as i:
                        step(r * steps + i, i)

        @contextmanager
        def stage(*names):
            stage.n += 1
            sems = [nc.alloc_semaphore(f"{n}_{stage.n}") for n in names]
            with nc.Block() as block:
                yield (block, *sems)
            nc.clear_and_free_semaphores(sems)
            nc.all_engine_barrier()
        stage.n = 0

        def two(ap):
            return ap.rearrange("p (b n) -> p b n", b=2)

        def windows(table, g, width):
            return table[bass.ds(g * GC, GC), 0:width].rearrange("(k p) f -> p k f", p=P)

        ident = sb("ident", [P, P])
        ones_mat = sb("ones_mat", [P, P])
        ones_bf = sb("ones_bf", [P, P], BF16)
        iota16 = sb("iota16", [P, P], I16)
        tri = sb("tri", [P, P])
        trash = sb("trash", [P, 1])
        eps_col = sb("eps_col", [P, 1])
        is_node = sb("is_node", [P, WIN, HEADS])
        src_idx = sb("src_idx", [P, TILES + H], I32)
        src_col = sb("src_col", [P, TILES])
        loc_col = sb("loc_col", [P, TILES])
        ew_col = sb("ew_col", [P, TILES])
        scat_idx = sb("scat_idx", [P, TILES], I32)
        base_row = sb("base_row", [1, TILES], I32)
        base_f = sb("base_f", [1, TILES])
        wide = sb("wide", [1, 2], I32)
        dinv = sb("dinv", [P, NP])
        kv = sb("kv", [P, HEADS, P])
        kv_sums = sb("kv_sums", [P, 2 * HEADS])
        key_sum = sb("key_sum", [P, HEADS, P])
        xT = sb("xT", [P, AW])
        acc = sb("acc", [P, HEADS, AW])
        wts = sb("wts", [P, 30, P])
        cols = sb("cols", [P, 24])
        bias_rows = sb("bias_rows", [P, 5, P])
        ps = ctx.enter_context(nc.psum_tensor("ps", [P, 8, 512], F32))
        flat = ps[:, :, :].rearrange("p b n -> p (b n)")

        xpad = dram("xpad", [NP, P])
        h_tab = dram("h_tab", [AW, HW])
        sums = [[dram(f"sums{m}_{k}", [AW, HW]) for k in range(TABS)] for m in range(2)]
        src_rows = dram("src_rows", [TILES + SH, P])
        tile_info = dram("tile_info", [2, CH * P])
        x_tab = dram("x_tab", [NP, P])
        xh_tab = dram("xh_tab", [NP, HEADS * P])
        k_tab = dram("k_tab", [NP, HEADS * P])
        q_tab = dram("q_tab", [HEADS * P, NP])
        rden_tab = dram("rden_tab", [HEADS * P, NP])
        deg_tab = dram("deg_tab", [P, NP])
        p_tab = dram("p_tab", [NP, P])
        q3_tab = dram("q3_tab", [AW, P])

        W0 = [0, 1, 2]
        W1A, W1B = 3, 4
        WQ, WK = [5, 6], [7, 8]
        WO = [[9 + h * (ORDER + 1) + k for k in range(ORDER + 1)] for h in range(HEADS)]
        W3 = [19, 20, 21]
        W3O = 22
        WIH, WHH = [23, 24, 25], [26, 27, 28]
        B03, B11, B12, BQ, BO, B32, BIH, BHH = 0, 1, 2, [3, 4], 5, 6, [7, 8, 9], [10, 11, 12]
        BRZ, BOH, VS = [13, 14], 15, [16, 17]

        def wt(n):
            return wts[:, n, :]

        def col(n):
            return cols[:, n:n + 1]

        def two_matmuls(eng, bank, lhsT, rhs, start=True, stop=True):
            for b in range(2):
                last = nc.tensor.matmul(ps[:, bank + b, 0:HC], lhsT, rhs[:, b * HC:(b + 1) * HC],
                                        start=start, stop=stop)
            return last

        def load_weights():
            with ExitStack() as st:
                raw = st.enter_context(nc.sbuf_tensor("raw_w", [P, 13, P], F32))
                with stage("w_in", "filled", "made", "turned", "copied", "padded") as (
                        block, w_in, filled, made, turned, copied, padded):
                    natural = [L0_gnn_W1, L0_gnn_W2, L0_gnn_W3]
                    natural += [L3_gnn_W1[:, k * P:(k + 1) * P] for k in range(3)] + [L3_gnn_W2]
                    natural += [L3_gnn_W_ih[k * P:(k + 1) * P, :] for k in range(3)]
                    natural += [L3_gnn_W_hh[k * P:(k + 1) * P, :] for k in range(3)]
                    places = W0 + W3 + [W3O] + WIH + WHH
                    direct = [(W1A, L1_gnn_W1), (W1B, L1_gnn_W2)]
                    for h in range(HEADS):
                        direct += [(WQ[h], L2_gnn_Wq_w[:, h * P:(h + 1) * P]),
                                   (WK[h], L2_gnn_Wk_w[:, h * P:(h + 1) * P])]
                        direct += [(WO[h][k], L2_gnn_Wo_w[(h * (ORDER + 1) + k) * P:(h * (ORDER + 1) + k + 1) * P, :])
                                   for k in range(ORDER + 1)]
                    columns = [(B03, L0_gnn_b3), (B11, L1_gnn_b1), (B12, L1_gnn_b2), (BO, L2_gnn_Wo_b),
                               (B32, L3_gnn_b2)]
                    columns += [(BQ[h], L2_gnn_Wq_b[h * P:(h + 1) * P]) for h in range(HEADS)]
                    columns += [(BIH[k], L3_gnn_b_ih[k * P:(k + 1) * P]) for k in range(3)]
                    columns += [(BHH[k], L3_gnn_b_hh[k * P:(k + 1) * P]) for k in range(3)]
                    along = [L0_gnn_b1, L0_gnn_b2, L3_gnn_b1, L2_gnn_Wk_b[0:P], L2_gnn_Wk_b[P:2 * P]]
                    loads = 16 * (len(natural) + len(direct) + len(columns) + len(along))

                    @block.sync
                    def _(sp):
                        for n, w in enumerate(natural):
                            sp.dma_start(raw[:, n, :], w).then_inc(w_in, 16)
                        for n, w in direct:
                            sp.dma_start(wt(n), w).then_inc(w_in, 16)
                        for n, b in columns:
                            sp.dma_start(col(n), b.rearrange("(p a) -> p a", a=1)).then_inc(w_in, 16)
                        for n, b in enumerate(along):
                            sp.dma_start(bias_rows[:, n, :], b.partition_broadcast(P)).then_inc(w_in, 16)
                        sp.dma_start(xpad[0:N, :], x).then_inc(padded, 16)
                        sp.wait_ge(filled, 3)
                        sp.dma_start(xpad[N:NP, :], acc[0:NP - N, 0, 0:P]).then_inc(padded, 16)
                        sp.dma_start(h_tab[NP:AW, :], acc[:, 0, 0:HW]).then_inc(padded, 16)
                        sp.dma_start(q3_tab[NP:AW, :], acc[:, 0, 0:P]).then_inc(padded, 16)
                        for m in range(2):
                            for k in range(TABS):
                                sp.dma_start(sums[m][k][NP:AW, :], acc[:, 0, 0:HW]).then_inc(padded, 16)
                        sp.wait_ge(padded, 16 * (4 + 2 * TABS))

                    @block.gpsimd
                    def _(pool):
                        nc.gpsimd.memset(ident[:, :], 0.0).then_inc(made, 1)
                        nc.gpsimd.memset(ones_mat[:, :], 1.0).then_inc(made, 1)
                        nc.gpsimd.iota(iota16[:, :], pattern=[[1, P]], base=0, channel_multiplier=0).then_inc(made, 1)
                        nc.gpsimd.iota(trash[:, :], pattern=[[0, 1]], base=TRASH, channel_multiplier=1,
                                       allow_small_or_imprecise_dtypes=True).then_inc(made, 1)
                        pool.wait_ge(made, 4)
                        nc.gpsimd.affine_select(out=ident[:, :], in_=ident[:, :], compare_op=ALU.not_equal, fill=1.0,
                                                base=0, pattern=[[-1, P]], channel_multiplier=1).then_inc(made, 1)
                        pool.wait_ge(filled, 1)
                        nc.gpsimd.affine_select(out=is_node[:, WIN - 1, :], in_=is_node[:, WIN - 1, :], compare_op=ALU.is_ge, fill=0.0,
                                                base=P - (NP - N) - 1, pattern=[[0, HEADS]], channel_multiplier=-1).then_inc(made, 1)
                        nc.gpsimd.affine_select(out=tri[:, :], in_=ones_mat[:, :], compare_op=ALU.is_gt, fill=0.0,
                                                base=0, pattern=[[-1, P]], channel_multiplier=1).then_inc(made, 1)

                    @block.vector
                    def _(dve):
                        nc.vector.memset(is_node[:, :, :], 1.0).then_inc(filled, 1)
                        nc.vector.memset(acc[:, :, :], 0.0).then_inc(filled, 1)
                        nc.vector.memset(xT[:, NP:AW], 0.0).then_inc(filled, 1)
                        nc.vector.memset(eps_col[:, :], EPS).then_inc(filled, 1)
                        dve.wait_ge(made, 7)
                        nc.vector.tensor_copy(ones_bf[:, :], ones_mat[:, :]).then_inc(filled, 1)
                        dve.wait_ge(w_in, loads)
                        for k in range(2):
                            nc.vector.tensor_tensor(col(BRZ[k]), col(BIH[k]), col(BHH[k]), ALU.add).then_inc(filled, 1)
                        nc.vector.tensor_scalar(col(BOH), col(BO), 1.0 / HEADS, None, ALU.mult).then_inc(filled, 1)

                    @block.tensor
                    def _(pe):
                        pe.wait_ge(w_in, loads)
                        pe.wait_ge(made, 7)
                        for n in range(len(natural)):
                            last = nc.tensor.transpose(flat[:, n * P:(n + 1) * P], raw[:, n, :], ident[:, :])
                        last.then_inc(turned, 1)

                    @block.scalar
                    def _(act):
                        act.wait_ge(turned, 1)
                        for n, place in enumerate(places):
                            nc.scalar.copy(wt(place), flat[:, n * P:(n + 1) * P]).then_inc(copied, 1)

        def prepare_edges():
            with ExitStack() as st:
                def tmp(name, shape, dt=F32):
                    return st.enter_context(nc.sbuf_tensor(name, shape, dt))
                src_i, dst_i = tmp("src_i", [P, CH, P], I32), tmp("dst_i", [P, CH, P], I32)
                src_f, dst_f, ew_f = tmp("src_f", [P, CH, P]), tmp("dst_f", [P, CH, P]), tmp("ew_f", [P, CH, P])
                loc_f = tmp("loc_f", [P, CH, P])
                info = tmp("info", [P, 2, CH])
                infos = tmp("infos", [1, 2, CH * P + 1])
                with stage("cleared", "e_in", "dve_done", "turned", "copied", "info_out", "info_in", "based") as (
                        block, cleared, e_in, dve_done, turned, copied, info_out, info_in, based):
                    last = CH - 1
                    lead = last * P
                    tail = FULL - lead
                    fill = (P - REST) // REST

                    @block.sync
                    def _(sp):
                        sp.wait_ge(cleared, 3)
                        for a, v in ((src_i, src), (dst_i, dst), (ew_f, edge_weight)):
                            sp.dma_start(a[:, 0:last, :], v[0:lead * P].rearrange("(c t p) -> t c p", c=last, p=P)).then_inc(e_in, 16)
                            sp.dma_start(a[0:tail, last, :], v[lead * P:FULL * P].rearrange("(t p) -> t p", p=P)).then_inc(e_in, 16)
                            for k in range(fill + 1):
                                sp.dma_start(a[tail:tail + 1, last, k * REST:(k + 1) * REST],
                                             v[FULL * P:E].rearrange("(t p) -> t p", t=1)).then_inc(e_in, 16)
                        sp.wait_ge(dve_done, 2)
                        sp.dma_start(src_rows[0:lead, :].rearrange("(c t) p -> t c p", c=last), src_f[:, 0:last, :]).then_inc(info_out, 16)
                        sp.dma_start(src_rows[lead:TILES, :], src_f[0:TILES - lead, last, :]).then_inc(info_out, 16)
                        sp.dma_start(src_rows[TILES:TILES + SH, :], src_f[0:SH, 0, :]).then_inc(info_out, 16)
                        sp.wait_ge(dve_done, 6)
                        for k in range(2):
                            sp.dma_start(tile_info[k, :].rearrange("(c t) -> t c", c=CH), info[:, k, :]).then_inc(info_out, 16)
                        sp.wait_ge(info_out, 80)
                        sp.dma_start(infos[0:1, 0, 0:CH * P], tile_info[0:1, :]).then_inc(info_in, 16)
                        sp.dma_start(infos[0:1, 1, 0:CH * P], tile_info[1:2, :]).then_inc(info_in, 16)

                    @block.vector
                    def _(dve):
                        for a in (src_i, dst_i, ew_f):
                            nc.vector.memset(a[:, last, :], 0).then_inc(cleared, 1)
                        dve.wait_ge(e_in, 16 * 3 * (fill + 3))
                        nc.vector.tensor_copy(src_f[:, :, :], src_i[:, :, :]).then_inc(dve_done, 1)
                        nc.vector.tensor_copy(dst_f[:, :, :], dst_i[:, :, :]).then_inc(dve_done, 1)
                        dve.wait_ge(dve_done, 2)
                        nc.vector.tensor_reduce(info[:, 0, :], dst_f[:, :, :], AX.X, ALU.min).then_inc(dve_done, 1)
                        nc.vector.tensor_reduce(info[:, 1, :], dst_f[:, :, :], AX.X, ALU.max).then_inc(dve_done, 1)
                        dve.wait_ge(dve_done, 4)
                        nc.vector.tensor_tensor(info[:, 1, :], info[:, 1, :], info[:, 0, :], ALU.subtract).then_inc(dve_done, 1)
                        nc.vector.tensor_tensor(loc_f[:, :, :], dst_f[:, :, :],
                                                info[:, 0, :].unsqueeze(2).to_broadcast([P, CH, P]), ALU.subtract).then_inc(dve_done, 1)
                        dve.wait_ge(info_in, 32)
                        nc.vector.tensor_copy(base_row[0:1, :], infos[0:1, 0, 0:TILES]).then_inc(based, 1)
                        nc.vector.tensor_copy(base_f[0:1, :], infos[0:1, 0, 0:TILES]).then_inc(based, 1)
                        nc.vector.tensor_reduce(infos[0:1, 0, CH * P:CH * P + 1], infos[0:1, 1, 0:TILES], AX.X, ALU.max).then_inc(based, 1)
                        dve.wait_ge(based, 3)
                        nc.vector.tensor_scalar(wide[0:1, 0:1], infos[0:1, 0, CH * P:CH * P + 1], float(P), None, ALU.is_ge).then_inc(based, 1)
                        dve.wait_ge(copied, 4)
                        nc.vector.memset(loc_col[:, FULL + 1:TILES], -1.0).then_inc(based, 1)
                        nc.vector.tensor_copy(src_col[:, FULL + 1:TILES], trash[:, 0:1].to_broadcast([P, TILES - FULL - 1])).then_inc(based, 1)
                        for p0 in range(REST, P, 32):
                            nc.vector.memset(loc_col[p0:p0 + 32, FULL:FULL + 1], -1.0).then_inc(based, 1)
                            nc.vector.tensor_copy(src_col[p0:p0 + 32, FULL:FULL + 1], trash[p0:p0 + 32, :]).then_inc(based, 1)

                    @block.tensor
                    def _(pe):
                        pe.wait_ge(dve_done, 6)
                        for n, a in enumerate((src_f, loc_f, ew_f)):
                            for c in range(CH):
                                lastmm = nc.tensor.transpose(flat[:, n * 1024 + c * P:n * 1024 + (c + 1) * P], a[:, c, :], ident[:, :])
                            lastmm.then_inc(turned, 1)

                    @block.scalar
                    def _(act):
                        for n, to in ((0, src_col), (0, src_idx), (1, loc_col), (2, ew_col)):
                            act.wait_ge(turned, n + 1)
                            nc.scalar.copy(to[:, 0:TILES], flat[:, n * 1024:n * 1024 + TILES]).then_inc(copied, 1)
                        nc.scalar.copy(src_idx[:, TILES:TILES + H], flat[:, 0:H]).then_inc(copied, 1)

        def lagged(eng, *works):
            most = max(lag for lag, work in works)

            def at(step):
                for lag, work in works:
                    if not isinstance(step, int) or 0 <= step - lag < G:
                        work(step - lag)

            for step in range(most):
                at(step)
            with nc.Fori(most, G, engines=(eng.engine,), hint_back_edge=True) as g:
                at(g)
            for step in range(G, G + most):
                at(step)

        class Norm:
            signals = ["ln_taken", "ln_turned", "ln_measured", "ln_rooted", "ln_normed", "ln_back", "ln_in_place", "ln_stored",
                       "ln_begun", "ln_zero"]
            MN = 2 * GW + 1

            def __init__(self, tmp, table):
                self.table, self.last = table, table is out
                self.xg, self.zeros = tmp("ln_xg", [P, GC]), tmp("ln_zeros", [P, NP - N])
                self.rows, self.parts = tmp("ln_rows", [P, GW, P]), tmp("ln_parts", [P, GW, 6])
                self.mean_var = tmp("mean_var", [P, GW, 2])
                self.sd, self.rstd = tmp("sd", [P, GW]), tmp("rstd", [P, GW])
                self.z = flat[:, 2048:2048 + GC].rearrange("p (k f) -> p k f", k=GW)

            def take(self, *signals):
                (self.taken, self.turned, self.measured, self.rooted, self.normed, self.back, self.in_place, self.stored,
                 self.begun, self.zero) = signals

            def start(self, eng):
                if eng is nc.vector:
                    nc.vector.memset(self.zeros[:, :], 0.0).then_inc(self.zero, 1)
                    nc.vector.sem_inc(self.normed, GW)
                elif eng is nc.tensor:
                    nc.tensor.sem_inc(self.turned, 1)
                    nc.tensor.sem_inc(self.back, 1)
                elif eng is nc.scalar:
                    nc.scalar.sem_inc(self.in_place, 1)
                    nc.scalar.sem_inc(self.stored, 16)

            def turn(self, g):
                nc.tensor.wait_ge(self.taken, g + 1)
                nc.tensor.wait_ge(self.normed, (g + 1) * GW)
                for k in range(GW):
                    last = nc.tensor.transpose(flat[:, 2048 + k * P:2048 + (k + 1) * P], self.xg[:, k * P:(k + 1) * P], ident[:, :])
                last.then_inc(self.turned, 1)

            def turn_back(self, g):
                if self.last:
                    return
                nc.tensor.wait_ge(self.normed, (g + 2) * GW)
                nc.tensor.wait_ge(self.in_place, g + 1)
                for k in range(GW):
                    last = nc.tensor.transpose(flat[:, 3072 + k * P:3072 + (k + 1) * P], self.rows[:, k, :], ident[:, :])
                last.then_inc(self.back, 1)

            def copy(self, g, ready):
                nc.scalar.wait_ge(self.turned, g + 1)
                ready(g)
                nc.scalar.sem_inc(self.begun, 1)
                xg = xT[:, bass.ds(g * GC, GC)]
                if isinstance(g, int) and g == G - 1:
                    n = GC - (NP - N)
                    nc.scalar.wait_ge(self.zero, 1)
                    nc.scalar.copy(self.xg[:, n:GC], self.zeros[:, :])
                    nc.scalar.copy(self.xg[:, 0:n], xT[:, g * GC:g * GC + n]).then_inc(self.taken, 1)
                else:
                    nc.scalar.copy(self.xg[:, :], xg).then_inc(self.taken, 1)

            def root(self, g):
                nc.scalar.wait_ge(self.measured, g * self.MN + 2 * GW)
                nc.scalar.activation(self.sd[:, :], self.mean_var[:, :, 1], ACT.Sqrt, bias=eps_col[:, 0:1]).then_inc(self.rooted, 1)

            def norm(self, g):
                MN, dve = self.MN, nc.vector
                dve.wait_ge(self.turned, g + 2)
                for k in range(GW):
                    nc.vector.bn_stats(self.parts[:, k, :], self.z[:, k, :]).then_inc(self.measured, 1)
                dve.wait_ge(self.measured, g * MN + GW)
                nc.vector.sem_inc(self.begun, 1)
                for k in range(GW):
                    nc.vector.bn_aggr(self.mean_var[:, k, :], self.parts[:, k, :]).then_inc(self.measured, 1)
                dve.wait_ge(self.rooted, g + 1)
                nc.vector.reciprocal(self.rstd[:, :], self.sd[:, :]).then_inc(self.measured, 1)
                dve.wait_ge(self.measured, g * MN + MN)
                dve.wait_ge(self.stored, 16 * g + 16)
                if not self.last:
                    dve.wait_ge(self.back, g + 1)
                for k in range(GW):
                    nc.vector.tensor_scalar(self.rows[:, k, :], self.z[:, k, :], self.mean_var[:, k, 0:1], self.rstd[:, k:k + 1],
                                            ALU.subtract, ALU.mult).then_inc(self.normed, 1)

            def put(self, g):
                if self.last:
                    return
                nc.scalar.wait_ge(self.back, g + 2)
                nc.scalar.sem_inc(self.begun, 1)
                nc.scalar.copy(xT[:, bass.ds(g * GC, GC)], flat[:, 3072:3072 + GC]).then_inc(self.in_place, 1)

            def store(self, g):
                act, table = nc.scalar, self.table
                act.wait_ge(self.normed, (g + 2) * GW)
                if self.last and isinstance(g, int) and g == G - 1:
                    act.dma_start(table[NP - GC:NP - P, :].rearrange("(k p) f -> p k f", p=P), self.rows[:, 0:GW - 1, :]).then_inc(self.stored, 16)
                    act.dma_start(table[NP - P:N, :], self.rows[0:N - (NP - P), GW - 1, :]).then_inc(self.stored, 16)
                else:
                    act.dma_start(windows(table, g, P), self.rows[:, :, :]).then_inc(self.stored, 16)

            def end(self):
                nc.scalar.wait_ge(self.stored, 16 * G + 16 + 16 * self.last)

        def first_linear():
            with ExitStack() as st:
                rows = st.enter_context(nc.sbuf_tensor("x_rows", [P, GW, P], F32))
                zT = st.enter_context(nc.sbuf_tensor("zT0", [P, GC], F32))
                h_rows = st.enter_context(nc.sbuf_tensor("h_rows0", [P, GW, HW], F32))
                with stage("x_in", "pe_done", "act_done", "dve_done", "stored", "filled", "zeroed") as (
                        block, x_in, pe_done, act_done, dve_done, stored, filled, zeroed):
                    @block.sync
                    def _(sp):
                        nc.sync.sem_inc(stored, 16)
                        sp.wait_ge(filled, 1)
                        with loop(sp, G) as g:
                            sp.wait_ge(pe_done, prev(g, 2, 1))
                            sp.dma_start(rows[:, :, :], windows(xpad, g, P)).then_inc(x_in, 16)
                            for k in range(TABS):
                                sp.dma_start(windows(sums[0][k], g, HW), acc[:, 0, 0:GW * HW].rearrange("p (k f) -> p k f", k=GW)).then_inc(zeroed, 16)
                            sp.wait_ge(dve_done, now(g, 1, 1))
                            sp.dma_start(windows(h_tab, g, HW), h_rows[:, :, :]).then_inc(stored, 16)
                        sp.wait_ge(stored, 16 * G + 16)
                        sp.wait_ge(zeroed, 16 * G * TABS)

                    @block.tensor
                    def _(pe):
                        nc.tensor.sem_inc(pe_done, 2)
                        with loop(pe, G) as g:
                            pe.wait_ge(x_in, 16 * g + 16)
                            pe.wait_ge(act_done, prev(g, 2, 2))
                            for k in range(GW):
                                last = nc.tensor.transpose(flat[:, k * P:(k + 1) * P], rows[:, k, :], ident[:, :])
                            last.then_inc(pe_done, 1)
                            pe.wait_ge(act_done, now(g, 2, 1))
                            pe.wait_ge(dve_done, prev(g, 1, 1))
                            for k in range(GW):
                                last = nc.tensor.matmul(flat[:, 1024 + k * P:1024 + (k + 1) * P], zT[:, k * P:(k + 1) * P],
                                                        wt(W0[0]), start=True, stop=True)
                            last.then_inc(pe_done, 1)

                    @block.scalar
                    def _(act):
                        nc.scalar.sem_inc(act_done, 2)
                        with loop(act, G) as g:
                            act.wait_ge(pe_done, now(g, 2, 1))
                            nc.scalar.copy(zT[:, :], flat[:, 0:GC]).then_inc(act_done, 1)
                            nc.scalar.copy(xT[:, bass.ds(g * GC, GC)], flat[:, 0:GC]).then_inc(act_done, 1)

                    @block.vector
                    def _(dve):
                        nc.vector.memset(h_rows[:, :, P:HW], 1.0).then_inc(filled, 1)
                        nc.vector.sem_inc(dve_done, 1)
                        with loop(dve, G) as g:
                            dve.wait_ge(pe_done, now(g, 2, 2))
                            dve.wait_ge(stored, 16 * g + 16)
                            nc.vector.tensor_tensor(h_rows[:, :, 0:P], flat[:, 1024:1024 + GC].rearrange("p (k f) -> p k f", k=GW),
                                                    bias_rows[:, 0:1, :].to_broadcast([P, GW, P]), ALU.add).then_inc(dve_done, 1)

        def scatter_pass(m, wide_path):
            W = 8
            OS = SU // 2
            ranking = m == 0 and not wide_path
            count = m == 1
            tag = f"{m}{'w' if wide_path else ''}"
            with ExitStack() as st:
                def tmp(name, shape, dt=F32):
                    return st.enter_context(nc.sbuf_tensor(f"{name}_sc{tag}", shape, dt))
                win = tmp("win", [P, W, HW])
                src_bc = tmp("src_bc", [P, NH, SH * P])
                onehot = tmp("onehot", [P, 2, P], BF16)
                same = tmp("same", [P, 2, P], BF16)
                hits = tmp("hits", [P, 2, P])
                earlier, to_row = tmp("earlier", [P, SH]), tmp("to_row", [P, SH])
                pick = tmp("pick", [P, 2, P])
                out_rows = tmp("out_rows", [P, OS, HW])
                idx = tmp("idx", [P, NH, SH], I32)
                names = [f"win_in{k}" for k in range(W)] + [f"bc{h}" for h in range(NH)] + [f"added{k}" for k in range(TABS)]
                names += ["matched", "ranked", "joined", "pick_copied", "summed", "sum_copied", "idx_copied", "begun", "moved", "zeroed", "counted", "added_up"]
                with stage(*names) as (block, *s):
                    win_in, bc, added = s[0:W], s[W:W + NH], s[W + NH:W + NH + TABS]
                    matched, ranked, joined, pick_copied, summed, sum_copied, idx_copied, begun, moved, zeroed, counted, added_up = s[W + NH + TABS:]
                    steps = TILES // SU
                    ZR = 4
                    per = SU // TABS

                    def scatter_rounds(eng, step):
                        if not wide_path:
                            step(0, 0)
                            with nc.Fori(1, steps, engines=(eng.engine,), hint_back_edge=True) as i:
                                step(i, i)
                            return
                        with when_wide(eng, f"wide_{tag}"):
                            step(0, 0)
                            with nc.Fori(1, steps, engines=(eng.engine,), hint_back_edge=True) as i:
                                step(i, i)
                            with nc.Fori(1, ROUNDS - 1, engines=(eng.engine,), hint_back_edge=True) as r:
                                with loop(eng, steps) as i:
                                    step(r * steps + i, i)

                    @block.sync
                    def _(sp):
                        regs = [nc.sync.alloc_register(f"win_base{tag}_{k}") for k in range(SH)]

                        def load_sources(slot, tile):
                            sp.dma_start(src_bc[:, slot, :], src_rows[bass.ds(tile, SH), :].rearrange("t p -> (t p)").partition_broadcast(P)
                                         ).then_inc(bc[slot], 16)

                        def step(n, i):
                            for h in range(NH):
                                nc.sync.load(regs, base_row[0:1, bass.ds(i * SU + h * SH, SH)])
                                base = [nc.sync.snap(x, min_val=0, max_val=NP) for x in regs]
                                sp.wait_ge(matched, prev(n, SU, (h + 2) * SH))
                                load_sources((h + 1) % NH, i * SU + (h + 1) * SH)
                                for k in range(SH):
                                    j = h * SH + k
                                    sp.wait_ge(summed, n * SU + j + 1)
                                    sp.dma_start(win[:, j % W, :], h_tab[bass.ds(base[k], P), :]).then_inc(win_in[j % W], 16)
                                    if ranking and j % (SU // TABS) == 0:
                                        sp.dma_start(sums[1][j // (SU // TABS)][bass.ds(i * (NP // steps), NP // steps), :].rearrange("(p r) f -> p (r f)", r=ZR),
                                                     acc[0:NP // steps // ZR, 0, 0:ZR * HW]).then_inc(zeroed, 16)

                        if not wide_path:
                            load_sources(0, 0)
                            rounds(sp, "", False, steps, step)
                            sp.wait_ge(bc[0], 16 * steps + 16)
                            if ranking:
                                sp.wait_ge(zeroed, 16 * TABS * steps)
                        else:
                            with when_wide(nc.sync, f"wide_sp_{tag}"):
                                load_sources(0, 0)
                                with loop(sp, ROUNDS - 1) as r:
                                    sp.wait_ge(moved, 3 * r + 3)
                                    nc.sync.sem_inc(begun, 1)
                                    with loop(sp, steps) as i:
                                        step(r * steps + i, i)
                                sp.wait_ge(bc[0], 16 * (ROUNDS - 1) * steps + 16)

                    @block.vector
                    def _(dve):
                        nc.vector.sem_inc(matched, SU)
                        nc.vector.sem_inc(added_up, 2)
                        regs = [nc.vector.alloc_register(f"count_base{tag}_{k}") for k in range(SH)]
                        if count and not wide_path:
                            nc.vector.memset(acc[:, 1, :], 0.0).then_inc(added_up, 1)
                            dve.wait_ge(added_up, 3)
                        else:
                            nc.vector.sem_inc(added_up, 1)

                        def add_up(n, j, base):
                            dve.wait_ge(counted, n * SU + j + 1)
                            dve.wait_ge(added_up, n * SU + j + 3)
                            a = acc[:, 1, bass.ds(base, P)]
                            nc.vector.tensor_tensor(a, a, ps[:, 4 + j % 2, 0:P], ALU.add).then_inc(added_up, 1)

                        def count_earlier(n, h, k):
                            if k >= 2:
                                dve.wait_ge(ranked, (NH * n + h) * (SH + 5) + k - 1)
                            nc.vector.scalar_tensor_tensor(
                                out=hits[:, k % 2, :], in0=src_bc[:, h, k * P:(k + 1) * P],
                                scalar=src_col[:, bass.ds(n * SU + h * SH + k, 1)], in1=tri[:, :],
                                op0=ALU.is_equal, op1=ALU.mult, accum_out=earlier[:, k:k + 1]).then_inc(ranked, 1)

                        def rank(n, h):
                            at = (NH * n + h) * (SH + 5) + SH
                            c = bass.ds(n * SU + h * SH, SH)
                            dve.wait_ge(ranked, at)
                            nc.vector.tensor_scalar(earlier[:, :], earlier[:, :], 1.0, None, ALU.min).then_inc(ranked, 1)
                            nc.vector.tensor_scalar(to_row[:, :], src_col[:, c], trash[:, 0:1], -1.0,
                                                    ALU.subtract, ALU.mult).then_inc(ranked, 1)
                            dve.wait_ge(ranked, at + 2)
                            nc.vector.tensor_tensor(to_row[:, :], to_row[:, :], earlier[:, :], ALU.mult).then_inc(ranked, 1)
                            dve.wait_ge(ranked, at + 3)
                            nc.vector.tensor_tensor(to_row[:, :], to_row[:, :], src_col[:, c], ALU.add).then_inc(ranked, 1)
                            dve.wait_ge(ranked, at + 4)
                            nc.vector.tensor_copy(scat_idx[:, c], to_row[:, :]).then_inc(ranked, 1)
                            dve.wait_ge(ranked, at + 5)

                        def rank_next(n, j, last):
                            h, k = (j // SH + 1) % NH, j % SH
                            n_next = n if h else n + 1
                            if last and not h:
                                return
                            if k == 0:
                                dve.wait_ge(bc[h], 16 * n_next + 16)
                            count_earlier(n_next, h, k)
                            if k == SH - 1:
                                rank(n_next, h)

                        def step(n, i, last=False):
                            bases = []
                            for j in range(SU):
                                t = bass.ds(i * SU + j, 1)
                                if count and j % SH == 0:
                                    nc.vector.load(regs, base_row[0:1, bass.ds(i * SU + j, SH)])
                                    bases += [nc.vector.snap(x, min_val=0, max_val=NP) for x in regs]
                                if j % SH == 0:
                                    dve.wait_ge(bc[j // SH], 16 * n + 16)
                                dve.wait_ge(joined, n * SU + j + 1)
                                nc.vector.tensor_scalar(onehot[:, j % 2, :], iota16[:, :], loc_col[:, t], None, ALU.is_equal)
                                nc.vector.tensor_scalar(same[:, j % 2, :], src_bc[:, j // SH, (j % SH) * P:(j % SH + 1) * P],
                                                        src_col[:, t], None, ALU.is_equal).then_inc(matched, 1)
                                if ranking:
                                    rank_next(n, j, last)
                                if count and j >= 2:
                                    add_up(n, j - 2, bases[j - 2])
                            if count:
                                for j in range(SU - 2, SU):
                                    add_up(n, j, bases[j])

                        if ranking:
                            dve.wait_ge(bc[0], 16)
                            for k in range(SH):
                                count_earlier(0, 0, k)
                            rank(0, 0)
                            with loop(dve, steps - 1) as i:
                                step(i, i)
                            step(steps - 1, steps - 1, last=True)
                        elif not wide_path:
                            rounds(dve, "", False, steps, step)
                        else:
                            with when_wide(nc.vector, f"wide_{tag}_dve"):
                                with loop(dve, ROUNDS - 1) as r:
                                    dve.wait_ge(summed, r * TILES + W)
                                    dve.wait_ge(matched, r * TILES + SU)
                                    move_windows(dve, moved, begun, r)
                                    with loop(dve, steps) as i:
                                        step(r * steps + i, i)
                                dve.wait_ge(summed, (ROUNDS - 1) * TILES + W)
                                dve.wait_ge(matched, (ROUNDS - 1) * TILES + SU)
                                windows_back(dve, moved)

                    @block.tensor
                    def _(pe):
                        nc.tensor.sem_inc(joined, 2)
                        nc.tensor.sem_inc(summed, W)

                        def sum_rows(n, j):
                            pe.wait_ge(pick_copied, n * SU + j + 3)
                            pe.wait_ge(win_in[j % W], 16 * (n * (SU // W) + j // W + 1))
                            pe.wait_ge(sum_copied, n * SU + j + 1)
                            nc.tensor.matmul(ps[:, 2 + j % 2, 0:HW], pick[:, j % 2, :], win[:, j % W, :],
                                             start=True, stop=True).then_inc(summed, 1)

                        def step(n, i):
                            for j in range(SU):
                                pe.wait_ge(matched, now(n, SU, j + 1))
                                pe.wait_ge(pick_copied, n * SU + j + 1)
                                if count:
                                    pe.wait_ge(added_up, n * SU + j + 2)
                                    nc.tensor.matmul(ps[:, 4 + j % 2, 0:P], ones_bf[:, :], onehot[:, j % 2, :],
                                                     start=True, stop=True).then_inc(counted, 1)
                                nc.tensor.matmul(ps[:, j % 2, 0:P], onehot[:, j % 2, :], same[:, j % 2, :],
                                                 start=True, stop=True).then_inc(joined, 1)
                                if j:
                                    sum_rows(n, j - 1)
                            sum_rows(n, SU - 1)

                        rounds(pe, f"wide_{tag}_pe", wide_path, steps, step)

                    @block.scalar
                    def _(act):
                        nc.scalar.sem_inc(pick_copied, 2)
                        nc.scalar.sem_inc(sum_copied, 2)

                        def copy_sum(n, j):
                            act.wait_ge(summed, n * SU + j + 1 + W)
                            wait_past(act, added[(j - OS) % TABS], 16 * (n * per + (j - OS) // TABS + 1))
                            nc.scalar.copy(out_rows[:, j % OS, :], ps[:, 2 + j % 2, 0:HW]).then_inc(sum_copied, 1)

                        def step(n, i):
                            for j in range(SU):
                                if j % SH == 0:
                                    for k in range(TABS):
                                        wait_past(act, added[k], 16 * ((n - 1) * per + (j // SH + 1) * (SH // TABS)))
                                    if ranking:
                                        act.wait_ge(ranked, (NH * n + j // SH + 1) * (SH + 5))
                                    nc.scalar.copy(idx[:, j // SH, :], scat_idx[:, bass.ds(i * SU + j, SH)]).then_inc(idx_copied, 1)
                                act.wait_ge(joined, n * SU + j + 3)
                                act.wait_ge(summed, n * SU + j - 1 + W)
                                nc.scalar.copy(pick[:, j % 2, :], ps[:, j % 2, 0:P]).then_inc(pick_copied, 1)
                                if j:
                                    copy_sum(n, j - 1)
                            copy_sum(n, SU - 1)

                        scatter_rounds(nc.scalar, step)

                    @block.gpsimd
                    def _(pool):
                        def step(n, i):
                            for j in range(SU):
                                if j % SH == 0:
                                    pool.wait_ge(idx_copied, n * NH + j // SH + 1)
                                pool.wait_ge(sum_copied, n * SU + j + 3)
                                wait_past(pool, added[j % TABS], 16 * (n * per + j // TABS))
                                nc.gpsimd.sem_inc(begun, 1)
                                nc.gpsimd.indirect_dma_start(
                                    sums[m][j % TABS],
                                    bass.IndirectOffsetOnAxis(ap=idx[:, j // SH, j % SH:j % SH + 1], axis=0),
                                    out_rows[:, j % OS, :], None, compute_op=ALU.add).then_inc(added[j % TABS], 16)

                        scatter_rounds(nc.gpsimd, step)
                        if not wide_path:
                            for k in range(TABS):
                                pool.wait_ge(added[k], 16 * (TILES // TABS))
                        else:
                            with when_wide(nc.gpsimd, f"wide_{tag}_end"):
                                for k in range(TABS):
                                    pool.wait_ge(added[k], 16 * (ROUNDS - 1) * (TILES // TABS))

        def degree_rows(g, dve, half_in, dve_done, tabs, h_rows, per):
            half = TABS // 2
            at = 0
            for b in range(2):
                dve.wait_ge(half_in[b], 16 * half * (g + 1))
                t = [tabs[:, b * half + k] for k in range(half)]
                nc.vector.tensor_tensor(t[0], t[0], t[1], ALU.add).then_inc(dve_done, 1)
                nc.vector.tensor_tensor(t[2], t[2], t[3], ALU.add).then_inc(dve_done, 1)
                dve.wait_ge(dve_done, now(g, per, at + 2))
                if b == 0:
                    dve.wait_ge(dve_done, now(g, per, 2))
                    nc.vector.tensor_tensor(tabs[:, TABS], t[0], t[2], ALU.add).then_inc(dve_done, 1)
                else:
                    nc.vector.tensor_tensor(t[0], t[0], t[2], ALU.add).then_inc(dve_done, 1)
                at += 3
            total, deg = tabs[:, TABS], tabs[:, TABS + 1]
            dve.wait_ge(dve_done, now(g, per, 6))
            nc.vector.tensor_tensor(total, total, tabs[:, half], ALU.add).then_inc(dve_done, 1)
            dve.wait_ge(dve_done, now(g, per, 7))
            nc.vector.tensor_scalar(deg[:, :, 0:1], total[:, :, P:P + 1], 1.0, None, ALU.max).then_inc(dve_done, 1)
            dve.wait_ge(dve_done, now(g, per, 8))
            nc.vector.reciprocal(deg[:, :, 1:2], deg[:, :, 0:1]).then_inc(dve_done, 1)
            dve.wait_ge(dve_done, now(g, per, 9))
            nc.vector.tensor_tensor(h_rows[:, :, :], total[:, :, 0:P], deg[:, :, 1:2].to_broadcast([P, GW, P]), ALU.mult).then_inc(dve_done, 1)

        def layer0_nodes(m):
            with ExitStack() as st:
                def tmp(name, shape, dt=F32):
                    return st.enter_context(nc.sbuf_tensor(f"{name}_n{m}", shape, dt))
                tabs = tmp("tabs", [P, TABS + 2, GW, HW])
                h_rows = tmp("h_rows", [P, GW, P])
                r_rows = tmp("r_rows", [P, GW, P])
                zT = tmp("zT", [P, GC])
                o_rows = tmp("o_rows", [P, GW, HW])
                ln = Norm(tmp, x_tab) if m else None
                ln_signals = ln.signals if m else []
                DN = 10
                with stage("half0_in", "half1_in", "pe_done", "act_done", "dve_done", "stored", "filled", "finished", *ln_signals) as (
                        block, half0_in, half1_in, pe_done, act_done, dve_done, stored, filled, finished, *s):
                    half_in = (half0_in, half1_in)
                    if m:
                        ln.take(*s)

                    @block.sync
                    def _(sp):
                        with loop(sp, G) as g:
                            for b, used in enumerate((3, 7)):
                                sp.wait_ge(dve_done, prev(g, DN, used))
                                for k in range(b * TABS // 2, (b + 1) * TABS // 2):
                                    sp.dma_start(tabs[:, k], windows(sums[m][k], g, HW)).then_inc(half_in[b], 16)

                    @block.vector
                    def _(dve):
                        nc.vector.memset(o_rows[:, :, P:HW], 1.0).then_inc(filled, 1)
                        nc.vector.sem_inc(dve_done, DN)
                        nc.vector.sem_inc(finished, 1)

                        def finish(g):
                            dve.wait_ge(pe_done, now(g, 2, 2))
                            if m == 0:
                                dve.wait_ge(stored, 16 * g + 16)
                                nc.vector.tensor_tensor(o_rows[:, :, 0:P], flat[:, 1024:1024 + GC].rearrange("p (k f) -> p k f", k=GW),
                                                        bias_rows[:, 1:2, :].to_broadcast([P, GW, P]), ALU.add).then_inc(finished, 1)
                            else:
                                xg = two(xT[:, bass.ds(g * GC, GC)])
                                nc.vector.scalar_tensor_tensor(out=xg, in0=ps[:, 2:4, 0:HC], scalar=col(B03), in1=xg,
                                                               op0=ALU.add, op1=ALU.add).then_inc(finished, 1)

                        def rows_of(g):
                            dve.wait_ge(act_done, prev(g, 2, 1))
                            degree_rows(g, dve, half_in, dve_done, tabs, h_rows, DN)

                        if m == 0:
                            lagged(dve, (0, rows_of), (1, finish))
                        else:
                            ln.start(dve)
                            lagged(dve, (0, rows_of), (1, finish), (2, ln.norm))

                    @block.scalar
                    def _(act):
                        nc.scalar.sem_inc(act_done, 2)
                        nc.scalar.sem_inc(stored, 16)
                        act.wait_ge(filled, 1)

                        def turn(g):
                            act.wait_ge(dve_done, now(g, DN, 10))
                            act.wait_ge(pe_done, prev(g, 2, 1))
                            nc.scalar.activation(r_rows[:, :, :], h_rows[:, :, :], ACT.Relu).then_inc(act_done, 1)
                            act.wait_ge(pe_done, now(g, 2, 1))
                            nc.scalar.copy(zT[:, :], flat[:, 0:GC]).then_inc(act_done, 1)

                        def store(g):
                            act.wait_ge(finished, g + 2)
                            act.dma_start(windows(h_tab, g, HW), o_rows[:, :, :]).then_inc(stored, 16)

                        if m == 0:
                            lagged(act, (0, turn), (1, store))
                            act.wait_ge(stored, 16 * G + 16)
                        else:
                            ln.start(act)
                            lagged(act, (0, turn), (1, lambda g: ln.copy(g, lambda g: act.wait_ge(finished, g + 2))), (2, ln.root),
                                   (2, ln.store), (3, ln.put))
                            ln.end()

                    @block.tensor
                    def _(pe):
                        nc.tensor.sem_inc(pe_done, 2)

                        def products(g):
                            pe.wait_ge(act_done, now(g, 2, 1))
                            for k in range(GW):
                                last = nc.tensor.transpose(flat[:, k * P:(k + 1) * P], r_rows[:, k, :], ident[:, :])
                            last.then_inc(pe_done, 1)
                            pe.wait_ge(act_done, now(g, 2, 2))
                            pe.wait_ge(finished, g + 1)
                            if m == 0:
                                for k in range(GW):
                                    last = nc.tensor.matmul(flat[:, 1024 + k * P:1024 + (k + 1) * P], zT[:, k * P:(k + 1) * P],
                                                            wt(W0[1]), start=True, stop=True)
                            else:
                                last = two_matmuls(pe, 2, wt(W0[2]), zT)
                            last.then_inc(pe_done, 1)

                        if m == 0:
                            lagged(pe, (0, products))
                        else:
                            ln.start(pe)
                            lagged(pe, (2, ln.turn), (0, products), (3, ln.turn_back))

        def normalize(n, table):
            with ExitStack() as st:
                def tmp(name, shape, dt=F32):
                    return st.enter_context(nc.sbuf_tensor(f"{name}_{n}", shape, dt))
                ln = Norm(tmp, table)
                with stage(*ln.signals) as (block, *s):
                    ln.take(*s)

                    @block.vector
                    def _(dve):
                        ln.start(dve)
                        lagged(dve, (1, ln.norm))

                    @block.tensor
                    def _(pe):
                        ln.start(pe)
                        lagged(pe, (1, ln.turn), (2, ln.turn_back))

                    @block.scalar
                    def _(act):
                        ln.start(act)
                        lagged(act, (1, ln.root), (0, lambda g: ln.copy(g, lambda g: None)), (1, ln.store), (2, ln.put))
                        ln.end()

        def gather_pass(n, table, heads, wide_path, weighted=False, aside=()):
            width = heads * P
            OH, AHEAD = 7, 4
            tag = f"{n}{'w' if wide_path else ''}"
            with ExitStack() as st:
                def tmp(name, shape, dt=F32):
                    return st.enter_context(nc.sbuf_tensor(f"{name}_g{tag}", shape, dt))
                rows = tmp("rows", [P, U, width])
                onehot = tmp("onehot", [P, OH, P])
                idx = tmp("idx", [P, 2, H], I32)
                phases = [] if wide_path else [[work(tmp) for work in works] for works in aside]
                aside = [work for works in phases for work in works]
                names = [f"rows_in{j}" for j in range(U)] + ["cleared", "idx_copied", "begun", "matched", "tile_done", "added", "moved"]
                names += [name for work in aside for name in work.signals]
                with stage(*names) as (block, *s):
                    rows_in = s[0:U]
                    cleared, idx_copied, begun, matched, tile_done, added, moved = s[U:U + 7]
                    at = U + 7
                    for work in aside:
                        work.take(*s[at:at + len(work.signals)])
                        at += len(work.signals)
                    steps = TILES // U
                    def pieces_of(works):
                        slots = max(work.parts for work in works)
                        return [[(work, k) for work in works if work.parts == slots] +
                                [(work, 0) for work in works if work.parts < slots and k == slots // 2] for k in range(slots)]

                    def steps_between(eng, name, step):
                        if not phases:
                            rounds(eng, name, wide_path, steps, step)
                            return
                        of_group = steps // G // len(phases)
                        for p, works in enumerate(phases):
                            pieces = pieces_of(works)
                            each = of_group // len(pieces)
                            with loop(eng, G) as g:
                                for k, piece in enumerate(pieces):
                                    n = g * of_group + (p * G * of_group + k * each)
                                    step(n, n, [(work, part, g) for work, part in piece])
                                    if each > 1:
                                        with nc.Fori(1, each, engines=(eng.engine,), hint_back_edge=True) as m:
                                            step(n + m, n + m)

                    @block.gpsimd
                    def _(pool):
                        def step(n, i):
                            for j in range(U):
                                if j % H == 0:
                                    pool.wait_ge(idx_copied, 2 * n + j // H + 1)
                                    nc.gpsimd.sem_inc(begun, 1)
                                nc.gpsimd.indirect_dma_start(
                                    rows[:, j, :], None, table,
                                    bass.IndirectOffsetOnAxis(ap=idx[:, j // H, j % H:j % H + 1], axis=0)).then_inc(rows_in[j], 16)

                        rounds(nc.gpsimd, f"wide_g{tag}_pool", wide_path, steps, step)

                    @block.scalar
                    def _(act):
                        def step(n, i, pieces=()):
                            for h in range(2):
                                act.wait_ge(tile_done, prev(n, U, H * (h + 1)))
                                nc.scalar.copy(idx[:, h, :], src_idx[:, bass.ds(i * U + h * H, H)]).then_inc(idx_copied, 1)
                            for work, part, g in pieces:
                                work.do(nc.scalar, part, g)

                        for work in aside:
                            work.start(nc.scalar)
                        steps_between(nc.scalar, f"wide_g{tag}_act", step)

                    @block.vector
                    def _(dve):
                        regs = [nc.vector.alloc_register(f"base{tag}_{k}") for k in range(H)]
                        nc.vector.sem_inc(added, 2)
                        if not wide_path:
                            nc.vector.memset(acc[:, 0:heads, :], 0.0).then_inc(cleared, 1)
                            dve.wait_ge(cleared, 1)

                        def add(n, j, base):
                            dve.wait_ge(tile_done, now(n, U, j + 1))
                            dve.wait_ge(added, n * U + j + 2)
                            a = acc[:, 0:heads, bass.ds(base, P)]
                            nc.vector.tensor_tensor(a, a, ps[:, j % 2, 0:heads * P].rearrange("p (h n) -> p h n", h=heads),
                                                    ALU.add).then_inc(added, 1)

                        def match(n, i, j):
                            dve.wait_ge(tile_done, now(n, U, j - OH + 1))
                            t = bass.ds(i * U + j, 1)
                            if weighted:
                                nc.vector.tensor_scalar(onehot[:, j % OH, :], iota16[:, :], loc_col[:, t], ew_col[:, t],
                                                        ALU.is_equal, ALU.mult).then_inc(matched, 1)
                            else:
                                nc.vector.tensor_scalar(onehot[:, j % OH, :], iota16[:, :], loc_col[:, t], None,
                                                        ALU.is_equal).then_inc(matched, 1)

                        def step(n, i, pieces=()):
                            bases = []
                            for j in range(AHEAD):
                                match(n, i, j)
                            for work, part, g in pieces:
                                work.do(nc.vector, part, g)
                            for j in range(U):
                                if j % H == 0:
                                    nc.vector.load(regs, base_row[0:1, bass.ds(i * U + j, H)])
                                    bases += [nc.vector.snap(r, min_val=0, max_val=NP) for r in regs]
                                if j + AHEAD < U:
                                    match(n, i, j + AHEAD)
                                if j:
                                    add(n, j - 1, bases[j - 1])
                            add(n, U - 1, bases[U - 1])

                        if not wide_path:
                            for work in aside:
                                work.start(nc.vector)
                            steps_between(nc.vector, "", step)
                            for work in aside:
                                work.end(nc.vector)
                        else:
                            with when_wide(nc.vector, f"wide_g{tag}_dve"):
                                with loop(dve, ROUNDS - 1) as r:
                                    move_windows(dve, moved, begun, r)
                                    with loop(dve, steps) as i:
                                        step(r * steps + i, i)
                                windows_back(dve, moved)

                    @block.tensor
                    def _(pe):
                        nc.tensor.sem_inc(tile_done, U)
                        def step(n, i, pieces=()):
                            for work, part, g in pieces:
                                work.do(nc.tensor, part, g)
                            for j in range(U):
                                pe.wait_ge(rows_in[j], 16 * n + 16)
                                pe.wait_ge(matched, n * U + j + 1)
                                pe.wait_ge(added, n * U + j + 1)
                                for h in range(heads):
                                    last = nc.tensor.matmul(ps[:, j % 2, h * P:(h + 1) * P], rows[:, j, h * P:(h + 1) * P],
                                                            onehot[:, j % OH, :], start=True, stop=True)
                                last.then_inc(tile_done, 1)

                        for work in aside:
                            work.start(nc.tensor)
                        steps_between(nc.tensor, f"wide_g{tag}_pe", step)

                    if aside:
                        @block.sync
                        def _(sp):
                            for work in aside:
                                work.start(nc.sync)
                            for works in phases:
                                with loop(nc.sync, G) as g:
                                    for work in sorted(works, key=lambda work: work.parts):
                                        for part in range(work.parts):
                                            work.do(nc.sync, part, g)
                            for work in aside:
                                work.end(nc.sync)

        class Degrees:
            parts = 1
            signals = ["deg_dve", "deg_out", "deg_begun"]

            def __init__(self, tmp):
                pass

            def take(self, dve_done, stored, begun):
                self.dve_done, self.stored, self.begun = dve_done, stored, begun

            def start(self, eng):
                if eng is nc.sync:
                    eng.dma_start(deg_tab, acc[:, 1, 0:NP]).then_inc(self.stored, 16)

            def do(self, eng, part, g):
                if eng is nc.vector:
                    c = bass.ds(g * GC, GC)
                    nc.vector.tensor_scalar(dinv[:, c], acc[:, 1, c], 1.0, 2.0, ALU.max, ALU.mult).then_inc(self.dve_done, 1)
                    eng.wait_ge(self.dve_done, 2 * g + 1)
                    eng.sem_inc(self.begun, 1)
                    nc.vector.reciprocal(dinv[:, c], dinv[:, c]).then_inc(self.dve_done, 1)

            def end(self, eng):
                if eng is nc.sync:
                    eng.wait_ge(self.stored, 16)

        def layer1_nodes():
            with ExitStack() as st:
                def tmp(name, shape, dt=F32):
                    return st.enter_context(nc.sbuf_tensor(f"{name}_1", shape, dt))
                mixed, hid = tmp("mix", [P, GC]), tmp("hid", [P, GC])
                ln = Norm(tmp, x_tab)
                with stage("mixed_done", "first_done", "relu_done", "second_done", "final", *ln.signals) as (
                        block, mixed_done, first_done, relu_done, second_done, final, *s):
                    ln.take(*s)

                    @block.vector
                    def _(dve):
                        nc.vector.sem_inc(final, 1)
                        ln.start(dve)

                        def mix(g):
                            c = bass.ds(g * GC, GC)
                            dve.wait_ge(first_done, g + 1)
                            nc.vector.tensor_tensor(mixed[:, :], xT[:, c], acc[:, 0, c], ALU.add).then_inc(mixed_done, 1)

                        def finish(g):
                            xg = two(xT[:, bass.ds(g * GC, GC)])
                            dve.wait_ge(second_done, g + 2)
                            dve.wait_ge(mixed_done, g + 1)
                            nc.vector.scalar_tensor_tensor(out=xg, in0=ps[:, 2:4, 0:HC], scalar=col(B12), in1=xg,
                                                           op0=ALU.add, op1=ALU.add).then_inc(final, 1)

                        lagged(dve, (0, mix), (1, finish), (2, ln.norm))

                    @block.tensor
                    def _(pe):
                        nc.tensor.sem_inc(first_done, 1)
                        nc.tensor.sem_inc(second_done, 1)
                        ln.start(pe)

                        def first(g):
                            pe.wait_ge(mixed_done, g + 1)
                            pe.wait_ge(relu_done, g + 1)
                            two_matmuls(pe, 0, wt(W1A), mixed).then_inc(first_done, 1)

                        def second(g):
                            pe.wait_ge(relu_done, g + 2)
                            pe.wait_ge(final, g + 1)
                            two_matmuls(pe, 2, wt(W1B), hid).then_inc(second_done, 1)

                        lagged(pe, (1, second), (2, ln.turn), (0, first), (3, ln.turn_back))

                    @block.scalar
                    def _(act):
                        nc.scalar.sem_inc(relu_done, 1)
                        ln.start(act)

                        def relu(g):
                            act.wait_ge(first_done, g + 2)
                            act.wait_ge(second_done, g + 1)
                            nc.scalar.activation(two(hid[:, :]), ps[:, 0:2, 0:HC], ACT.Relu, bias=col(B11)).then_inc(relu_done, 1)

                        lagged(act, (0, relu), (1, lambda g: ln.copy(g, lambda g: act.wait_ge(final, g + 2))), (2, ln.root),
                               (2, ln.store), (3, ln.put))
                        ln.end()

        def layer2_keys():
            KW = HEADS * P
            with ExitStack() as st:
                def tmp(name, shape, dt=F32):
                    return st.enter_context(nc.sbuf_tensor(f"{name}_k", shape, dt))
                xg = tmp("xg", [P, GC])
                k_raw, kk, k_rows = [tmp(k, [P, GW, KW]) for k in ("k_raw", "kk", "k_rows")]
                knorm = tmp("knorm", [P, 4, GW * HEADS])
                with stage("pe_done", "xg_copied", "norms", "dve_done", "k_out", "summed", "added", "begun") as (
                        block, pe_done, xg_copied, norms, dve_done, k_out, summed, added, begun):
                    DN = 6

                    @block.tensor
                    def _(pe):
                        nc.tensor.sem_inc(pe_done, 1)
                        nc.tensor.sem_inc(summed, 1)

                        def products(g):
                            pe.wait_ge(xg_copied, g + 1)
                            pe.wait_ge(dve_done, prev(g, DN, 1))
                            for k in range(GW):
                                last = nc.tensor.matmul(flat[:, k * KW:(k + 1) * KW], xg[:, k * P:(k + 1) * P],
                                                        wts[:, WK[0]:WK[1] + 1, :].rearrange("p a n -> p (a n)"), start=True, stop=True)
                            last.then_inc(pe_done, 1)

                        def sums(g):
                            pe.wait_ge(dve_done, now(g, DN, 6))
                            pe.wait_ge(added, g + 1)
                            for h in range(HEADS):
                                for k in range(GW):
                                    last = nc.tensor.matmul(ps[:, 4 + h, 0:1], k_rows[:, k, h * P:(h + 1) * P], ones_mat[:, 0:1],
                                                            start=(k == 0), stop=(k == GW - 1))
                            last.then_inc(summed, 1)

                        lagged(pe, (0, products), (1, sums))

                    @block.scalar
                    def _(act):
                        def take(g):
                            act.wait_ge(pe_done, g + 1)
                            nc.scalar.sem_inc(begun, 1)
                            nc.scalar.copy(xg[:, :], xT[:, bass.ds(g * GC, GC)]).then_inc(xg_copied, 1)

                        def root(g):
                            act.wait_ge(dve_done, now(g, DN, 3))
                            nc.scalar.activation(knorm[:, 1, :], knorm[:, 0, :], ACT.Sqrt).then_inc(norms, 1)

                        lagged(act, (0, take), (1, root))

                    @block.vector
                    def _(dve):
                        nc.vector.sem_inc(dve_done, DN)
                        nc.vector.memset(kv_sums[:, :], 0.0).then_inc(added, 1)

                        def norm(g):
                            dve.wait_ge(pe_done, g + 2)
                            dve.wait_ge(dve_done, prev(g, DN, 6))
                            nc.vector.tensor_tensor(k_raw[:, :, :], flat[:, 0:GW * KW].rearrange("p (k f) -> p k f", k=GW),
                                                    bias_rows[:, 3:5, :].rearrange("p (o a) n -> p o (a n)", o=1).to_broadcast([P, GW, KW]),
                                                    ALU.add).then_inc(dve_done, 1)
                            dve.wait_ge(dve_done, now(g, DN, 1))
                            nc.vector.tensor_tensor(kk[:, :, :], k_raw[:, :, :], k_raw[:, :, :], ALU.mult).then_inc(dve_done, 1)
                            dve.wait_ge(dve_done, now(g, DN, 2))
                            nc.vector.tensor_reduce(knorm[:, 0, :], kk[:, :, :].rearrange("p k (h f) -> p (k h) f", h=HEADS),
                                                    AX.X, ALU.add).then_inc(dve_done, 1)
                            dve.wait_ge(norms, g + 1)
                            nc.vector.reciprocal(knorm[:, 2, :], knorm[:, 1, :]).then_inc(dve_done, 1)
                            dve.wait_ge(dve_done, now(g, DN, 4))
                            nc.vector.tensor_tensor(knorm[:, 3, :].rearrange("p (k h) -> p k h", h=HEADS), knorm[:, 2, :].rearrange("p (k h) -> p k h", h=HEADS),
                                                    is_node[:, bass.ds(g * GW, GW), :], ALU.mult).then_inc(dve_done, 1)
                            dve.wait_ge(dve_done, now(g, DN, 5))
                            def heads_of(k):
                                return k[:, :, :].rearrange("p k (h f) -> p (k h) f", h=HEADS)
                            dve.wait_ge(k_out, 16 * g + 16)
                            dve.wait_ge(summed, g + 1)
                            nc.vector.tensor_tensor(heads_of(k_rows), heads_of(k_raw), knorm[:, 3, :].unsqueeze(2).to_broadcast([P, GW * HEADS, P]),
                                                    ALU.mult).then_inc(dve_done, 1)

                        def add_sums(g):
                            dve.wait_ge(summed, g + 2)
                            dve.wait_ge(added, g + 1)
                            nc.vector.tensor_tensor(kv_sums[:, HEADS:2 * HEADS], kv_sums[:, HEADS:2 * HEADS],
                                                    ps[:, 4:6, 0:1].rearrange("p b n -> p (b n)"), ALU.add).then_inc(added, 1)

                        lagged(dve, (0, norm), (1, add_sums))
                        dve.wait_ge(added, G + 1)
                        for h in range(HEADS):
                            nc.vector.tensor_copy(key_sum[:, h, :], kv_sums[:, HEADS + h:HEADS + h + 1].to_broadcast([P, P])).then_inc(added, 1)

                    @block.sync
                    def _(sp):
                        nc.sync.sem_inc(k_out, 16)
                        with loop(sp, G) as g:
                            sp.wait_ge(dve_done, now(g, DN, 6))
                            sp.dma_start(windows(k_tab, g, KW), k_rows[:, :, :]).then_inc(k_out, 16)
                        sp.wait_ge(k_out, 16 * G + 16)

        def keys_values(table, heads):
            KW = HEADS * P

            class KeysValues:
                parts = 1
                signals = ["kv_rows_in", "kv_done", "kv_added", "kv_begun"]

                def __init__(self, tmp):
                    self.k_rows = tmp("k_rows", [P, GW, KW])
                    self.x_rows = tmp("x_rows", [P, GW, heads * P])

                def take(self, rows_in, done, added, begun):
                    self.rows_in, self.done, self.added, self.begun = rows_in, done, added, begun

                def start(self, eng):
                    if eng is nc.vector:
                        nc.vector.memset(kv[:, :, :], 0.0).then_inc(self.added, 1)
                        nc.vector.memset(kv_sums[:, 0:HEADS], 0.0).then_inc(self.added, 1)
                    elif eng is nc.tensor:
                        nc.tensor.sem_inc(self.done, 1)

                def do(self, eng, part, g):
                    if eng is nc.sync:
                        eng.wait_ge(self.done, g + 1)
                        eng.sem_inc(self.begun, 1)
                        eng.dma_start(self.k_rows[:, :, :], windows(k_tab, g, KW)).then_inc(self.rows_in, 16)
                        eng.dma_start(self.x_rows[:, :, :], windows(table, g, heads * P)).then_inc(self.rows_in, 16)
                    elif eng is nc.tensor:
                        eng.wait_ge(self.rows_in, 32 * g + 32)
                        eng.wait_ge(self.added, 2 * g + 2)
                        for h in range(HEADS):
                            at = (h % heads) * P
                            for k in range(GW):
                                nc.tensor.matmul(ps[:, 2 + h, 0:P], self.k_rows[:, k, h * P:(h + 1) * P], self.x_rows[:, k, at:at + P],
                                                 start=(k == 0), stop=(k == GW - 1))
                            for k in range(GW):
                                last = nc.tensor.matmul(ps[:, 4 + h, 0:1], self.x_rows[:, k, at:at + P], ones_mat[:, 0:1],
                                                        start=(k == 0), stop=(k == GW - 1))
                        last.then_inc(self.done, 1)
                    elif eng is nc.vector:
                        eng.wait_ge(self.done, g + 2)
                        eng.wait_ge(self.added, 2 * g + 2)
                        nc.vector.tensor_tensor(kv[:, :, :], kv[:, :, :], ps[:, 2:4, 0:P], ALU.add).then_inc(self.added, 1)
                        nc.vector.tensor_tensor(kv_sums[:, 0:HEADS], kv_sums[:, 0:HEADS], ps[:, 4:6, 0:1].rearrange("p b n -> p (b n)"),
                                                ALU.add).then_inc(self.added, 1)

                def end(self, eng):
                    pass

            return KeysValues

        class Queries:
            parts = HEADS + 2
            signals = ["q_pe", "q_act", "q_dve", "q_out", "q_zero", "q_begun"]
            PN, AN, DN = 2 * HEADS + 1, 3 * HEADS, 4 * HEADS + 2

            def __init__(self, tmp):
                self.q, self.norm = [tmp(k, [P, HEADS, GC]) for k in ("q", "qnorm")]
                self.t, self.qd, self.rden = [tmp(k, [P, GC]) for k in ("q_t", "qd", "rden")]
                self.zero = tmp("q_zeros", [P, NP - N])

            def take(self, pe_done, act_done, dve_done, stored, zeroed, begun):
                self.pe_done, self.act_done, self.dve_done = pe_done, act_done, dve_done
                self.stored, self.zeroed, self.begun = stored, zeroed, begun

            def start(self, eng):
                if eng is nc.vector:
                    nc.vector.memset(self.zero[:, :], 0.0).then_inc(self.zeroed, 1)
                    nc.vector.sem_inc(self.dve_done, self.DN)
                elif eng is nc.tensor:
                    nc.tensor.sem_inc(self.pe_done, self.PN)
                elif eng is nc.scalar:
                    nc.scalar.sem_inc(self.act_done, self.AN)
                elif eng is nc.sync:
                    nc.sync.sem_inc(self.stored, 32 * HEADS)

            def do(self, eng, part, g):
                if eng is nc.tensor and part < HEADS:
                    self.products(eng, part, g)
                elif eng is nc.tensor and part == HEADS:
                    eng.wait_ge(self.act_done, now(g, self.AN, self.AN))
                elif eng is nc.scalar and part < HEADS:
                    self.norms(eng, part, g)
                elif eng is nc.vector and 1 <= part <= HEADS:
                    self.quotients(eng, part - 1, g)
                elif eng is nc.sync and 1 <= part <= HEADS:
                    self.store(eng, part - 1, g)
                elif part > HEADS:
                    self.output(eng, g)

            def products(self, eng, h, g):
                PN, AN, DN = self.PN, self.AN, self.DN
                eng.wait_ge(self.act_done, now(g, AN, 3 * h) if h else prev(g, AN, AN))
                for b in range(2):
                    last = nc.tensor.matmul(ps[:, 2 + b, 0:HC], wt(WQ[h]), xT[:, bass.ds(g * GC + b * HC, HC)], start=True, stop=True)
                last.then_inc(self.pe_done, 1)
                eng.wait_ge(self.act_done, now(g, AN, 3 * h + 2))
                eng.wait_ge(self.dve_done, now(g, DN, 4 * h - 3) if h else prev(g, DN, DN - 1))
                two_matmuls(eng, 4, ones_mat[:, :], self.norm[:, h, :])
                two_matmuls(eng, 6, key_sum[:, h, :], self.q[:, h, :]).then_inc(self.pe_done, 1)

            def norms(self, eng, h, g):
                PN, DN = self.PN, self.DN
                q, norm = self.q[:, h, :], self.norm[:, h, :]
                eng.wait_ge(self.pe_done, now(g, PN, 2 * h + 1))
                eng.wait_ge(self.dve_done, prev(g, DN, 4 * h + 4))
                nc.scalar.activation(two(q), ps[:, 2:4, 0:HC], ACT.Identity, bias=col(BQ[h])).then_inc(self.act_done, 1)
                nc.scalar.activation(two(norm), ps[:, 2:4, 0:HC], ACT.Square, bias=col(BQ[h])).then_inc(self.act_done, 1)
                eng.wait_ge(self.pe_done, now(g, PN, 2 * h + 2))
                nc.scalar.activation(two(norm), ps[:, 4:6, 0:HC], ACT.Sqrt).then_inc(self.act_done, 1)

            def quotients(self, eng, h, g):
                AN, DN = self.AN, self.DN
                q, norm = self.q[:, h, :], self.norm[:, h, :]
                eng.wait_ge(self.act_done, now(g, AN, 3 * h + 3))
                eng.wait_ge(self.dve_done, now(g, DN, 4 * h) if h else prev(g, DN, DN))
                nc.vector.scalar_tensor_tensor(out=two(self.t[:, :]), in0=two(norm), scalar=float(N), in1=ps[:, 6:8, 0:HC],
                                               op0=ALU.mult, op1=ALU.add).then_inc(self.dve_done, 1)
                eng.wait_ge(self.dve_done, now(g, DN, 4 * h + 1))
                nc.vector.reciprocal(self.t[:, :], self.t[:, :]).then_inc(self.dve_done, 1)
                eng.wait_ge(self.dve_done, now(g, DN, 4 * h + 2))
                eng.wait_ge(self.stored, 32 * (HEADS * g + h) + 32 * HEADS)
                nc.vector.tensor_tensor(self.qd[:, :], q, self.t[:, :], ALU.mult).then_inc(self.dve_done, 1)
                nc.vector.tensor_tensor(self.rden[:, :], norm, self.t[:, :], ALU.mult).then_inc(self.dve_done, 1)

            def store(self, eng, h, g):
                eng.wait_ge(self.dve_done, now(g, self.DN, 4 * h + 4))
                eng.sem_inc(self.begun, 1)
                c = bass.ds(g * GC, GC)
                eng.dma_start(q_tab[h * P:(h + 1) * P, c], self.qd[:, :]).then_inc(self.stored, 16)
                eng.dma_start(rden_tab[h * P:(h + 1) * P, c], self.rden[:, :]).then_inc(self.stored, 16)

            def output(self, eng, g):
                PN, DN = self.PN, self.DN
                if eng is nc.tensor:
                    eng.wait_ge(self.dve_done, now(g, DN, 4 * HEADS - 3))
                    for h in range(HEADS):
                        for b in range(2):
                            last = nc.tensor.matmul(ps[:, 6 + b, 0:HC], wt(WO[h][0]), xT[:, bass.ds(g * GC + b * HC, HC)],
                                                    start=(h == 0), stop=(h == HEADS - 1))
                    last.then_inc(self.pe_done, 1)
                elif eng is nc.vector:
                    xg = xT[:, bass.ds(g * GC, GC)]
                    eng.wait_ge(self.pe_done, now(g, PN, PN))
                    eng.wait_ge(self.dve_done, now(g, DN, 4 * HEADS))
                    nc.vector.tensor_scalar(two(self.t[:, :]), ps[:, 6:8, 0:HC], 1.0 / HEADS, col(BOH), ALU.mult, ALU.add).then_inc(self.dve_done, 1)
                    eng.wait_ge(self.dve_done, now(g, DN, DN - 1))
                    nc.vector.tensor_tensor(xg, xg, self.t[:, :], ALU.add).then_inc(self.dve_done, 1)

            def end(self, eng):
                if eng is nc.sync:
                    eng.wait_ge(self.stored, 32 * HEADS * (G + 1))
                    eng.wait_ge(self.zeroed, 1)
                    for h in range(HEADS):
                        for t in (q_tab, rden_tab):
                            eng.dma_start(t[h * P:(h + 1) * P, N:NP], self.zero[:, :]).then_inc(self.stored, 16)
                    eng.wait_ge(self.stored, 32 * HEADS * (G + 2))

        def layer2_step(step):
            before_last = step == ORDER - 1
            with ExitStack() as st:
                def tmp(name, shape, dt=F32):
                    return st.enter_context(nc.sbuf_tensor(f"{name}_s{step}", shape, dt))
                q, rden, xh, mean = [tmp(k, [P, HEADS, GC]) for k in ("q", "rden", "xh", "mean")]
                rows = tmp("rows", [P, HEADS, GW, P])
                y_rows = tmp("y_rows", [P, GW, P])
                with stage("in0", "in1", "pe_done", "act_done", "dve_done", "out0", "out1", "y_out", "begun") as (
                        block, in0, in1, pe_done, act_done, dve_done, out0, out1, y_out, begun):
                    PN, AN, DN = 5 + before_last, 2 + before_last, 7
                    loaded, stored = (in0, in1), (out0, out1)

                    @block.sync
                    def _(sp):
                        with loop(sp, G) as g:
                            c = bass.ds(g * GC, GC)
                            for h in range(HEADS):
                                sp.wait_ge(pe_done, prev(g, PN, 1 + h))
                                nc.sync.sem_inc(begun, 1)
                                sp.wait_ge(dve_done, prev(g, DN, 3 + 2 * h))
                                nc.sync.sem_inc(begun, 1)
                                sp.dma_start(q[:, h, :], q_tab[h * P:(h + 1) * P, c]).then_inc(loaded[h], 16)
                                sp.dma_start(rden[:, h, :], rden_tab[h * P:(h + 1) * P, c]).then_inc(loaded[h], 16)

                    @block.tensor
                    def _(pe):
                        nc.tensor.sem_inc(pe_done, PN)
                        with loop(pe, G) as g:
                            for h in range(HEADS):
                                pe.wait_ge(loaded[h], 32 * g + 32)
                                pe.wait_ge(dve_done, prev(g, DN, 3 + 2 * h))
                                if before_last and h == 0:
                                    pe.wait_ge(act_done, prev(g, AN, 3))
                                two_matmuls(pe, 2 * h, kv[:, h, :], q[:, h, :]).then_inc(pe_done, 1)
                            for h in range(HEADS):
                                pe.wait_ge(dve_done, now(g, DN, 4 + 2 * h))
                                pe.wait_ge(act_done, now(g, AN, h) if h else prev(g, AN, 2))
                                for k in range(GW):
                                    last = nc.tensor.transpose(flat[:, 3072 + k * P:3072 + (k + 1) * P], xh[:, h, k * P:(k + 1) * P], ident[:, :])
                                last.then_inc(pe_done, 1)
                                if h == 0:
                                    pe.wait_ge(dve_done, prev(g, DN, 7))
                                last = two_matmuls(pe, 4, wt(WO[h][step]), xh[:, h, :], start=(h == 0), stop=(h == HEADS - 1))
                            last.then_inc(pe_done, 1)
                            if before_last:
                                for k in range(GW):
                                    for h in range(HEADS):
                                        last = nc.tensor.matmul(flat[:, k * P:(k + 1) * P], xh[:, h, k * P:(k + 1) * P], wt(WO[h][ORDER]),
                                                                start=(h == 0), stop=(h == HEADS - 1))
                                last.then_inc(pe_done, 1)

                    @block.scalar
                    def _(act):
                        nc.scalar.sem_inc(act_done, AN)
                        for sem in (out0, out1, y_out):
                            nc.scalar.sem_inc(sem, 16)
                        with loop(act, G) as g:
                            for h in range(HEADS):
                                act.wait_ge(pe_done, now(g, PN, 3 + h))
                                act.wait_ge(stored[h], 16 * g + 16)
                                nc.scalar.copy(rows[:, h, :, :], flat[:, 3072:3072 + GC].rearrange("p (k f) -> p k f", k=GW)).then_inc(act_done, 1)
                                act.wait_ge(act_done, now(g, AN, 1 + h))
                                act.dma_start(xh_tab[bass.ds(g * GC, GC), h * P:(h + 1) * P].rearrange("(k p) f -> p k f", p=P),
                                              rows[:, h, :, :]).then_inc(stored[h], 16)
                            if before_last:
                                act.wait_ge(pe_done, now(g, PN, 6))
                                act.wait_ge(y_out, 16 * g + 16)
                                nc.scalar.copy(y_rows[:, :, :], flat[:, 0:GC].rearrange("p (k f) -> p k f", k=GW)).then_inc(act_done, 1)
                                act.wait_ge(act_done, now(g, AN, 3))
                                act.dma_start(windows(x_tab, g, P), y_rows[:, :, :]).then_inc(y_out, 16)
                        for sem in (out0, out1, y_out)[0:2 + before_last]:
                            act.wait_ge(sem, 16 * G + 16)

                    @block.vector
                    def _(dve):
                        nc.vector.sem_inc(dve_done, DN)
                        with loop(dve, G) as g:
                            c = bass.ds(g * GC, GC)
                            for h in range(HEADS):
                                nc.vector.tensor_tensor(mean[:, h, :], acc[:, h if step > 1 else 0, c], dinv[:, c], ALU.mult).then_inc(dve_done, 1)
                            for h in range(HEADS):
                                dve.wait_ge(loaded[h], 32 * g + 32)
                                dve.wait_ge(pe_done, prev(g, PN, PN))
                                dve.wait_ge(pe_done, now(g, PN, 1 + h))
                                nc.vector.scalar_tensor_tensor(out=two(xh[:, h, :]), in0=two(rden[:, h, :]), scalar=kv_sums[:, h:h + 1],
                                                               in1=ps[:, 2 * h:2 * h + 2, 0:HC], op0=ALU.mult, op1=ALU.add).then_inc(dve_done, 1)
                                dve.wait_ge(dve_done, now(g, DN, 3 + 2 * h))
                                nc.vector.tensor_tensor(xh[:, h, :], xh[:, h, :], mean[:, h, :], ALU.add).then_inc(dve_done, 1)
                            dve.wait_ge(pe_done, now(g, PN, 5))
                            nc.vector.scalar_tensor_tensor(out=two(xT[:, c]), in0=ps[:, 4:6, 0:HC], scalar=1.0 / HEADS, in1=two(xT[:, c]),
                                                           op0=ALU.mult, op1=ALU.add).then_inc(dve_done, 1)

        class LastAttention:
            parts = 2
            signals = ["la_in", "la_pe", "la_dve", "la_begun"]
            DN = HEADS + 1

            def __init__(self, tmp):
                self.q, self.rden, self.att = [tmp(k, [P, HEADS, GC]) for k in ("la_q", "la_rden", "att")]

            def take(self, loaded, pe_done, dve_done, begun):
                self.loaded, self.pe_done, self.dve_done, self.begun = loaded, pe_done, dve_done, begun

            def start(self, eng):
                if eng is nc.vector:
                    nc.vector.sem_inc(self.dve_done, self.DN)
                elif eng is nc.tensor:
                    nc.tensor.sem_inc(self.pe_done, 2)

            def do(self, eng, part, g):
                DN = self.DN
                c = bass.ds(g * GC, GC)
                if eng is nc.sync and part == 0:
                    eng.wait_ge(self.dve_done, prev(g, DN, HEADS))
                    eng.sem_inc(self.begun, 1)
                    for h in range(HEADS):
                        eng.dma_start(self.q[:, h, :], q_tab[h * P:(h + 1) * P, c]).then_inc(self.loaded, 16)
                        eng.dma_start(self.rden[:, h, :], rden_tab[h * P:(h + 1) * P, c]).then_inc(self.loaded, 16)
                elif eng is nc.tensor and part == 0:
                    eng.wait_ge(self.loaded, 32 * HEADS * (g + 1))
                    eng.wait_ge(self.dve_done, prev(g, DN, HEADS))
                    for h in range(HEADS):
                        last = two_matmuls(eng, 2 + 2 * h, kv[:, h, :], self.q[:, h, :])
                    last.then_inc(self.pe_done, 1)
                elif eng is nc.tensor:
                    eng.wait_ge(self.dve_done, now(g, DN, HEADS))
                    eng.wait_ge(self.dve_done, prev(g, DN, DN))
                    for h in range(HEADS):
                        last = two_matmuls(eng, 6, wt(WO[h][ORDER]), self.att[:, h, :], start=(h == 0), stop=(h == HEADS - 1))
                    last.then_inc(self.pe_done, 1)
                elif eng is nc.vector and part == 1:
                    eng.wait_ge(self.pe_done, now(g, 2, 1))
                    eng.wait_ge(self.loaded, 32 * HEADS * (g + 1))
                    for h in range(HEADS):
                        nc.vector.scalar_tensor_tensor(out=two(self.att[:, h, :]), in0=two(self.rden[:, h, :]), scalar=kv_sums[:, h:h + 1],
                                                       in1=ps[:, 2 + 2 * h:4 + 2 * h, 0:HC], op0=ALU.mult, op1=ALU.add).then_inc(self.dve_done, 1)
                    eng.wait_ge(self.pe_done, now(g, 2, 2))
                    nc.vector.scalar_tensor_tensor(out=two(xT[:, c]), in0=ps[:, 6:8, 0:HC], scalar=1.0 / HEADS, in1=two(xT[:, c]),
                                                   op0=ALU.mult, op1=ALU.add).then_inc(self.dve_done, 1)

            def end(self, eng):
                pass

        def layer2_last():
            with ExitStack() as st:
                def tmp(name, shape, dt=F32):
                    return st.enter_context(nc.sbuf_tensor(f"{name}_t", shape, dt))
                xg = tmp("xg", [P, GC])
                p_rows, q_rows = [tmp(k, [P, GW, P]) for k in ("p_rows", "q_rows")]
                ln = Norm(tmp, x_tab)
                with stage("halved", "final", "x_taken", "product_done", "p_copied", "q_made", "p_out", "q_out", *ln.signals) as (
                        block, halved, final, x_taken, product_done, p_copied, q_made, p_out, q_out, *s):
                    ln.take(*s)

                    def bank_rows(m):
                        return flat[:, 1024 * m:1024 * m + GC].rearrange("p (k f) -> p k f", k=GW)

                    @block.vector
                    def _(dve):
                        nc.vector.sem_inc(q_made, 1)
                        ln.start(dve)

                        def add(g):
                            c = bass.ds(g * GC, GC)
                            nc.vector.scalar_tensor_tensor(out=acc[:, 0, c], in0=acc[:, 0, c], scalar=1.0 / HEADS, in1=dinv[:, c],
                                                           op0=ALU.mult, op1=ALU.mult).then_inc(halved, 1)
                            dve.wait_ge(halved, g + 1)
                            nc.vector.tensor_tensor(xT[:, c], xT[:, c], acc[:, 0, c], ALU.add).then_inc(final, 1)

                        def target_rows(g):
                            dve.wait_ge(product_done, g + 2)
                            dve.wait_ge(q_out, 16 * g + 16)
                            nc.vector.tensor_tensor(q_rows[:, :, :], bank_rows(1), bias_rows[:, 2:3, :].to_broadcast([P, GW, P]),
                                                    ALU.add).then_inc(q_made, 1)

                        lagged(dve, (0, add), (1, ln.norm), (3, target_rows))

                    @block.tensor
                    def _(pe):
                        nc.tensor.sem_inc(product_done, 1)
                        ln.start(pe)

                        def products(g):
                            pe.wait_ge(x_taken, g + 1)
                            pe.wait_ge(p_copied, g + 1)
                            pe.wait_ge(q_made, g + 1)
                            for m in range(2):
                                for k in range(GW):
                                    last = nc.tensor.matmul(flat[:, 1024 * m + k * P:1024 * m + (k + 1) * P], xg[:, k * P:(k + 1) * P],
                                                            wt(W3[m]), start=True, stop=True)
                            last.then_inc(product_done, 1)

                        lagged(pe, (1, ln.turn), (2, ln.turn_back), (3, products))

                    @block.scalar
                    def _(act):
                        nc.scalar.sem_inc(p_copied, 1)
                        nc.scalar.sem_inc(p_out, 16)
                        ln.start(act)

                        def take(g):
                            act.wait_ge(ln.in_place, g + 2)
                            act.wait_ge(product_done, g + 1)
                            nc.scalar.sem_inc(ln.begun, 1)
                            nc.scalar.copy(xg[:, :], xT[:, bass.ds(g * GC, GC)]).then_inc(x_taken, 1)

                        def source_rows(g):
                            act.wait_ge(product_done, g + 2)
                            act.wait_ge(p_out, 16 * g + 16)
                            nc.scalar.copy(p_rows[:, :, :], bank_rows(0)).then_inc(p_copied, 1)
                            act.wait_ge(p_copied, g + 2)
                            act.dma_start(windows(p_tab, g, P), p_rows[:, :, :]).then_inc(p_out, 16)

                        lagged(act, (0, lambda g: ln.copy(g, lambda g: act.wait_ge(final, g + 1))), (1, ln.root), (1, ln.store),
                               (2, ln.put), (2, take), (3, source_rows))
                        ln.end()
                        act.wait_ge(p_out, 16 * G + 16)

                    @block.sync
                    def _(sp):
                        nc.sync.sem_inc(q_out, 16)
                        with loop(sp, G) as g:
                            sp.wait_ge(q_made, g + 2)
                            sp.dma_start(windows(q3_tab, g, P), q_rows[:, :, :]).then_inc(q_out, 16)
                        sp.wait_ge(q_out, 16 * G + 16)

        def message_pass(wide_path):
            W = 14
            OH = 7
            tag = "_w" if wide_path else ""
            with ExitStack() as st:
                def tmp(name, shape, dt=F32):
                    return st.enter_context(nc.sbuf_tensor(f"{name}_m{tag}", shape, dt))
                rows = tmp("rows", [P, U, P])
                attr = tmp("attr", [P, 2, MH, P])
                win = tmp("win", [P, W, P])
                onehot = tmp("onehot", [P, OH, P])
                turn = tmp("turn", [P, 2, 2, P])
                pre, hid = tmp("pre", [P, 2, P]), tmp("hid", [P, 2, P])
                idx = tmp("idx", [P, 2, H], I32)
                names = [f"rows_in{j}" for j in range(U)] + [f"win_in{k}" for k in range(W)] + ["attr_in0", "attr_in1"]
                names += ["cleared", "idx_copied", "begun", "matched", "turned", "copied", "mixed", "met", "rectified", "summed",
                          "added", "moved", "rest_in"]
                with stage(*names) as (block, *s):
                    rows_in, win_in, attr_in = s[0:U], s[U:U + W], s[U + W:U + W + 2]
                    cleared, idx_copied, begun, matched, turned, copied, mixed, met, rectified, summed, added, moved, rest_in = s[U + W + 2:]
                    steps = TILES // MU
                    lead = MH + 1

                    def done(n, j):
                        return n * MU + j + 1 + lead

                    ends = FULL - (steps - 1) * MU

                    def ended_rounds(eng, step):
                        if not wide_path:
                            with loop(eng, steps - 1) as i:
                                step(i, i, 0, False)
                            step(steps - 1, steps - 1, 0, True)
                            return
                        with loop(eng, ROUNDS - 1) as r:
                            if eng is nc.sync:
                                eng.wait_ge(moved, 3 * r + 3)
                                eng.sem_inc(begun, 1)
                            with loop(eng, steps - 1) as i:
                                step(r * steps + i, i, r, False)
                            step(r * steps + (steps - 1), steps - 1, r, True)

                    @block.gpsimd
                    def _(pool):
                        def step(n, i):
                            for j in range(U):
                                if j % H == 0:
                                    pool.wait_ge(idx_copied, 2 * n + j // H + 1)
                                    nc.gpsimd.sem_inc(begun, 1)
                                nc.gpsimd.indirect_dma_start(
                                    rows[:, j, :], None, p_tab,
                                    bass.IndirectOffsetOnAxis(ap=idx[:, j // H, j % H:j % H + 1], axis=0)).then_inc(rows_in[j], 16)

                        rounds(nc.gpsimd, "wide_m_pool", wide_path, TILES // U, step)

                    @block.sync
                    def _(sp):
                        regs = [nc.sync.alloc_register(f"msg_base{tag}{k}") for k in range(H)]

                        def step(n, i, r, last):
                            for j in range(MU):
                                if j % H == 0:
                                    nc.sync.load(regs, base_row[0:1, bass.ds(i * MU + j, H)])
                                    base = [nc.sync.snap(r, min_val=0, max_val=NP) for r in regs]
                                if j % MH == 0:
                                    h = j // MH
                                    sp.wait_ge(turned, done(n, j - MH - 1))
                                    nc.sync.sem_inc(begun, 1)
                                    for k in range(0, MH, H):
                                        whole = min(H, ends - j - k) if last else H
                                        sp.dma_start(attr[:, h, k:k + whole, :],
                                                     edge_attr_128[bass.ds((i * MU + j + k) * P, whole * P), :].rearrange("(t p) f -> p t f", p=P)
                                                     ).then_inc(attr_in[h], 16)
                                        if whole < H:
                                            sp.dma_start(attr[0:REST, h, k + whole, :], edge_attr_128[FULL * P:E, :]).then_inc(rest_in, 16)
                                sp.wait_ge(mixed, done(n, j - W))
                                sp.dma_start(win[:, j % W, :], q3_tab[bass.ds(base[j % H], P), :]).then_inc(win_in[j % W], 16)

                        if not wide_path:
                            ended_rounds(nc.sync, step)
                        else:
                            with when_wide(nc.sync, "wide_m_sp"):
                                ended_rounds(nc.sync, step)

                    @block.vector
                    def _(dve):
                        regs = [nc.vector.alloc_register(f"msg_sum_base{tag}{k}") for k in range(H)]
                        for sem in (matched, met, added):
                            nc.vector.sem_inc(sem, lead)
                        if not wide_path:
                            nc.vector.memset(acc[:, 0, :], 0.0).then_inc(cleared, 1)
                            dve.wait_ge(cleared, 1)

                        def meet(n, j):
                            dve.wait_ge(mixed, done(n, j))
                            dve.wait_ge(rows_in[j % U], 16 * (n * (MU // U) + j // U + 1))
                            dve.wait_ge(rectified, done(n, j - 2))
                            nc.vector.tensor_tensor(pre[:, j % 2, :], ps[:, 2 + j % 2, 0:P], rows[:, j % U, :], ALU.add).then_inc(met, 1)

                        def add(n, j, base):
                            dve.wait_ge(summed, done(n, j))
                            dve.wait_ge(added, done(n, j - 1))
                            a = acc[:, 0, bass.ds(base, P)]
                            nc.vector.tensor_tensor(a, a, ps[:, 4 + j % 2, 0:P], ALU.add).then_inc(added, 1)

                        def step(n, i):
                            bases = []
                            for j in range(MU + 4):
                                if j < MU:
                                    dve.wait_ge(summed, done(n, j - OH))
                                    nc.vector.tensor_scalar(onehot[:, j % OH, :], iota16[:, :], loc_col[:, bass.ds(i * MU + j, 1)], None,
                                                            ALU.is_equal).then_inc(matched, 1)
                                if 2 <= j < MU + 2:
                                    meet(n, j - 2)
                                if j >= 4:
                                    if (j - 4) % H == 0:
                                        nc.vector.load(regs, base_row[0:1, bass.ds(i * MU + j - 4, H)])
                                        bases += [nc.vector.snap(r, min_val=0, max_val=NP) for r in regs]
                                    add(n, j - 4, bases[j - 4])

                        if not wide_path:
                            rounds(dve, "", False, steps, step)
                        else:
                            with when_wide(nc.vector, "wide_m_dve"):
                                with loop(dve, ROUNDS - 1) as r:
                                    dve.wait_ge(mixed, r * TILES + lead)
                                    move_windows(dve, moved, begun, r)
                                    with loop(dve, steps) as i:
                                        step(r * steps + i, i)
                                dve.wait_ge(mixed, (ROUNDS - 1) * TILES + lead)
                                windows_back(dve, moved)

                    @block.tensor
                    def _(pe):
                        for sem in (turned, mixed, summed):
                            nc.tensor.sem_inc(sem, lead)

                        def mix(n, j):
                            pe.wait_ge(copied, done(n, j))
                            pe.wait_ge(win_in[j % W], 16 * (n * (MU // W) + j // W + 1))
                            pe.wait_ge(met, done(n, j - 2))
                            nc.tensor.matmul(ps[:, 2 + j % 2, 0:P], turn[:, j % 2, 0, :], win[:, j % W, :], start=True, stop=False)
                            nc.tensor.matmul(ps[:, 2 + j % 2, 0:P], turn[:, j % 2, 1, :], wt(W3[2]), start=False, stop=True).then_inc(mixed, 1)

                        def total(n, j):
                            pe.wait_ge(rectified, done(n, j))
                            pe.wait_ge(added, done(n, j - 2))
                            nc.tensor.matmul(ps[:, 4 + j % 2, 0:P], hid[:, j % 2, :], onehot[:, j % OH, :], start=True, stop=True).then_inc(summed, 1)

                        def step(n, i, r, last):
                            for j in range(MU + 3):
                                if j < MU:
                                    if j % MH == 0:
                                        pe.wait_ge(attr_in[j // MH], 32 * n + 32)
                                    if last and j == ends:
                                        pe.wait_ge(rest_in, 16 * r + 16)
                                    pe.wait_ge(matched, done(n, j))
                                    pe.wait_ge(copied, done(n, j - 2))
                                    nc.tensor.transpose(ps[:, j % 2, 0:P], onehot[:, j % OH, :], ident[:, :])
                                    nc.tensor.transpose(ps[:, j % 2, P:2 * P], attr[:, j // MH, j % MH, :], ident[:, :]).then_inc(turned, 1)
                                if 1 <= j <= MU:
                                    mix(n, j - 1)
                                if j >= 3:
                                    total(n, j - 3)

                        if not wide_path:
                            ended_rounds(nc.tensor, step)
                        else:
                            with when_wide(nc.tensor, "wide_m_pe"):
                                ended_rounds(nc.tensor, step)

                    @block.scalar
                    def _(act):
                        for sem in (copied, rectified):
                            nc.scalar.sem_inc(sem, lead)
                        nc.scalar.copy(idx[:, 0, :], src_idx[:, 0:H]).then_inc(idx_copied, 1)

                        def rectify(n, j):
                            act.wait_ge(met, done(n, j))
                            act.wait_ge(summed, done(n, j - 2))
                            nc.scalar.activation(hid[:, j % 2, :], pre[:, j % 2, :], ACT.Relu).then_inc(rectified, 1)

                        def step(n, i):
                            for j in range(MU + 2):
                                if j < MU:
                                    if j % H == 3:
                                        act.wait_ge(met, done(n, j - 4))
                                        nc.scalar.copy(idx[:, (j // H + 1) % 2, :], src_idx[:, bass.ds(i * MU + j - 3 + H, H)]).then_inc(idx_copied, 1)
                                    act.wait_ge(turned, done(n, j))
                                    act.wait_ge(mixed, done(n, j - 2))
                                    nc.scalar.copy(turn[:, j % 2, :, :], ps[:, j % 2, 0:2 * P].rearrange("p (a n) -> p a n", a=2)).then_inc(copied, 1)
                                if j >= 2:
                                    rectify(n, j - 2)

                        rounds(nc.scalar, "wide_m_act", wide_path, steps, step)

        def layer3_nodes():
            with ExitStack() as st:
                def tmp(name, shape, dt=F32):
                    return st.enter_context(nc.sbuf_tensor(f"{name}_u", shape, dt))
                deg, msg, r, z, hn, cand, diff = [tmp(k, [P, GC]) for k in ("deg", "msg", "r", "z", "hn", "cand", "diff")]
                with stage("deg_in", "summed", "gated", "made", "gates", "hidden", "tanh_done", "updated") as (
                        block, deg_in, summed, gated, made, gates, hidden, tanh_done, updated):
                    @block.sync
                    def _(sp):
                        with loop(sp, G) as g:
                            sp.wait_ge(made, g + 1)
                            sp.dma_start(deg[:, :], deg_tab[:, bass.ds(g * GC, GC)]).then_inc(deg_in, 16)

                    @block.tensor
                    def _(pe):
                        nc.tensor.sem_inc(gated, 3)

                        def product(bank, w, rhs, start, stop):
                            for b in range(2):
                                last = nc.tensor.matmul(ps[:, bank + b, 0:HC], wt(w), rhs(b), start=start, stop=stop)
                            return last

                        with loop(pe, G) as g:
                            def sums(b):
                                return acc[:, 0, bass.ds(g * GC + b * HC, HC)]

                            def xs(b):
                                return xT[:, bass.ds(g * GC + b * HC, HC)]

                            def msgs(b):
                                return msg[:, b * HC:(b + 1) * HC]
                            pe.wait_ge(hidden, prev(g, 2, 1))
                            product(0, W3O, sums, True, True).then_inc(summed, 1)
                            for k in range(2):
                                pe.wait_ge(gates, prev(g, 2, 1 + k))
                                product(2 + 2 * k, WHH[k], xs, True, False)
                            pe.wait_ge(made, g + 2)
                            for k in range(2):
                                product(2 + 2 * k, WIH[k], msgs, False, True).then_inc(gated, 1)
                            product(0, WHH[2], xs, True, True)
                            pe.wait_ge(hidden, prev(g, 2, 2))
                            product(6, WIH[2], msgs, True, True).then_inc(gated, 1)

                    @block.scalar
                    def _(act):
                        nc.scalar.sem_inc(gates, 2)
                        with loop(act, G) as g:
                            act.wait_ge(gated, now(g, 3, 1))
                            act.wait_ge(hidden, prev(g, 2, 1))
                            nc.scalar.activation(two(r[:, :]), ps[:, 2:4, 0:HC], ACT.Sigmoid, bias=col(BRZ[0])).then_inc(gates, 1)
                            act.wait_ge(gated, now(g, 3, 2))
                            act.wait_ge(updated, prev(g, 4, 2))
                            nc.scalar.activation(two(z[:, :]), ps[:, 4:6, 0:HC], ACT.Sigmoid, bias=col(BRZ[1])).then_inc(gates, 1)
                            act.wait_ge(hidden, now(g, 2, 2))
                            act.wait_ge(updated, prev(g, 4, 3))
                            nc.scalar.activation(cand[:, :], hn[:, :], ACT.Tanh, bias=col(BIH[2])).then_inc(tanh_done, 1)

                    @block.vector
                    def _(dve):
                        nc.vector.sem_inc(made, 1)
                        nc.vector.sem_inc(hidden, 2)
                        nc.vector.sem_inc(updated, 4)

                        def make(g):
                            dve.wait_ge(summed, g + 1)
                            dve.wait_ge(deg_in, 16 * g + 16)
                            dve.wait_ge(gated, 3 * g + 3)
                            nc.vector.scalar_tensor_tensor(out=two(msg[:, :]), in0=two(deg[:, :]), scalar=col(B32), in1=ps[:, 0:2, 0:HC],
                                                           op0=ALU.mult, op1=ALU.add).then_inc(made, 1)

                        def hide(g):
                            dve.wait_ge(gated, now(g, 3, 3))
                            dve.wait_ge(gates, now(g, 2, 1))
                            nc.vector.scalar_tensor_tensor(out=two(hn[:, :]), in0=ps[:, 0:2, 0:HC], scalar=col(BHH[2]), in1=two(r[:, :]),
                                                           op0=ALU.add, op1=ALU.mult).then_inc(hidden, 1)
                            dve.wait_ge(hidden, now(g, 2, 1))
                            nc.vector.tensor_tensor(two(hn[:, :]), two(hn[:, :]), ps[:, 6:8, 0:HC], ALU.add).then_inc(hidden, 1)

                        def update(g):
                            xg = xT[:, bass.ds(g * GC, GC)]
                            dve.wait_ge(tanh_done, g + 1)
                            nc.vector.tensor_tensor(diff[:, :], xg, cand[:, :], ALU.subtract).then_inc(updated, 1)
                            dve.wait_ge(updated, now(g, 4, 1))
                            dve.wait_ge(gates, now(g, 2, 2))
                            nc.vector.tensor_tensor(diff[:, :], diff[:, :], z[:, :], ALU.mult).then_inc(updated, 1)
                            dve.wait_ge(updated, now(g, 4, 2))
                            nc.vector.tensor_tensor(diff[:, :], diff[:, :], cand[:, :], ALU.add).then_inc(updated, 1)
                            dve.wait_ge(updated, now(g, 4, 3))
                            nc.vector.tensor_tensor(xg, xg, diff[:, :], ALU.add).then_inc(updated, 1)

                        make(0)
                        with loop(dve, G - 1) as g:
                            hide(g)
                            make(g + 1)
                            update(g)
                        hide(G - 1)
                        update(G - 1)

        def over_edges(pass_, *args, **kwargs):
            for wide_path in (False, True):
                pass_(*args, wide_path=wide_path, **kwargs)

        run = [load_weights, prepare_edges, first_linear, lambda: over_edges(scatter_pass, 0), lambda: layer0_nodes(0),
               lambda: over_edges(scatter_pass, 1), lambda: layer0_nodes(1),
               lambda: over_edges(gather_pass, 0, x_tab, 1, weighted=True, aside=[[Degrees]]), layer1_nodes,
               layer2_keys,
               lambda: over_edges(gather_pass, 1, x_tab, 1, aside=[[keys_values(x_tab, 1), Queries]]), lambda: layer2_step(1),
               lambda: over_edges(gather_pass, 2, xh_tab, HEADS, aside=[[keys_values(xh_tab, HEADS)]]), lambda: layer2_step(2),
               lambda: over_edges(gather_pass, 3, xh_tab, HEADS, aside=[[keys_values(xh_tab, HEADS)]]), lambda: layer2_step(3),
               lambda: over_edges(gather_pass, 4, x_tab, 1, aside=[[keys_values(xh_tab, HEADS)], [LastAttention]]), layer2_last,
               lambda: over_edges(message_pass), layer3_nodes, lambda: normalize(3, out)]
        for f in run:
            f()


_INS = ["x", "src", "dst", "edge_attr_128", "edge_weight", "L0_gnn_W1", "L0_gnn_b1", "L0_gnn_W2", "L0_gnn_b2",
        "L0_gnn_W3", "L0_gnn_b3", "L1_gnn_W1", "L1_gnn_b1", "L1_gnn_W2", "L1_gnn_b2", "L2_gnn_Wq_w", "L2_gnn_Wq_b",
        "L2_gnn_Wk_w", "L2_gnn_Wk_b", "L2_gnn_Wo_w", "L2_gnn_Wo_b", "L3_gnn_W1", "L3_gnn_b1", "L3_gnn_W2", "L3_gnn_b2",
        "L3_gnn_W_ih", "L3_gnn_b_ih", "L3_gnn_W_hh", "L3_gnn_b_hh"]


def kernel(**inputs):
    import numpy as np
    import concourse.bacc as bacc
    from concourse.bass_utils import run_bass_kernel_spmd

    nc = bacc.Bacc("TRN2", target_bir_lowering=False, num_devices=1)
    arrays, args = {}, {}
    for name in _INS:
        a = np.ascontiguousarray(inputs[name])
        arrays[f"in_{name}"] = a
        args[name] = nc.dram_tensor(f"in_{name}", a.shape, mybir.dt.from_np(a.dtype), kind="ExternalInput").ap()
    out = nc.dram_tensor("out_0", (N, P), F32, kind="ExternalOutput").ap()
    gnn_resnorm(nc, out, **args)
    r = run_bass_kernel_spmd(nc, [arrays], core_ids=[0])
    return r.results[0]["out_0"]
```
